# Optimizing a Trainium2 kernel written in Bass

```python
import numpy as np
import jax
import jax.numpy as jnp

def _softmax(x, axis=-1):
    return jax.nn.softmax(x, axis=axis)

def _gelu(x):
    return jax.nn.gelu(x, approximate=True)

def _silu(x):
    return jax.nn.silu(x)

def _sigmoid(x):
    return jax.nn.sigmoid(x)

def _layernorm(x, axis=-1, eps=1e-05):
    m = jnp.mean(x, axis=axis, keepdims=True)
    v = jnp.var(x, axis=axis, keepdims=True)
    return (x - m) / jnp.sqrt(v + eps)

def _scatter_add(tgt, idx, src, axis=0):
    return tgt.at[idx].add(src)

def _segment_sum(src, seg, n):
    return jax.ops.segment_sum(src, seg, n)
kernel_name = 'mk_prb_d2_jaxref_r8_6cacd9'

def setup_inputs(seed: int=0):
    np.random.seed(seed)
    _w = jnp.asarray

    def _L0_attn_setup():
        import jax, jax.numpy as jnp
        import numpy as np
        B, T, C = (4, 128, 128)
        HS = 64
        H = C // HS

        def wkv7(r, w, k, v, a, b):
            Bn, Tn, Cn = r.shape
            N = Cn // H

            def rs(z):
                return z.reshape(Bn, Tn, H, N).transpose(1, 0, 2, 3)
            r_, w_, k_, v_, a_, b_ = map(rs, (r, w, k, v, a, b))
            decay = jnp.exp(w_)
            S0 = jnp.zeros((Bn, H, N, N), dtype=r.dtype)

            def step(S, inp):
                rt, dt, kt, vt, at, bt = inp
                sa = jnp.einsum('bhij,bhj->bhi', S, at)
                S = S * dt[:, :, None, :] + sa[..., None] * bt[:, :, None, :] + vt[..., None] * kt[:, :, None, :]
                y = jnp.einsum('bhij,bhj->bhi', S, rt)
                return (S, y)
            _, ys = jax.lax.scan(step, S0, (r_, decay, k_, v_, a_, b_))
            return ys.transpose(1, 0, 2, 3).reshape(Bn, Tn, Cn)

        def timemix(x, lambdas, k_A, k_B, g_A, g_B, w_A, w_B, w_miu, a_A, a_B, a_time, x_A, x_B, x_miu, x_time, gn_gamma, gn_beta, rW, kW, vW, oW):
            Bn, Tn, Cn = x.shape
            Hn, Nn = x_time.shape
            x_last = jnp.concatenate([jnp.zeros_like(x[:, :1]), x[:, :-1]], axis=1)
            dx = x_last - x
            xm = x + dx * x_miu
            mix = jnp.tanh(xm @ x_A).reshape(Bn, Tn, 6, 32)
            miu = lambdas + jnp.einsum('btgk,gkc->gbtc', mix, x_B)
            xd = x[None] + dx[None] * miu
            r_in, w_in, k_in, v_in, a_in, g_in = xd
            v = v_in @ vW.T
            r = r_in @ rW.T
            g = jnp.tanh(g_in @ g_A) @ g_B
            w = -jax.nn.softplus(-(w_miu + jnp.tanh(w_in @ w_A) @ w_B)) - 0.5
            k = k_in @ kW.T + jnp.tanh(k_in @ k_A) @ k_B
            k = k / jnp.maximum(jnp.linalg.norm(k, axis=-1, keepdims=True), 1e-12)
            a_gate = jax.nn.sigmoid(a_time + a_in @ a_A @ a_B) * 2.0
            kk = k * jnp.exp(jnp.minimum(w * 0.5, 0.0))
            y = wkv7(r, w, kk, v, -k, k * a_gate)
            eps = 1e-05 * Hn
            yg = y.reshape(Bn * Tn, Hn, Nn)
            mean = yg.mean(-1, keepdims=True)
            var = yg.var(-1, keepdims=True)
            yg = (yg - mean) / jnp.sqrt(var + eps)
            y = yg.reshape(Bn * Tn, Cn) * gn_gamma + gn_beta
            y = y.reshape(Bn, Tn, Cn)
            rh = r.reshape(Bn, Tn, Hn, Nn)
            kh = k.reshape(Bn, Tn, Hn, Nn)
            vh = v.reshape(Bn, Tn, Hn, Nn)
            bonus = ((rh * kh * x_time).sum(-1, keepdims=True) * vh).reshape(Bn, Tn, Cn)
            out = (y + bonus) * g @ oW.T
            return out
        key = jax.random.key(seed)
        ks = jax.random.split(key, 24)
        s = 0.02
        d = {'x': jax.random.normal(ks[0], (B, T, C), jnp.float32), 'lambdas': jax.random.normal(ks[1], (6, 1, 1, C), jnp.float32) * s, 'k_A': jax.random.normal(ks[2], (C, 64), jnp.float32) * s, 'k_B': jax.random.normal(ks[3], (64, C), jnp.float32) * s, 'g_A': jax.random.normal(ks[4], (C, 128), jnp.float32) * s, 'g_B': jax.random.normal(ks[5], (128, C), jnp.float32) * s, 'w_A': jax.random.normal(ks[6], (C, 64), jnp.float32) * s, 'w_B': jax.random.normal(ks[7], (64, C), jnp.float32) * s, 'w_miu': jax.random.normal(ks[8], (1, 1, C), jnp.float32) * s, 'a_A': jax.random.normal(ks[9], (C, 64), jnp.float32) * s, 'a_B': jax.random.normal(ks[10], (64, C), jnp.float32) * s, 'a_time': jax.random.normal(ks[11], (1, 1, C), jnp.float32) * s, 'x_A': jax.random.normal(ks[12], (C, 32 * 6), jnp.float32) * s, 'x_B': jax.random.normal(ks[13], (6, 32, C), jnp.float32) * s, 'x_miu': jax.random.normal(ks[14], (1, 1, C), jnp.float32) * s, 'x_time': jax.random.normal(ks[15], (H, HS), jnp.float32) * s, 'gn_gamma': jnp.ones((C,), jnp.float32), 'gn_beta': jnp.zeros((C,), jnp.float32), 'rW': jax.random.normal(ks[16], (C, C), jnp.float32) * s, 'kW': jax.random.normal(ks[17], (C, C), jnp.float32) * s, 'vW': jax.random.normal(ks[18], (C, C), jnp.float32) * s, 'oW': jax.random.normal(ks[19], (C, C), jnp.float32) * s}
        return d
    _L0_attn_in = _L0_attn_setup()

    def _L0_ffn_setup():
        import jax, jax.numpy as jnp
        import numpy as np
        DIM = 128
        NUM_EXPERTS = 8
        TOP_K = 2
        HIDDEN = int(DIM * 1.5)
        key = jax.random.key(seed)
        k_x, k_r, k_w1, k_w2, k_w3 = jax.random.split(key, 5)
        B, T = (2, 512)
        s_in = 1.0 / np.sqrt(DIM)
        s_h = 1.0 / np.sqrt(HIDDEN)
        return {'x': jax.random.normal(k_x, (B, T, DIM), dtype=jnp.float32), 'Wr': jax.random.uniform(k_r, (DIM, NUM_EXPERTS), minval=-s_in, maxval=s_in, dtype=jnp.float32), 'W1': jax.random.uniform(k_w1, (NUM_EXPERTS, DIM, HIDDEN), minval=-s_in, maxval=s_in, dtype=jnp.float32), 'W2': jax.random.uniform(k_w2, (NUM_EXPERTS, HIDDEN, DIM), minval=-s_h, maxval=s_h, dtype=jnp.float32), 'W3': jax.random.uniform(k_w3, (NUM_EXPERTS, DIM, HIDDEN), minval=-s_in, maxval=s_in, dtype=jnp.float32)}
    _L0_ffn_in = _L0_ffn_setup()

    def _L1_attn_setup():
        import jax, jax.numpy as jnp
        import numpy as np
        B, L, D_IN, D_OUT, H, WIN = (1, 256, 128, 128, 16, 64)
        D_H = D_OUT // H
        key = jax.random.key(seed)
        ks = jax.random.split(key, 5)
        s = 0.02
        return {'x': jax.random.normal(ks[0], (B, L, D_IN), dtype=jnp.float32), 'Wq': jax.random.normal(ks[1], (D_IN, D_OUT), dtype=jnp.float32) * s, 'Wk': jax.random.normal(ks[2], (D_IN, D_OUT), dtype=jnp.float32) * s, 'Wv': jax.random.normal(ks[3], (D_IN, D_OUT), dtype=jnp.float32) * s, 'Wo': jax.random.normal(ks[4], (D_OUT, D_IN), dtype=jnp.float32) * s}
    _L1_attn_in = _L1_attn_setup()

    def _L1_ffn_setup():
        import jax, jax.numpy as jnp
        import numpy as np
        D_MODEL = 128
        N_EXPERTS = 8
        TOP_K = 2
        HIDDEN = 4 * D_MODEL
        key = jax.random.key(seed)
        ks = jax.random.split(key, 6)
        B, S = (2, 256)
        x = jax.random.normal(ks[0], (B, S, D_MODEL), dtype=jnp.float32)
        shared_w1 = jax.random.normal(ks[1], (HIDDEN, D_MODEL), dtype=jnp.float32) * 0.02
        shared_w2 = jax.random.normal(ks[2], (D_MODEL, HIDDEN), dtype=jnp.float32) * 0.02
        experts_w1 = jax.random.normal(ks[3], (N_EXPERTS, HIDDEN, D_MODEL), dtype=jnp.float32) * 0.02
        experts_w2 = jax.random.normal(ks[4], (N_EXPERTS, D_MODEL, HIDDEN), dtype=jnp.float32) * 0.02
        gate_w = jax.random.normal(ks[5], (N_EXPERTS, D_MODEL), dtype=jnp.float32) * 0.02
        return {'x': x, 'shared_w1': shared_w1, 'shared_w2': shared_w2, 'experts_w1': experts_w1, 'experts_w2': experts_w2, 'gate_w': gate_w}
    _L1_ffn_in = _L1_ffn_setup()
    _d = {'L0_attn_x': _L0_attn_in['x'], 'L0_attn_lambdas': _L0_attn_in['lambdas'], 'L0_attn_k_A': _L0_attn_in['k_A'], 'L0_attn_k_B': _L0_attn_in['k_B'], 'L0_attn_g_A': _L0_attn_in['g_A'], 'L0_attn_g_B': _L0_attn_in['g_B'], 'L0_attn_w_A': _L0_attn_in['w_A'], 'L0_attn_w_B': _L0_attn_in['w_B'], 'L0_attn_w_miu': _L0_attn_in['w_miu'], 'L0_attn_a_A': _L0_attn_in['a_A'], 'L0_attn_a_B': _L0_attn_in['a_B'], 'L0_attn_a_time': _L0_attn_in['a_time'], 'L0_attn_x_A': _L0_attn_in['x_A'], 'L0_attn_x_B': _L0_attn_in['x_B'], 'L0_attn_x_miu': _L0_attn_in['x_miu'], 'L0_attn_x_time': _L0_attn_in['x_time'], 'L0_attn_gn_gamma': _L0_attn_in['gn_gamma'], 'L0_attn_gn_beta': _L0_attn_in['gn_beta'], 'L0_attn_rW': _L0_attn_in['rW'], 'L0_attn_kW': _L0_attn_in['kW'], 'L0_attn_vW': _L0_attn_in['vW'], 'L0_attn_oW': _L0_attn_in['oW'], 'L0_ffn_Wr': _L0_ffn_in['Wr'], 'L0_ffn_W1': _L0_ffn_in['W1'], 'L0_ffn_W2': _L0_ffn_in['W2'], 'L0_ffn_W3': _L0_ffn_in['W3'], 'L1_attn_Wq': _L1_attn_in['Wq'], 'L1_attn_Wk': _L1_attn_in['Wk'], 'L1_attn_Wv': _L1_attn_in['Wv'], 'L1_attn_Wo': _L1_attn_in['Wo'], 'L1_ffn_shared_w1': _L1_ffn_in['shared_w1'], 'L1_ffn_shared_w2': _L1_ffn_in['shared_w2'], 'L1_ffn_experts_w1': _L1_ffn_in['experts_w1'], 'L1_ffn_experts_w2': _L1_ffn_in['experts_w2'], 'L1_ffn_gate_w': _L1_ffn_in['gate_w']}
    _x0 = _d['L0_attn_x']
    _d['L0_attn_x'] = jax.random.normal(jax.random.fold_in(jax.random.key(seed), 1), (4, 1024, 128), dtype=_x0.dtype)
    del _x0
    return _d

def reference(L0_attn_x, L0_attn_lambdas, L0_attn_k_A, L0_attn_k_B, L0_attn_g_A, L0_attn_g_B, L0_attn_w_A, L0_attn_w_B, L0_attn_w_miu, L0_attn_a_A, L0_attn_a_B, L0_attn_a_time, L0_attn_x_A, L0_attn_x_B, L0_attn_x_miu, L0_attn_x_time, L0_attn_gn_gamma, L0_attn_gn_beta, L0_attn_rW, L0_attn_kW, L0_attn_vW, L0_attn_oW, L0_ffn_Wr, L0_ffn_W1, L0_ffn_W2, L0_ffn_W3, L1_attn_Wq, L1_attn_Wk, L1_attn_Wv, L1_attn_Wo, L1_ffn_shared_w1, L1_ffn_shared_w2, L1_ffn_experts_w1, L1_ffn_experts_w2, L1_ffn_gate_w):

    def _L0_attn_ref(x, lambdas, k_A, k_B, g_A, g_B, w_A, w_B, w_miu, a_A, a_B, a_time, x_A, x_B, x_miu, x_time, gn_gamma, gn_beta, rW, kW, vW, oW):
        import jax, jax.numpy as jnp
        import numpy as np
        B, T, C = (4, 128, 128)
        HS = 64
        H = C // HS

        def wkv7(r, w, k, v, a, b):
            Bn, Tn, Cn = r.shape
            N = Cn // H

            def rs(z):
                return z.reshape(Bn, Tn, H, N).transpose(1, 0, 2, 3)
            r_, w_, k_, v_, a_, b_ = map(rs, (r, w, k, v, a, b))
            decay = jnp.exp(w_)
            S0 = jnp.zeros((Bn, H, N, N), dtype=r.dtype)

            def step(S, inp):
                rt, dt, kt, vt, at, bt = inp
                sa = jnp.einsum('bhij,bhj->bhi', S, at)
                S = S * dt[:, :, None, :] + sa[..., None] * bt[:, :, None, :] + vt[..., None] * kt[:, :, None, :]
                y = jnp.einsum('bhij,bhj->bhi', S, rt)
                return (S, y)
            _, ys = jax.lax.scan(step, S0, (r_, decay, k_, v_, a_, b_))
            return ys.transpose(1, 0, 2, 3).reshape(Bn, Tn, Cn)

        def timemix(x, lambdas, k_A, k_B, g_A, g_B, w_A, w_B, w_miu, a_A, a_B, a_time, x_A, x_B, x_miu, x_time, gn_gamma, gn_beta, rW, kW, vW, oW):
            Bn, Tn, Cn = x.shape
            Hn, Nn = x_time.shape
            x_last = jnp.concatenate([jnp.zeros_like(x[:, :1]), x[:, :-1]], axis=1)
            dx = x_last - x
            xm = x + dx * x_miu
            mix = jnp.tanh(xm @ x_A).reshape(Bn, Tn, 6, 32)
            miu = lambdas + jnp.einsum('btgk,gkc->gbtc', mix, x_B)
            xd = x[None] + dx[None] * miu
            r_in, w_in, k_in, v_in, a_in, g_in = xd
            v = v_in @ vW.T
            r = r_in @ rW.T
            g = jnp.tanh(g_in @ g_A) @ g_B
            w = -jax.nn.softplus(-(w_miu + jnp.tanh(w_in @ w_A) @ w_B)) - 0.5
            k = k_in @ kW.T + jnp.tanh(k_in @ k_A) @ k_B
            k = k / jnp.maximum(jnp.linalg.norm(k, axis=-1, keepdims=True), 1e-12)
            a_gate = jax.nn.sigmoid(a_time + a_in @ a_A @ a_B) * 2.0
            kk = k * jnp.exp(jnp.minimum(w * 0.5, 0.0))
            y = wkv7(r, w, kk, v, -k, k * a_gate)
            eps = 1e-05 * Hn
            yg = y.reshape(Bn * Tn, Hn, Nn)
            mean = yg.mean(-1, keepdims=True)
            var = yg.var(-1, keepdims=True)
            yg = (yg - mean) / jnp.sqrt(var + eps)
            y = yg.reshape(Bn * Tn, Cn) * gn_gamma + gn_beta
            y = y.reshape(Bn, Tn, Cn)
            rh = r.reshape(Bn, Tn, Hn, Nn)
            kh = k.reshape(Bn, Tn, Hn, Nn)
            vh = v.reshape(Bn, Tn, Hn, Nn)
            bonus = ((rh * kh * x_time).sum(-1, keepdims=True) * vh).reshape(Bn, Tn, Cn)
            out = (y + bonus) * g @ oW.T
            return out
        return timemix(x, lambdas, k_A, k_B, g_A, g_B, w_A, w_B, w_miu, a_A, a_B, a_time, x_A, x_B, x_miu, x_time, gn_gamma, gn_beta, rW, kW, vW, oW)

    def _L0_ffn_ref(x, Wr, W1, W2, W3):
        import jax, jax.numpy as jnp
        import numpy as np
        DIM = 128
        NUM_EXPERTS = 8
        TOP_K = 2
        HIDDEN = int(DIM * 1.5)
        B, T, C = x.shape
        xf = x.reshape(-1, C)
        gate_logits = xf @ Wr
        w, idx = jax.lax.top_k(gate_logits, TOP_K)
        w = jax.nn.softmax(w, axis=-1)
        comb = jnp.sum(w[:, :, None] * jax.nn.one_hot(idx, NUM_EXPERTS, dtype=w.dtype), axis=1)
        h = jnp.einsum('nc,ech->neh', xf, W1)
        g = jnp.einsum('nc,ech->neh', xf, W3)
        y = jnp.einsum('neh,ehc->nec', jax.nn.silu(h) * g, W2)
        out = jnp.einsum('nec,ne->nc', y, comb)
        return out.reshape(B, T, C)

    def _L1_attn_ref(x, Wq, Wk, Wv, Wo):
        import jax, jax.numpy as jnp
        import numpy as np
        B, L, D_IN, D_OUT, H, WIN = (1, 256, 128, 128, 16, 64)
        D_H = D_OUT // H
        Bx, Lx, _ = x.shape
        W = min(WIN, Lx)
        scale = D_H ** (-0.5)

        def split_heads(t):
            return t.reshape(Bx, Lx, H, D_H).transpose(0, 2, 1, 3)
        q = split_heads(x @ Wq)
        k = split_heads(x @ Wk)
        v = split_heads(x @ Wv)
        offsets = jnp.arange(W) - (W - 1)
        idx = jnp.arange(Lx)[:, None] + offsets[None, :]
        invalid = idx < 0
        idx = jnp.clip(idx, 0, Lx - 1)
        k_win = jnp.take(k, idx, axis=2)
        v_win = jnp.take(v, idx, axis=2)
        scores = jnp.einsum('bhld,bhlwd->bhlw', q, k_win) * scale
        scores = jnp.where(invalid[None, None, :, :], -jnp.inf, scores)
        attn = jax.nn.softmax(scores, axis=-1)
        ctx = jnp.einsum('bhlw,bhlwd->bhld', attn, v_win)
        ctx = ctx.transpose(0, 2, 1, 3).reshape(Bx, Lx, D_OUT)
        return ctx @ Wo

    def _L1_ffn_ref(x, shared_w1, shared_w2, experts_w1, experts_w2, gate_w):
        import jax, jax.numpy as jnp
        import numpy as np
        D_MODEL = 128
        N_EXPERTS = 8
        TOP_K = 2
        HIDDEN = 4 * D_MODEL
        B, S, D = x.shape
        T = B * S
        x_flat = x.reshape(T, D)
        shared = jnp.einsum('td,dh->th', x_flat, shared_w1.T)
        shared = jnp.einsum('th,hd->td', jax.nn.silu(shared), shared_w2.T)
        gate_logits = x_flat @ gate_w.T
        top_k_gates, top_k_idx = jax.lax.top_k(gate_logits, TOP_K)
        top_k_gates = jax.nn.softmax(top_k_gates, axis=1)
        gates = jnp.zeros((T, N_EXPERTS), dtype=x.dtype)
        gates = gates.at[jnp.arange(T)[:, None], top_k_idx].set(top_k_gates)
        h = jnp.einsum('td,ehd->teh', x_flat, experts_w1)
        expert_out = jnp.einsum('teh,edh->ted', jax.nn.silu(h), experts_w2)
        selected = jnp.einsum('ted,te->td', expert_out, gates)
        return (shared + selected).reshape(B, S, D)
    x = L0_attn_x
    xn = _layernorm(x, axis=-1)
    x = x + _L0_attn_ref(xn, L0_attn_lambdas, L0_attn_k_A, L0_attn_k_B, L0_attn_g_A, L0_attn_g_B, L0_attn_w_A, L0_attn_w_B, L0_attn_w_miu, L0_attn_a_A, L0_attn_a_B, L0_attn_a_time, L0_attn_x_A, L0_attn_x_B, L0_attn_x_miu, L0_attn_x_time, L0_attn_gn_gamma, L0_attn_gn_beta, L0_attn_rW, L0_attn_kW, L0_attn_vW, L0_attn_oW) + _L0_ffn_ref(xn, L0_ffn_Wr, L0_ffn_W1, L0_ffn_W2, L0_ffn_W3)
    xn = _layernorm(x, axis=-1)
    x = x + _L1_attn_ref(xn, L1_attn_Wq, L1_attn_Wk, L1_attn_Wv, L1_attn_Wo) + _L1_ffn_ref(xn, L1_ffn_shared_w1, L1_ffn_shared_w2, L1_ffn_experts_w1, L1_ffn_experts_w2, L1_ffn_gate_w)
    return x

_drawn_inputs = setup_inputs


def setup_inputs(seed=0):
    import zlib

    import numpy as np

    out = dict(_drawn_inputs(seed))
    spreads = {'L0_attn_gn_gamma': (1.0, 0.6), 'L0_attn_gn_beta': (0.0, 0.8)}
    factors = {'L0_attn_lambdas': 8.0,
     'L0_attn_k_A': 8.0,
     'L0_attn_k_B': 8.0,
     'L0_attn_g_A': 5.063,
     'L0_attn_g_B': 5.109,
     'L0_attn_w_A': 8.0,
     'L0_attn_w_B': 8.0,
     'L0_attn_w_miu': 8.0,
     'L0_attn_a_A': 8.0,
     'L0_attn_a_B': 8.0,
     'L0_attn_a_time': 38.52,
     'L0_attn_x_A': 8.0,
     'L0_attn_x_B': 8.0,
     'L0_attn_x_miu': 8.0,
     'L0_attn_x_time': 8.0,
     'L0_attn_rW': 5.072,
     'L0_attn_kW': 5.14,
     'L0_attn_vW': 5.119,
     'L0_attn_oW': 5.056,
     'L1_attn_Wq': 8.0,
     'L1_attn_Wk': 8.0,
     'L1_attn_Wv': 8.0,
     'L1_attn_Wo': 8.0,
     'L1_ffn_shared_w1': 3.032,
     'L1_ffn_shared_w2': 3.022,
     'L1_ffn_experts_w1': 4.31,
     'L1_ffn_experts_w2': 4.271,
     'L1_ffn_gate_w': 4.961}
    for name, (base, spread) in spreads.items():
        noise = np.random.default_rng([zlib.crc32(name.encode()), seed]).standard_normal(out[name].shape)
        drawn = base * np.exp(spread * noise) if base else spread * noise
        out[name] = jnp.asarray(drawn.astype(out[name].dtype))
    for name, factor in factors.items():
        out[name] = (out[name] * factor).astype(out[name].dtype)
    return out
```

```python
from contextlib import ExitStack

import numpy as np

import concourse.bass as bass
from concourse import mybir

ALU = mybir.AluOpType
ACT = mybir.ActivationFunctionType
AX = mybir.AxisListType
F32 = mybir.dt.float32
BF16 = mybir.dt.bfloat16
I32 = mybir.dt.int32
U32 = mybir.dt.uint32

P = 128
NB = 4
TOK = NB * P
LN_EPS = 1e-5

NG = 6
MIXK = 32
LORA = 64
NH = 2
HS = P // NH
NU = NB * NH
GN_EPS = 1e-5 * NH
LEVELS = [1, 2, 4, 8, 16, 32, 64]

NE = 8
HID0 = 192
K0 = NE * HID0 // P
PAIR_TILES = 2 * HID0 // P

H1 = 16
D1 = P // H1
WIN = 64
KEYS = WIN + P
HPG = 32 // D1
NPAIR = H1 // 2
MASKED = -1.0e30

NF = NE + 1
K1 = 4

VECS = ["w_miu", "a_time", "x_miu", "x_time"]


def psum_plan():
    plan, turn = [], [0]

    def use(name, bank=None):
        if bank is None:
            bank = turn[0] % 8
            turn[0] += 1
        plan.append((name, bank))

    for n in ["xnT0", "logit0", "mixA", "mixB"] + [f"miu{g}" for g in range(NG)]:
        use(n)
    for n in ["low_w", "low_k", "low_a", "low_g", "r", "w", "k", "a", "v", "g", "norm"]:
        use(n)
    for n in [0] + LEVELS:
        for u in range(NU):
            use(f"lev{n}_{u}")
    for n in LEVELS[1:]:
        for s in ("T", "Z", "D"):
            for q in range(2):
                use(f"inv{n}{s}{q}")
    for n in ["btok", "ktok", "bonus", "X0", "X1", "U", "Y0", "Y1", "S", "zT", "o0"]:
        use(n)
    for j in range(NE // 2):
        for k in range(PAIR_TILES):
            use(f"h0_{PAIR_TILES * j + k}")
            use(f"g0_{PAIR_TILES * j + k}")
        for e in (2 * j, 2 * j + 1):
            use(f"y0_{e}")
    for n in ["xnT1", "logit1", "q1", "k1", "v1", "v1p"]:
        use(n)
    for b in range(NB):
        for p in range(NPAIR):
            n = b * NPAIR + p
            use(f"sc{n}", n % 3)
            use(f"pt{n}", 3 + n % 3)
            if p == 0:
                use(f"av{b}", 6 + b % 2)
    for n in ["cT", "o1"]:
        use(n)
    for e in range(NF):
        for k in range(K1):
            use(f"h1_{K1 * e + k}")
        use(f"y1_{e}")
    return plan


def build(nc, io, out):
    x_dram = io["x"]
    T = x_dram.shape[1]
    NT = T // P
    plan = psum_plan()
    bank_of, turn_of, turns = {}, {}, [0] * 8
    fill_of, fills_of = {}, [0] * 8
    for name, b in plan:
        bank_of[name], turn_of[name], fill_of[name] = b, turns[b], fills_of[b]
        turns[b] += 1
        fills_of[b] += not name.startswith("av")

    with ExitStack() as ctx:
        def sb(name, shape, dt=F32):
            return ctx.enter_context(nc.sbuf_tensor(name, shape, dt))

        def sem(name):
            return ctx.enter_context(nc.semaphore(name))

        banks = [ctx.enter_context(nc.psum_tensor(f"bank{b}", [P, 512], F32)) for b in range(8)]
        bank_filled = [sem(f"bank_filled{b}") for b in range(8)]
        bank_taken = [sem(f"bank_taken{b}") for b in range(8)]

        def bank(name):
            return banks[bank_of[name]]

        def is_free(i, name):
            return bank_taken[bank_of[name]], i * turns[bank_of[name]] + turn_of[name] + 1

        def is_filled(i, name):
            return bank_filled[bank_of[name]], i * fills_of[bank_of[name]] + fill_of[name] + 1

        def is_taken(i, name):
            return bank_taken[bank_of[name]], i * turns[bank_of[name]] + turn_of[name] + 2

        def fills(name):
            return bank_filled[bank_of[name]], 1

        def takes(name):
            return bank_taken[bank_of[name]], 1

        x_tile = sb("x_tile", [P, NB, P])
        xA = sb("xA", [P, NG * MIXK])
        xB_lo = sb("xB_lo", [P, P])
        xB_hi = sb("xB_hi", [2 * MIXK, P])
        lowA = {g: sb(f"{g}_A", [P, n]) for g, n in (("w", LORA), ("k", LORA), ("a", LORA), ("g", P))}
        lowB = {g: sb(f"{g}_B", [n, P]) for g, n in (("w", LORA), ("k", LORA), ("a", LORA), ("g", P))}
        proj = {g: sb(f"{g}W_T", [P, P]) for g in "rkvo"}
        lam = sb("lam", [P, NG])
        vec = {n: sb(n, [P, 1]) for n in VECS}
        neg_w_miu = sb("neg_w_miu", [P, 1])
        neg_a_time = sb("neg_a_time", [P, 1])
        gamma = sb("gamma", [P, P])
        beta = sb("beta", [P, P])
        Wr = sb("Wr", [P, NE])
        W1 = sb("W1", [P, NE * HID0])
        W3 = sb("W3", [P, NE * HID0])
        W2 = sb("W2", [P, K0, P])
        attnW = {g: sb(f"W{g}", [P, P]) for g in "qkvo"}
        gateW = sb("gateW", [P, NE])
        F1 = sb("F1", [P, NF * K1 * P])
        F2 = sb("F2", [P, NF * K1, P])

        ident = sb("ident", [P, P])
        ident16 = sb("ident16", [P, P], BF16)
        ones = sb("ones", [P, P])
        head_ones = sb("head_ones", [P, NH])
        group_head = sb("group_head", [P, HPG])
        level_mask = sb("level_mask", [P, len(LEVELS), P])
        expert_no = sb("expert_no", [P, NE])
        key_mask = sb("key_mask", [P, 2, KEYS], BF16)
        key_mask_now = sb("key_mask_now", [P, 2, KEYS], BF16)

        xnT = sb("xnT", [P, NB, 1 + P])
        state = sb("state", [P, NB, HS])
        x1nT = sb("x1nT", [P, NB, KEYS])
        kT1 = sb("kT1", [P, NB, KEYS])

        stats = sb("stats", [P, NB, 6])
        moments = sb("moments", [P, NB, 2])
        rstd = sb("rstd", [P, NB])
        dx = sb("dx", [P, NB, P])
        mixA = sb("mixA", [P, TOK])
        mixB = sb("mixB", [2 * MIXK, TOK])
        xd = sb("xd", [P, NG, TOK])
        xn = xd[:, 0, :].rearrange("p (b t) -> p b t", b=NB)
        x1n = xd[:, 1, :].rearrange("p (b t) -> p b t", b=NB)
        ctx1 = xn
        q1 = xd[:, 2:2 + HPG, :]
        low = {g: sb(f"low_{g}", [n, TOK]) for g, n in (("w", LORA), ("k", LORA), ("g", P))}
        low["a"] = mixB
        r_raw = sb("r_raw", [P, TOK])
        k_raw = sb("k_raw", [P, TOK])
        xm = k_raw
        k_sq = sb("k_sq", [P, TOK])
        rkx = k_sq
        kn = sb("kn", [P, TOK])
        decay = sb("decay", [P, TOK])
        v_tok = sb("v_tok", [P, NB, P])
        g_tok = sb("g_tok", [P, NB, P])
        ra = sb("ra", [P, 2, TOK])
        bk = sb("bk", [P, 2, TOK])
        root_decay, gate_a = bk[:, 0, :], bk[:, 1, :]
        block_decay = {2 * n: sb(f"block_decay{2 * n}", [P, TOK // (2 * n)]) for n in LEVELS}
        A = sb("A", [P, NU, 4, P])
        A_level = sb("A_level", [P, NU, P])
        inv = sb("inv", [P, NU, P])
        invT = sb("invT", [P, NU, P])
        AZ = sb("AZ", [P, NU, P])
        b_tok, k_tok = A_level[:, 0:NB, :], A_level[:, NB:2 * NB, :]
        bonus = sb("bonus", [P, NU])
        XU = AZ[:].rearrange("p (s u) (v d) -> p s (u v) d", s=2, d=HS)
        X, U = XU[:, 0], XU[:, 1]
        y = sb("y", [P, NU, HS])
        gn_stats = sb("gn_stats", [P, NU, 6])
        gn_mom = sb("gn_mom", [P, NU, 2])
        gn_rstd = sb("gn_rstd", [P, NU])
        y_mul = y
        bonus_v = dx[:].rearrange("p b (h d) -> p (b h) d", h=NH)
        zT = sb("zT", [P, TOK])
        state_dec = sb("state_dec", [P, NB, HS])

        logits = sb("logits", [P, NB, NE])
        top = sb("top", [P, NB, 8])
        top_at = sb("top_at", [P, NB, 8], U32)
        top_atf = sb("top_atf", [P, NB, 8])
        top_gap = sb("top_gap", [P, NB])
        top_exp = sb("top_exp", [P, NB])
        top_sum = sb("top_sum", [P, NB])
        top_w = sb("top_w", [P, 2, NB])
        hot = sb("hot", [P, 2, NB, NE])
        comb = [sb(f"comb{l}", [P, NB, NE]) for l in range(2)]
        acc0 = sb("acc0", [P, NB, P])
        act0 = sb("act0", [P, 2, TOK])
        hid = sb("hid", [P, 2, K1, TOK])
        v1 = sb("v1", [P, NB, P])
        v1p = low["k"][:].rearrange("p (b d) -> p b d", b=NB)
        neg_max = sb("neg_max", [P, 3, 2])
        prob = sb("prob", [P, 3, 2, KEYS])
        prob_sum = sb("prob_sum", [P, NB, H1])
        prob_inv = sb("prob_inv", [P, NB, H1])
        pT = sb("pT", [P, 2, 2, P])
        pTp = sb("pTp", [WIN, 2, 2, WIN])
        cT = zT
        acc1 = sb("acc1", [P, NB, P])
        out_tile = sb("out_tile", [P, NB, P])

        weights_in = sem("weights_in")
        x_in = sem("x_in")
        out_done = sem("out_done")
        const_step = sem("const_step")
        consts = sem("consts")
        settled = sem("settled")
        per_tile, counted = {}, {}

        def step(name, n=1):
            per_tile[name] = (sem(name), n)

        for name, n in [
            ("norm_stats0", NB), ("norm_moments0", NB), ("norm_var0", 1), ("norm_root0", 1), ("norm_rstd0", 1), ("xn_ready", NB), ("front_kept", 1), ("dx_ready", 1), ("xm_ready", 1),
            ("xd_ready", NG), ("k_sq_ready", 1), ("kn_ready", 1), ("decay_step", 3), ("gate_step", 3), ("root_in", 1), ("root_ready", 1),
            ("wkv_in", 4), ("rkx_ready", 1), ("blocks_grown", 2 * len(LEVELS)), ("block_decay_ready", len(LEVELS)),
            ("inv_base", 1), ("inv_start", 1), ("A_level_ready", len(LEVELS) - 1), ("state_step", 1),
            ("gn_stats_ready", NU), ("gn_mom_ready", NU), ("y_step", 4), ("bonus_v_ready", 1), ("z_step", 2), ("z_ready", 1), ("av_done", NB * NPAIR),
            ("top_ready0", 3), ("gap_ready0", 1), ("top_exp0", 1), ("top_w_step0", 3), ("hot_step0", 2), ("comb_ready0", 1),
            ("top_ready1", 3), ("gap_ready1", 1), ("top_exp1", 1), ("top_w_step1", 3), ("hot_step1", 2), ("comb_ready1", 1),
            ("norm_stats1", NB), ("norm_moments1", NB), ("norm_var1", 1), ("norm_root1", 1), ("norm_rstd1", 1), ("gn_var", 1), ("gn_root", 1), ("norm_sq", 1), ("norm_root", 1),
            ("x1n_ready", NB), ("fronts_kept", 2), ("neg_max_ready", NB * NPAIR), ("mask_kept", 1),
            ("prob_inv_ready", NB), ("tile_done", 1),
        ]:
            step(name, n)

        def made(i, name, k=None):
            s, n = per_tile[name]
            return s, i * n + (n if k is None else k)

        def last_tile(i):
            return per_tile["tile_done"][0], i + 1

        def makes(name):
            counted[name] = counted.get(name, 0) + 1
            return per_tile[name][0], 1

        def settle(eng):
            eng.sem_inc(settled, 1)

        block = ctx.enter_context(nc.Block())

        loads = [
            (xA, io["x_A"]), (xB_lo, io["x_B_lo"]), (xB_hi, io["x_B_hi"]), (lam, io["lambdas"]),
            *[(vec[n], io[n]) for n in VECS],
            *[(lowA[g], io[f"{g}_A"]) for g in "wkag"], *[(lowB[g], io[f"{g}_B"]) for g in "wkag"],
            *[(proj[g], io[f"{g}W_T"]) for g in "rkvo"],
            (Wr, io["Wr"]), (W1, io["W1"]), (W3, io["W3"]), (W2, io["W2"]),
            *[(attnW[g], io[f"W{g}"]) for g in "qkvo"], (gateW, io["gateW"]), (F1, io["F1"]), (F2, io["F2"]),
        ]

        @block.sync
        def _(sp):
            sp.dma_start(x_tile[:], x_dram[:, 0:P, :].rearrange("b t d -> t b d")).then_inc(x_in, 16)
            for dst, src in loads:
                sp.dma_start(dst[:], src[:]).then_inc(weights_in, 16)
            for dst, src in ((gamma, io["gn_gamma"]), (beta, io["gn_beta"])):
                sp.dma_start(dst[:], src[:].partition_broadcast(P)).then_inc(weights_in, 16)
            with sp.Fori(0, NT) as i:
                sp.wait_ge(*is_taken(i, "o0"))
                sp.dma_start(x_tile[:], x_dram[:, bass.ds(sp.snap((i + 1) % NT * P), P), :].rearrange("b t d -> t b d")).then_inc(x_in, 16)
                sp.wait_ge(per_tile["tile_done"][0], i + 2)
                sp.dma_start(out[:, bass.ts(i, P), :].rearrange("b t d -> t b d"), out_tile[:]).then_inc(out_done, 16)
            sp.wait_ge(out_done, 16 * NT + 16)

        @block.gpsimd
        def _(pool):
            for s in bank_taken + [per_tile["tile_done"][0]]:
                pool.sem_inc(s, 1)
            pool.sem_inc(out_done, 16)
            n = 0

            def link(ins):
                nonlocal n
                n += 1
                ins.then_inc(const_step, 1)
                pool.wait_ge(const_step, n)

            link(pool.memset(ident[:], 0.0))
            link(pool.affine_select(out=ident[:], in_=ident[:], compare_op=ALU.not_equal, fill=1.0, base=0,
                                    pattern=[[-1, P]], channel_multiplier=1))
            link(pool.tensor_copy(ident16[:], ident[:]))
            link(pool.memset(ones[:], 1.0))
            link(pool.memset(head_ones[:], 1.0))
            link(pool.affine_select(out=head_ones[:, 0:1], in_=head_ones[:, 0:1], compare_op=ALU.is_ge, fill=0.0,
                                    base=HS - 1, pattern=[[0, 1]], channel_multiplier=-1))
            link(pool.affine_select(out=head_ones[:, 1:2], in_=head_ones[:, 1:2], compare_op=ALU.is_ge, fill=0.0,
                                    base=-HS, pattern=[[0, 1]], channel_multiplier=1))
            link(pool.memset(group_head[:], 0.0))
            for grp in range(P // 32):
                for j in range(HPG):
                    lo = 32 * grp + D1 * j
                    link(pool.affine_select(out=level_mask[:, 0, 0:1], in_=ones[:, 0:1], compare_op=ALU.is_ge, fill=0.0,
                                            base=-lo, pattern=[[0, 1]], channel_multiplier=1))
                    link(pool.affine_select(out=level_mask[:, 0, 0:1], in_=level_mask[:, 0, 0:1], compare_op=ALU.is_ge,
                                            fill=0.0, base=lo + D1 - 1, pattern=[[0, 1]], channel_multiplier=-1))
                    link(pool.tensor_tensor(group_head[:, j:j + 1], group_head[:, j:j + 1], level_mask[:, 0, 0:1], ALU.add))
            link(pool.tensor_scalar(group_head[:], group_head[:], float(D1) ** -0.5, None, ALU.mult))
            link(pool.memset(level_mask[:], 0.0))
            for m, L in enumerate(LEVELS):
                v = level_mask[:, m, :].rearrange("p (g h t) -> p g h t", h=2, t=L)[:, :, 1, :]
                G = P // (2 * L)
                link(pool.memset(v, 1.0))
                link(pool.affine_select(out=v, in_=v, compare_op=ALU.is_ge, fill=0.0, base=0,
                                        pattern=[[-2 * L, G], [0, L]], channel_multiplier=1))
                link(pool.affine_select(out=v, in_=v, compare_op=ALU.is_ge, fill=0.0, base=L - 1,
                                        pattern=[[2 * L, G], [0, L]], channel_multiplier=-1))
            link(pool.iota(expert_no[:], pattern=[[1, NE]], base=0, channel_multiplier=0,
                           allow_small_or_imprecise_dtypes=True))
            link(pool.memset(key_mask[:], 0.0))
            link(pool.affine_select(out=key_mask[:], in_=key_mask[:], compare_op=ALU.is_ge, fill=MASKED, base=WIN,
                                    pattern=[[0, 2], [-1, KEYS]], channel_multiplier=1))
            link(pool.affine_select(out=key_mask[:], in_=key_mask[:], compare_op=ALU.is_ge, fill=MASKED, base=-1,
                                    pattern=[[0, 2], [1, KEYS]], channel_multiplier=-1))
            link(pool.affine_select(out=key_mask_now[:], in_=key_mask[:], compare_op=ALU.is_ge, fill=MASKED, base=-WIN,
                                    pattern=[[0, 2], [1, KEYS]], channel_multiplier=0))
            link(pool.memset(A[:], 0.0))
            link(pool.memset(state[:], 0.0))
            link(pool.memset(xnT[:, :, P:P + 1], 0.0))
            link(pool.memset(x1nT[:, :, P:KEYS], 0.0))
            link(pool.memset(kT1[:, :, P:KEYS], 0.0))
            pool.wait_ge(weights_in, 16 * (len(loads) + 2))
            link(pool.tensor_scalar(neg_w_miu[:], vec["w_miu"][:], -1.0, None, ALU.mult))
            pool.tensor_scalar(neg_a_time[:], vec["a_time"][:], -1.0, None, ALU.mult).then_inc(consts, 1)

            with pool.Fori(0, NT) as i:
                pool.wait_ge(*last_tile(i))
                settle(pool)
                pool.tensor_copy(xnT[:, :, 0:1], xnT[:, :, P:P + 1]).then_inc(*makes("front_kept"))
                for g in range(NG):
                    pool.wait_ge(*is_taken(i, f"miu{g}"))
                    pool.tensor_tensor(xd[:, g, :].rearrange("p (b t) -> p b t", b=NB), xnT[:, :, 1:1 + P],
                                            xd[:, g, :].rearrange("p (b t) -> p b t", b=NB), ALU.add).then_inc(*makes("xd_ready"))
                pool.wait_ge(*is_taken(i, "k"))
                pool.tensor_tensor(k_sq[:], k_raw[:], k_raw[:], ALU.mult).then_inc(*makes("k_sq_ready"))
                for n, L in enumerate(LEVELS[1:]):
                    if n == 0:
                        pool.wait_ge(*made(i, "inv_base"))
                    else:
                        pool.wait_ge(*is_filled(i, f"inv{LEVELS[n]}Z1"))
                    pool.tensor_tensor(A_level[:], A[:, :, 3, :],
                                            level_mask[:, n + 1, :].unsqueeze(1).broadcast_to([P, NU, P]), ALU.mult).then_inc(*makes("A_level_ready"))
                pool.wait_ge(*is_taken(i, "bonus"))
                pool.tensor_tensor(bonus_v, v_tok[:].rearrange("p b (h n) -> p (b h) n", h=NH),
                                        bonus[:].unsqueeze(2).broadcast_to([P, NU, HS]), ALU.mult).then_inc(*makes("bonus_v_ready"))
                pool.tensor_copy(x1nT[:, :, 0:WIN], x1nT[:, :, P:KEYS]).then_inc(*makes("fronts_kept"))
                pool.tensor_copy(kT1[:, :, 0:WIN], kT1[:, :, P:KEYS]).then_inc(*makes("fronts_kept"))
                pool.wait_ge(*is_filled(i, f"sc{NB * NPAIR - 1}"))
                settle(pool)
                pool.tensor_copy(key_mask_now[:], key_mask[:]).then_inc(*makes("mask_kept"))

        @block.scalar
        def _(act):
            act.wait_ge(consts, 1)
            with act.Fori(0, NT) as i:
                act.wait_ge(*made(i, "norm_var0"))
                act.activation(rstd[:], rstd[:], ACT.Sqrt).then_inc(*makes("norm_root0"))
                act.wait_ge(*made(i, "front_kept"))
                act.wait_ge(*is_filled(i, "xnT0"))
                act.activation(xnT[:, :, 1:1 + P], bank("xnT0")[:].rearrange("p (b t) -> p b t", b=NB), ACT.Copy).then_inc(*takes("xnT0"))
                act.wait_ge(*made(i, "gap_ready0"))
                act.activation(top_exp[:], top_gap[:], ACT.Exp).then_inc(*makes("top_exp0"))
                act.wait_ge(*is_filled(i, "mixA"))
                act.activation(mixA[:], bank("mixA")[:], ACT.Tanh).then_inc(*takes("mixA"))
                act.wait_ge(*is_filled(i, "mixB"))
                act.activation(mixB[:], bank("mixB")[0:2 * MIXK, :], ACT.Tanh).then_inc(*takes("mixB"))
                for g, f in (("w", ACT.Tanh), ("k", ACT.Tanh), ("a", ACT.Copy), ("g", ACT.Tanh)):
                    m = low[g].shape[0]
                    act.wait_ge(*is_filled(i, f"low_{g}"))
                    act.activation(low[g][:], bank(f"low_{g}")[0:m, :], f).then_inc(*takes(f"low_{g}"))
                act.wait_ge(*is_filled(i, "r"))
                act.activation(r_raw[:], bank("r")[:], ACT.Copy).then_inc(*takes("r"))
                act.wait_ge(*is_filled(i, "w"))
                act.activation(decay[:], bank("w")[:], ACT.Exp, bias=neg_w_miu[:], scale=-1.0).then_inc(*takes("w"))
                act.wait_ge(*is_filled(i, "k"))
                act.activation(k_raw[:], bank("k")[:], ACT.Copy).then_inc(*takes("k"))
                act.wait_ge(*is_filled(i, "a"))
                act.activation(gate_a, bank("a")[:], ACT.Exp, bias=neg_a_time[:], scale=-1.0).then_inc(*takes("a"))
                act.wait_ge(*is_filled(i, "v"))
                act.activation(v_tok[:].rearrange("p b d -> p (b d)"), bank("v")[:], ACT.Copy).then_inc(*takes("v"))
                act.wait_ge(*is_filled(i, "g"))
                act.activation(g_tok[:].rearrange("p b d -> p (b d)"), bank("g")[:], ACT.Copy).then_inc(*takes("g"))
                act.wait_ge(*made(i, "root_in"))
                act.activation(root_decay, root_decay, ACT.Sqrt).then_inc(*makes("root_ready"))
                act.wait_ge(*is_taken(i, "norm"))
                act.activation(kn[:], kn[:], ACT.Sqrt).then_inc(*makes("norm_root"))
                for n in LEVELS[1:]:
                    for q in range(2):
                        act.wait_ge(*is_filled(i, f"inv{n}T{q}"))
                        act.activation(inv[:, 4 * q:4 * q + 4, :].rearrange("p u t -> p (u t)"), bank(f"inv{n}T{q}")[:], ACT.Copy).then_inc(*takes(f"inv{n}T{q}"))
                    for q in range(2):
                        act.wait_ge(*is_filled(i, f"inv{n}Z{q}"))
                        act.activation(AZ[:, 4 * q:4 * q + 4, :].rearrange("p u t -> p (u t)"), bank(f"inv{n}Z{q}")[:], ACT.Copy).then_inc(*takes(f"inv{n}Z{q}"))
                act.wait_ge(*is_filled(i, "btok"))
                act.activation(b_tok.rearrange("p b d -> p (b d)"), bank("btok")[:], ACT.Copy).then_inc(*takes("btok"))
                act.wait_ge(*is_filled(i, "ktok"))
                act.activation(k_tok.rearrange("p b d -> p (b d)"), bank("ktok")[:], ACT.Copy).then_inc(*takes("ktok"))
                act.wait_ge(*is_filled(i, "bonus"))
                act.activation(bonus[:], bank("bonus")[:, 0:NU], ACT.Copy).then_inc(*takes("bonus"))
                for h in range(NH):
                    act.wait_ge(*is_filled(i, f"X{h}"))
                    act.activation(X.rearrange("p (b h) d -> p h b d", h=NH)[:, h], bank(f"X{h}")[:, 0:NB * HS].rearrange("p (b d) -> p b d", b=NB), ACT.Copy).then_inc(*takes(f"X{h}"))
                act.wait_ge(*is_filled(i, "U"))
                act.activation(U.rearrange("p u d -> p (u d)"), bank("U")[:], ACT.Copy).then_inc(*takes("U"))
                for h in range(NH):
                    act.wait_ge(*is_filled(i, f"Y{h}"))
                    act.activation(y[:].rearrange("p (b h) d -> p h b d", h=NH)[:, h], bank(f"Y{h}")[:, 0:NB * HS].rearrange("p (b d) -> p b d", b=NB), ACT.Copy).then_inc(*takes(f"Y{h}"))
                act.wait_ge(*made(i, "gn_var"))
                act.activation(gn_rstd[:], gn_rstd[:], ACT.Sqrt).then_inc(*makes("gn_root"))
                act.wait_ge(*is_filled(i, "zT"))
                act.activation(zT[:], bank("zT")[:], ACT.Copy).then_inc(*takes("zT"))
                for k in range(K0):
                    act.wait_ge(*is_filled(i, f"h0_{k}"))
                    if k >= 2:
                        act.wait_ge(*is_taken(i, f"g0_{k - 2}"))
                    act.activation(act0[:, k % 2, :], bank(f"h0_{k}")[:], ACT.Silu).then_inc(*takes(f"h0_{k}"))
                act.wait_ge(*made(i, "norm_var1"))
                act.activation(rstd[:], rstd[:], ACT.Sqrt).then_inc(*makes("norm_root1"))
                act.wait_ge(*made(i, "fronts_kept"))
                act.wait_ge(*is_filled(i, "xnT1"))
                act.activation(x1nT[:, :, WIN:KEYS], bank("xnT1")[:].rearrange("p (b t) -> p b t", b=NB), ACT.Copy).then_inc(*takes("xnT1"))
                act.wait_ge(*made(i, "gap_ready1"))
                act.activation(top_exp[:], top_gap[:], ACT.Exp).then_inc(*makes("top_exp1"))
                act.wait_ge(*is_filled(i, "q1"))
                for j in range(HPG):
                    ins = act.activation(q1[:, j, :], bank("q1")[:], ACT.Copy, scale=group_head[:, j:j + 1])
                ins.then_inc(*takes("q1"))
                act.wait_ge(*is_filled(i, "k1"))
                act.activation(kT1[:, :, WIN:KEYS], bank("k1")[:].rearrange("p (b t) -> p b t", b=NB), ACT.Copy).then_inc(*takes("k1"))
                act.wait_ge(*is_filled(i, "v1"))
                act.activation(v1[:].rearrange("p b d -> p (b d)"), bank("v1")[:], ACT.Copy).then_inc(*takes("v1"))
                act.wait_ge(*is_filled(i, "v1p"))
                act.activation(v1p.rearrange("p b d -> p (b d)"), bank("v1p")[0:WIN, :], ACT.Copy).then_inc(*takes("v1p"))
                for n in range(NB * NPAIR):
                    b, p = n // NPAIR, n % NPAIR
                    act.wait_ge(*made(i, "neg_max_ready", n + 1))
                    if n >= 3:
                        act.wait_ge(*is_filled(i, f"pt{n - 3}"))
                    for j in range(2):
                        ins = act.activation(prob[:, n % 3, j, :], bank(f"sc{n}")[:, KEYS * j:KEYS * (j + 1)], ACT.Exp,
                                             bias=neg_max[:, n % 3, j:j + 1],
                                             accum_out=prob_sum[:, b, 2 * p + j:2 * p + j + 1])
                    ins.then_inc(*takes(f"sc{n}"))
                act.wait_ge(*is_filled(i, "cT"))
                act.activation(cT[:], bank("cT")[:], ACT.Copy).then_inc(*takes("cT"))
                for k in range(NF * K1):
                    e = k // K1
                    act.wait_ge(*is_filled(i, f"h1_{k}"))
                    if e >= 2 and k % K1 == 0:
                        act.wait_ge(*is_filled(i, f"y1_{e - 2}"))
                    act.activation(hid[:, e % 2, k % K1, :], bank(f"h1_{k}")[:], ACT.Silu).then_inc(*takes(f"h1_{k}"))

        @block.vector
        def _(dve):
            def layer_norm(i, layer, src, dst, ready):
                for b in range(NB):
                    dve.bn_stats(stats[:, b, :], src(b)).then_inc(*makes(f"norm_stats{layer}"))
                for b in range(NB):
                    dve.wait_ge(*made(i, f"norm_stats{layer}", b + 1))
                    settle(dve)
                    dve.bn_aggr(moments[:, b, :], stats[:, b, :]).then_inc(*makes(f"norm_moments{layer}"))
                dve.wait_ge(*made(i, f"norm_moments{layer}"))
                dve.tensor_scalar(rstd[:], moments[:, :, 1], LN_EPS, None, ALU.add).then_inc(*makes(f"norm_var{layer}"))
                dve.wait_ge(*made(i, f"norm_root{layer}"))
                dve.reciprocal(rstd[:], rstd[:]).then_inc(*makes(f"norm_rstd{layer}"))
                dve.wait_ge(*made(i, f"norm_rstd{layer}"))
                for b in range(NB):
                    dve.tensor_scalar(dst[:, b, :], src(b), moments[:, b, 0:1], rstd[:, b:b + 1],
                                           ALU.subtract, ALU.mult).then_inc(*makes(ready))

            def route(i, layer):
                L = str(layer)
                dve.wait_ge(*is_filled(i, "logit" + L))
                dve.tensor_copy(logits[:], bank("logit" + L)[:, 0:NB * NE].rearrange("p (b e) -> p b e", b=NB)).then_inc(*takes("logit" + L))
                dve.wait_ge(*is_taken(i, "logit" + L))
                settle(dve)
                for b in range(NB):
                    ins = dve.max(top[:, b, :], logits[:, b, :])
                ins.then_inc(*makes("top_ready" + L))
                dve.wait_ge(*made(i, "top_ready" + L, 1))
                settle(dve)
                for b in range(NB):
                    ins = dve.max_index(top_at[:, b, :], top[:, b, :], logits[:, b, :])
                ins.then_inc(*makes("top_ready" + L))
                dve.tensor_tensor(top_gap[:], top[:, :, 1], top[:, :, 0], ALU.subtract).then_inc(*makes("gap_ready" + L))
                dve.wait_ge(*made(i, "top_ready" + L, 2))
                dve.tensor_copy(top_atf[:], top_at[:]).then_inc(*makes("top_ready" + L))
                dve.wait_ge(*made(i, "top_exp" + L))
                dve.tensor_scalar(top_sum[:], top_exp[:], 1.0, None, ALU.add).then_inc(*makes("top_w_step" + L))
                dve.wait_ge(*made(i, "top_w_step" + L, 1))
                dve.reciprocal(top_w[:, 0, :], top_sum[:]).then_inc(*makes("top_w_step" + L))
                dve.wait_ge(*made(i, "top_w_step" + L, 2))
                dve.tensor_tensor(top_w[:, 1, :], top_w[:, 0, :], top_exp[:], ALU.mult).then_inc(*makes("top_w_step" + L))
                dve.wait_ge(*made(i, "top_ready" + L))
                for j in range(2):
                    ins = dve.tensor_tensor(hot[:, j], expert_no[:].unsqueeze(1).broadcast_to([P, NB, NE]),
                                            top_atf[:, :, j:j + 1].broadcast_to([P, NB, NE]), ALU.is_equal)
                ins.then_inc(*makes("hot_step" + L))
                dve.wait_ge(*made(i, "hot_step" + L, 1))
                dve.wait_ge(*made(i, "top_w_step" + L))
                for j in range(2):
                    ins = dve.tensor_tensor(hot[:, j], hot[:, j], top_w[:, j, :].unsqueeze(2).broadcast_to([P, NB, NE]), ALU.mult)
                ins.then_inc(*makes("hot_step" + L))
                dve.wait_ge(*made(i, "hot_step" + L))
                dve.tensor_tensor(comb[layer][:], hot[:, 0], hot[:, 1], ALU.add).then_inc(*makes("comb_ready" + L))

            def probs_out(i, n):
                b, p = n // NPAIR, n % NPAIR
                if n >= 2:
                    dve.wait_ge(*made(i, "av_done", n - 1))
                dve.wait_ge(*is_filled(i, f"pt{n}"))
                dve.tensor_copy(pT[:, n % 2], bank(f"pt{n}")[:, 0:2 * P].rearrange("p (j t) -> p j t", j=2))
                dve.tensor_copy(pTp[:, n % 2], bank(f"pt{n}")[0:WIN, 2 * P:2 * KEYS].rearrange("p (j t) -> p j t", j=2)).then_inc(*takes(f"pt{n}"))

            def context_out(i, b):
                dve.reciprocal(prob_inv[:, b, :], prob_sum[:, b, :]).then_inc(*makes("prob_inv_ready"))
                dve.wait_ge(*made(i, "av_done", NPAIR * (b + 1)))
                dve.wait_ge(*made(i, "prob_inv_ready", b + 1))
                dve.tensor_tensor(ctx1[:, b, :].rearrange("p (h d) -> p h d", d=D1),
                                        bank(f"av{b}")[:, 0:P].rearrange("p (h d) -> p h d", d=D1),
                                        prob_inv[:, b, :].unsqueeze(2).broadcast_to([P, H1, D1]), ALU.mult).then_inc(*takes(f"av{b}"))

            def halves(t, L):
                return t[:].rearrange("p s (g h t) -> p s g h t", h=2, t=L)

            dve.wait_ge(consts, 1)
            with dve.Fori(0, NT) as i:
                dve.wait_ge(*last_tile(i))
                dve.wait_ge(x_in, 16 * i + 16)
                layer_norm(i, 0, lambda b: x_tile[:, b, :], xn, "xn_ready")
                dve.wait_ge(*is_taken(i, "xnT0"))
                dve.tensor_tensor(dx[:], xnT[:, :, 0:P], xnT[:, :, 1:1 + P], ALU.subtract).then_inc(*makes("dx_ready"))
                dve.wait_ge(*made(i, "dx_ready"))
                dve.scalar_tensor_tensor(out=xm[:].rearrange("p (b t) -> p b t", b=NB), in0=dx[:], scalar=vec["x_miu"][:],
                                              in1=xnT[:, :, 1:1 + P], op0=ALU.mult, op1=ALU.add).then_inc(*makes("xm_ready"))
                route(i, 0)
                for g in range(NG):
                    dve.wait_ge(*is_filled(i, f"miu{g}"))
                    dve.scalar_tensor_tensor(out=xd[:, g, :], in0=bank(f"miu{g}")[:], scalar=lam[:, g:g + 1],
                                                   in1=dx[:].rearrange("p b t -> p (b t)"), op0=ALU.add, op1=ALU.mult).then_inc(*takes(f"miu{g}"))
                dve.wait_ge(*is_taken(i, "w"))
                dve.tensor_scalar(decay[:], decay[:], 1.0, None, ALU.add).then_inc(*makes("decay_step"))
                dve.wait_ge(*made(i, "decay_step", 1))
                dve.reciprocal(decay[:], decay[:]).then_inc(*makes("decay_step"))
                dve.wait_ge(*made(i, "decay_step", 2))
                dve.tensor_scalar(decay[:], decay[:], float(np.exp(-0.5)), None, ALU.mult).then_inc(*makes("decay_step"))
                dve.wait_ge(*made(i, "decay_step"))
                dve.tensor_scalar(root_decay, decay[:], 2.0 ** -116, None, ALU.max).then_inc(*makes("root_in"))
                dve.wait_ge(*is_taken(i, "a"))
                dve.tensor_scalar(gate_a, gate_a, 1.0, None, ALU.add).then_inc(*makes("gate_step"))
                dve.wait_ge(*made(i, "gate_step", 1))
                dve.reciprocal(gate_a, gate_a).then_inc(*makes("gate_step"))
                dve.wait_ge(*made(i, "gate_step", 2))
                dve.tensor_scalar(gate_a, gate_a, 2.0, None, ALU.mult).then_inc(*makes("gate_step"))
                dve.wait_ge(*is_filled(i, "norm"))
                dve.tensor_scalar(kn[:], bank("norm")[:], 1e-24, None, ALU.max).then_inc(*takes("norm"))
                dve.wait_ge(*made(i, "norm_root"))
                dve.reciprocal(kn[:], kn[:]).then_inc(*makes("norm_sq"))
                dve.wait_ge(*made(i, "norm_sq"))
                dve.tensor_tensor(kn[:], k_raw[:], kn[:], ALU.mult).then_inc(*makes("kn_ready"))
                dve.wait_ge(*made(i, "kn_ready"))
                dve.wait_ge(*made(i, "root_ready"))
                dve.wait_ge(*made(i, "gate_step"))
                dve.tensor_tensor(bk[:, 0, :], kn[:], root_decay, ALU.mult).then_inc(*makes("wkv_in"))
                dve.tensor_tensor(bk[:, 1, :], kn[:], gate_a, ALU.mult).then_inc(*makes("wkv_in"))
                dve.tensor_scalar(ra[:, 1, :], kn[:], -1.0, None, ALU.mult).then_inc(*makes("wkv_in"))
                dve.tensor_tensor(ra[:, 0, :], r_raw[:], decay[:], ALU.mult).then_inc(*makes("wkv_in"))
                dve.scalar_tensor_tensor(out=rkx[:], in0=r_raw[:], scalar=vec["x_time"][:], in1=kn[:],
                                              op0=ALU.mult, op1=ALU.mult).then_inc(*makes("rkx_ready"))

                def keep_level(m, L):
                    for u in range(NU):
                        name = f"lev{L}_{u}"
                        dve.wait_ge(*is_filled(i, name))
                        if L == 0:
                            dst = A[:, u].rearrange("p (s q) t -> p s q t", s=2)[:, :, 0, :]
                            mask = ident[:].bitcast(I32).unsqueeze(1).broadcast_to([P, 2, P])
                            src = bank(name)[:, 0:2 * P].rearrange("p (s t) -> p s t", s=2)
                        else:
                            dst = A[:, u]
                            mask = level_mask[:, m, :].bitcast(I32).unsqueeze(1).broadcast_to([P, 4, P])
                            src = bank(name)[:].rearrange("p (s t) -> p s t", s=4)
                        settle(dve)
                        dve.copy_predicated(dst, mask, src).then_inc(*takes(name))

                keep_level(None, 0)
                for m, L in enumerate(LEVELS):
                    keep_level(m, L)
                    G = TOK // (2 * L)
                    d = decay[:] if L == 1 else block_decay[L][:]
                    dv = d.rearrange("p (g h) -> p g h", h=2)
                    if L > 1:
                        dve.wait_ge(*made(i, "block_decay_ready", m))
                        dve.wait_ge(*made(i, "blocks_grown", 2 * m))
                    v = halves(ra, L)[:, :, :, 1, :]
                    dve.tensor_tensor(v, v, dv[:, :, 0:1].unsqueeze(1).broadcast_to([P, 2, G, L]), ALU.mult).then_inc(*makes("blocks_grown"))
                    v = halves(bk, L)[:, :, :, 0, :]
                    dve.tensor_tensor(v, v, dv[:, :, 1:2].unsqueeze(1).broadcast_to([P, 2, G, L]), ALU.mult).then_inc(*makes("blocks_grown"))
                    dve.tensor_tensor(block_decay[2 * L][:], dv[:, :, 0], dv[:, :, 1], ALU.mult).then_inc(*makes("block_decay_ready"))
                for u in range(NU):
                    dve.wait_ge(*is_taken(i, f"lev{LEVELS[-1]}_{u}"))
                dve.tensor_tensor(invT[:], A[:, :, 3, :], level_mask[:, 0, :].unsqueeze(1).broadcast_to([P, NU, P]), ALU.mult).then_inc(*makes("inv_base"))
                dve.wait_ge(*made(i, "inv_base"))
                dve.tensor_tensor(invT[:], invT[:], ident[:].unsqueeze(1).broadcast_to([P, NU, P]), ALU.add).then_inc(*makes("inv_start"))
                for n in LEVELS[1:]:
                    for q in range(2):
                        dve.wait_ge(*is_filled(i, f"inv{n}D{q}"))
                        v = invT[:, 4 * q:4 * q + 4, :].rearrange("p u t -> p (u t)")
                        dve.tensor_tensor(v, v, bank(f"inv{n}D{q}")[:], ALU.add).then_inc(*takes(f"inv{n}D{q}"))
                D = block_decay[2 * LEVELS[-1]]
                dve.wait_ge(*made(i, "block_decay_ready"))
                dve.tensor_tensor(state_dec[:], state[:], D[:].unsqueeze(2).broadcast_to([P, NB, HS]), ALU.mult).then_inc(*makes("state_step"))
                dve.wait_ge(*made(i, "state_step", 1))
                dve.wait_ge(*is_filled(i, "S"))
                dve.tensor_tensor(state[:], state_dec[:], bank("S")[:, 0:NB * HS].rearrange("p (b d) -> p b d", b=NB), ALU.add).then_inc(*takes("S"))
                dve.wait_ge(*is_taken(i, "Y0"))
                dve.wait_ge(*is_taken(i, "Y1"))
                for u in range(NU):
                    dve.bn_stats(gn_stats[:, u, :], y[:, u, :]).then_inc(*makes("gn_stats_ready"))
                for u in range(NU):
                    dve.wait_ge(*made(i, "gn_stats_ready", u + 1))
                    settle(dve)
                    dve.bn_aggr(gn_mom[:, u, :], gn_stats[:, u, :]).then_inc(*makes("gn_mom_ready"))
                dve.wait_ge(*made(i, "gn_mom_ready"))
                dve.tensor_scalar(gn_rstd[:], gn_mom[:, :, 1], GN_EPS, None, ALU.add).then_inc(*makes("gn_var"))
                dve.wait_ge(*made(i, "gn_root"))
                dve.reciprocal(gn_rstd[:], gn_rstd[:]).then_inc(*makes("y_step"))
                dve.tensor_tensor(y_mul[:], y[:], gn_mom[:, :, 0:1].broadcast_to([P, NU, HS]), ALU.subtract).then_inc(*makes("y_step"))
                dve.wait_ge(*made(i, "y_step", 2))
                dve.tensor_tensor(y_mul[:], y_mul[:], gn_rstd[:].unsqueeze(2).broadcast_to([P, NU, HS]), ALU.mult).then_inc(*makes("y_step"))
                dve.wait_ge(*made(i, "y_step", 3))
                ym = y_mul[:].rearrange("p (b h) d -> p b (h d)", h=NH)
                dve.tensor_tensor(ym, ym, gamma[:].unsqueeze(1).broadcast_to([P, NB, P]), ALU.mult).then_inc(*makes("y_step"))
                dve.wait_ge(*made(i, "y_step", 4))
                dve.tensor_tensor(ym, ym, beta[:].unsqueeze(1).broadcast_to([P, NB, P]), ALU.add).then_inc(*makes("z_step"))
                dve.wait_ge(*made(i, "z_step", 1))
                dve.wait_ge(*made(i, "bonus_v_ready"))
                dve.tensor_tensor(y_mul[:], y_mul[:], bonus_v, ALU.add).then_inc(*makes("z_step"))
                dve.wait_ge(*made(i, "z_step", 2))
                dve.wait_ge(*is_taken(i, "g"))
                dve.tensor_tensor(ym, ym, g_tok[:], ALU.mult).then_inc(*makes("z_ready"))
                dve.wait_ge(*is_filled(i, "o0"))
                dve.tensor_tensor(acc0[:], x_tile[:],
                                        bank("o0")[:].rearrange("p (b d) -> p b d", b=NB), ALU.add).then_inc(*takes("o0"))
                for j in range(NE // 2):
                    for k in range(PAIR_TILES * j, PAIR_TILES * (j + 1)):
                        dve.wait_ge(*is_taken(i, f"h0_{k}"))
                        dve.wait_ge(*is_filled(i, f"g0_{k}"))
                        ins = dve.tensor_tensor(hid[:, j % 2, k % PAIR_TILES, :], act0[:, k % 2, :], bank(f"g0_{k}")[:], ALU.mult)
                        ins.then_inc(*takes(f"g0_{k}"))
                    for e in (2 * j, 2 * j + 1):
                        dve.wait_ge(*is_filled(i, f"y0_{e}"))
                        dve.wait_ge(*is_taken(i, f"y0_{e - 1}" if e else "o0"))
                        for b in range(NB):
                            ins = dve.scalar_tensor_tensor(out=acc0[:, b, :], in0=bank(f"y0_{e}")[:, b * P:(b + 1) * P],
                                                           scalar=comb[0][:, b, e:e + 1], in1=acc0[:, b, :],
                                                           op0=ALU.mult, op1=ALU.add)
                        ins.then_inc(*takes(f"y0_{e}"))
                dve.wait_ge(*is_taken(i, f"y0_{NE - 1}"))
                layer_norm(i, 1, lambda b: acc0[:, b, :], x1n, "x1n_ready")
                route(i, 1)
                for n in range(NB * NPAIR):
                    dve.wait_ge(*is_filled(i, f"sc{n}"))
                    if n >= 3:
                        dve.wait_ge(*is_taken(i, f"sc{n - 3}"))
                    dve.tensor_reduce(neg_max[:, n % 3, :], bank(f"sc{n}")[:, 0:2 * KEYS].rearrange("p (j s) -> p j s", j=2),
                                           AX.X, ALU.max, negate=True).then_inc(*makes("neg_max_ready"))
                    if n >= 2:
                        probs_out(i, n - 2)
                    if n >= 4 and (n - 4) % NPAIR == NPAIR - 1:
                        context_out(i, (n - 4) // NPAIR)
                probs_out(i, NB * NPAIR - 2)
                probs_out(i, NB * NPAIR - 1)
                context_out(i, NB - 1)
                dve.wait_ge(*is_filled(i, "o1"))
                dve.tensor_tensor(acc1[:], acc0[:], bank("o1")[:].rearrange("p (b d) -> p b d", b=NB), ALU.add).then_inc(*takes("o1"))
                for e in range(NF):
                    dve.wait_ge(*is_filled(i, f"y1_{e}"))
                    dve.wait_ge(*is_taken(i, f"y1_{e - 1}" if e else "o1"))
                    if e == 0:
                        dve.tensor_tensor(acc1[:], acc1[:], bank("y1_0")[:].rearrange("p (b d) -> p b d", b=NB), ALU.add).then_inc(*takes("y1_0"))
                        continue
                    for b in range(NB):
                        ins = dve.scalar_tensor_tensor(out=acc1[:, b, :], in0=bank(f"y1_{e}")[:, b * P:(b + 1) * P],
                                                       scalar=comb[1][:, b, e - 1:e], in1=acc1[:, b, :],
                                                       op0=ALU.mult, op1=ALU.add)
                    ins.then_inc(*takes(f"y1_{e}"))
                dve.wait_ge(*is_taken(i, f"y1_{NF - 1}"))
                dve.wait_ge(out_done, 16 * i + 16)
                dve.tensor_copy(out_tile[:], acc1[:]).then_inc(*makes("tile_done"))

        @block.tensor
        def _(pe):
            def mm(dst, lhsT, rhs, start=True, stop=True, onto=False):
                return pe.matmul(dst, lhsT, rhs, start=start, stop=stop, skip_group_check=onto)

            def cols(b, n=P):
                return slice(b * n, (b + 1) * n)

            def rows(h):
                return slice(h * HS, (h + 1) * HS)

            pe.wait_ge(consts, 1)
            with pe.Fori(0, NT) as i:
                pe.wait_ge(*is_free(i, "xnT0"))
                for b in range(NB):
                    pe.wait_ge(*made(i, "xn_ready", b + 1))
                    ins = pe.transpose(bank("xnT0")[:, cols(b)], xn[:, b, :], ident[:])
                ins.then_inc(*fills("xnT0"))
                pe.wait_ge(*is_taken(i, "xnT0"))
                pe.wait_ge(*is_free(i, "logit0"))
                for b in range(NB):
                    ins = mm(bank("logit0")[:, cols(b, NE)], xnT[:, b, 1:1 + P], Wr[:])
                ins.then_inc(*fills("logit0"))
                pe.wait_ge(*made(i, "xm_ready"))
                pe.wait_ge(*is_free(i, "mixA"))
                mm(bank("mixA")[:], xA[:, 0:P], xm[:]).then_inc(*fills("mixA"))
                pe.wait_ge(*is_free(i, "mixB"))
                mm(bank("mixB")[0:2 * MIXK, :], xA[:, P:NG * MIXK], xm[:]).then_inc(*fills("mixB"))
                for g in range(NG):
                    pe.wait_ge(*is_taken(i, "mixA" if g < 4 else "mixB"))
                    pe.wait_ge(*is_free(i, f"miu{g}"))
                    w, m, at = (xB_lo, mixA, g) if g < 4 else (xB_hi, mixB, g - 4)
                    r = slice(MIXK * at, MIXK * (at + 1))
                    mm(bank(f"miu{g}")[:], w[r, :], m[r, :]).then_inc(*fills(f"miu{g}"))
                at = {g: n for n, g in enumerate("rwkvag")}
                for g in "wkag":
                    pe.wait_ge(*made(i, "xd_ready", at[g] + 1))
                    pe.wait_ge(*is_free(i, f"low_{g}"))
                    mm(bank(f"low_{g}")[0:low[g].shape[0], :], lowA[g][:], xd[:, at[g], :]).then_inc(*fills(f"low_{g}"))
                pe.wait_ge(*is_free(i, "r"))
                mm(bank("r")[:], proj["r"][:], xd[:, at["r"], :]).then_inc(*fills("r"))
                pe.wait_ge(*is_taken(i, "low_w"))
                pe.wait_ge(*is_free(i, "w"))
                mm(bank("w")[:], lowB["w"][:], low["w"][:]).then_inc(*fills("w"))
                pe.wait_ge(*is_free(i, "k"))
                mm(bank("k")[:], proj["k"][:], xd[:, at["k"], :], stop=False)
                pe.wait_ge(*is_taken(i, "low_k"))
                mm(bank("k")[:], lowB["k"][:], low["k"][:], start=False).then_inc(*fills("k"))
                pe.wait_ge(*is_taken(i, "low_a"))
                pe.wait_ge(*is_free(i, "a"))
                mm(bank("a")[:], lowB["a"][:], low["a"][:]).then_inc(*fills("a"))
                pe.wait_ge(*is_free(i, "v"))
                for b in range(NB):
                    ins = mm(bank("v")[:, cols(b)], xd[:, at["v"], cols(b)], proj["v"][:])
                ins.then_inc(*fills("v"))
                pe.wait_ge(*is_taken(i, "low_g"))
                pe.wait_ge(*is_free(i, "g"))
                for b in range(NB):
                    ins = mm(bank("g")[:, cols(b)], low["g"][:, cols(b)], lowB["g"][:])
                ins.then_inc(*fills("g"))
                pe.wait_ge(*made(i, "k_sq_ready"))
                pe.wait_ge(*is_free(i, "norm"))
                mm(bank("norm")[:], ones[:], k_sq[:]).then_inc(*fills("norm"))
                pe.wait_ge(*made(i, "wkv_in"))
                pe.wait_ge(*is_taken(i, "r"))
                for m, L in enumerate([0] + LEVELS):
                    if L > 1:
                        pe.wait_ge(*made(i, "blocks_grown", 2 * (m - 1)))
                    for u in range(NU):
                        b, h = u // NH, u % NH
                        name = f"lev{L}_{u}"
                        pe.wait_ge(*is_free(i, name))
                        for s in range(2):
                            if L == 0:
                                ins = mm(bank(name)[:, cols(s)], bk[rows(h), s, cols(b)], r_raw[rows(h), cols(b)])
                            else:
                                ins = mm(bank(name)[:, cols(s, 2 * P)], bk[rows(h), s, cols(b)], ra[rows(h), :, cols(b)])
                        ins.then_inc(*fills(name))
                for n, L in enumerate(LEVELS[1:]):
                    for q in range(2):
                        name = f"inv{L}T{q}"
                        if n == 0:
                            pe.wait_ge(*made(i, "inv_start"))
                        else:
                            pe.wait_ge(*is_taken(i, f"inv{LEVELS[n]}D{q}"))
                        pe.wait_ge(*is_free(i, name))
                        for u in range(4):
                            ins = pe.transpose(bank(name)[:, cols(u)], invT[:, 4 * q + u, :], ident[:])
                        ins.then_inc(*fills(name))
                    pe.wait_ge(*made(i, "A_level_ready", n + 1))
                    for q in range(2):
                        name = f"inv{L}Z{q}"
                        pe.wait_ge(*is_taken(i, f"inv{L}T{q}"))
                        pe.wait_ge(*is_free(i, name))
                        for u in range(4):
                            ins = mm(bank(name)[:, cols(u)], A_level[:, 4 * q + u, :], inv[:, 4 * q + u, :])
                        ins.then_inc(*fills(name))
                    for q in range(2):
                        name = f"inv{L}D{q}"
                        pe.wait_ge(*is_taken(i, f"inv{L}Z{q}"))
                        pe.wait_ge(*is_free(i, name))
                        for u in range(4):
                            ins = mm(bank(name)[:, cols(u)], AZ[:, 4 * q + u, :], invT[:, 4 * q + u, :])
                        ins.then_inc(*fills(name))
                pe.wait_ge(*made(i, "blocks_grown"))
                for name, s in (("btok", 1), ("ktok", 0)):
                    pe.wait_ge(*is_free(i, name))
                    for b in range(NB):
                        ins = pe.transpose(bank(name)[:, cols(b)], bk[:, s, cols(b)], ident[:])
                    ins.then_inc(*fills(name))
                pe.wait_ge(*made(i, "rkx_ready"))
                pe.wait_ge(*is_free(i, "bonus"))
                for b in range(NB):
                    ins = mm(bank("bonus")[:, cols(b, NH)], rkx[:, cols(b)], head_ones[:])
                ins.then_inc(*fills("bonus"))
                pe.wait_ge(*is_taken(i, "v"))
                for h in range(NH):
                    pe.wait_ge(*is_free(i, f"X{h}"))
                    for b in range(NB):
                        mm(bank(f"X{h}")[:, cols(b, HS)], ra[rows(h), 1, cols(b)], state[rows(h), b, :], stop=False)
                        ins = mm(bank(f"X{h}")[:, cols(b, HS)], A[:, NH * b + h, 1, :], v_tok[:, b, rows(h)], start=False)
                    ins.then_inc(*fills(f"X{h}"))
                pe.wait_ge(*is_taken(i, "X0"))
                pe.wait_ge(*is_taken(i, "X1"))
                pe.wait_ge(*is_taken(i, f"inv{LEVELS[-1]}D1"))
                pe.wait_ge(*is_free(i, "U"))
                for u in range(NU):
                    ins = mm(bank("U")[:, cols(u, HS)], invT[:, u, :], X[:, u, :])
                ins.then_inc(*fills("U"))
                pe.wait_ge(*is_taken(i, "U"))
                for h in range(NH):
                    pe.wait_ge(*is_free(i, f"Y{h}"))
                    for b in range(NB):
                        u = NH * b + h
                        mm(bank(f"Y{h}")[:, cols(b, HS)], ra[rows(h), 0, cols(b)], state[rows(h), b, :], stop=False)
                        mm(bank(f"Y{h}")[:, cols(b, HS)], A[:, u, 2, :], U[:, u, :], start=False, stop=False)
                        ins = mm(bank(f"Y{h}")[:, cols(b, HS)], A[:, u, 0, :], v_tok[:, b, rows(h)], start=False)
                    ins.then_inc(*fills(f"Y{h}"))
                pe.wait_ge(*is_taken(i, "btok"))
                pe.wait_ge(*is_taken(i, "ktok"))
                pe.wait_ge(*is_free(i, "S"))
                for u in range(NU):
                    b, h = u // NH, u % NH
                    mm(bank("S")[rows(h), cols(b, HS)], b_tok[:, b, rows(h)], U[:, u, :], stop=False)
                    ins = mm(bank("S")[rows(h), cols(b, HS)], k_tok[:, b, rows(h)], v_tok[:, b, rows(h)], start=False)
                ins.then_inc(*fills("S"))
                pe.wait_ge(*made(i, "z_ready"))
                pe.wait_ge(*is_free(i, "zT"))
                for b in range(NB):
                    ins = pe.transpose(bank("zT")[:, cols(b)], y_mul[:, NH * b:NH * (b + 1), :].rearrange("p h d -> p (h d)"), ident[:])
                ins.then_inc(*fills("zT"))
                pe.wait_ge(*is_taken(i, "zT"))
                pe.wait_ge(*is_free(i, "o0"))
                for b in range(NB):
                    ins = mm(bank("o0")[:, cols(b)], zT[:, cols(b)], proj["o"][:])
                ins.then_inc(*fills("o0"))
                for j in range(NE // 2):
                    for k in range(PAIR_TILES * j, PAIR_TILES * (j + 1)):
                        for name, w in ((f"h0_{k}", W1), (f"g0_{k}", W3)):
                            pe.wait_ge(*is_free(i, name))
                            mm(bank(name)[:], w[:, cols(k)], xnT[:, :, 1:1 + P]).then_inc(*fills(name))
                    for e in (2 * j, 2 * j + 1):
                        pe.wait_ge(*is_taken(i, f"g0_{PAIR_TILES * (j + 1) - 1}"))
                        pe.wait_ge(*is_free(i, f"y0_{e}"))
                        parts = [(0, 0, P), (1, 0, P // 2)] if e % 2 == 0 else [(1, P // 2, P), (2, 0, P)]
                        for b in range(NB):
                            for n, (k, lo, hi) in enumerate(parts):
                                ins = mm(bank(f"y0_{e}")[:, cols(b)], hid[lo:hi, j % 2, k, cols(b)],
                                         W2[lo:hi, PAIR_TILES * j + k, :], start=n == 0, stop=n == 1)
                        ins.then_inc(*fills(f"y0_{e}"))
                pe.wait_ge(*is_free(i, "xnT1"))
                for b in range(NB):
                    pe.wait_ge(*made(i, "x1n_ready", b + 1))
                    ins = pe.transpose(bank("xnT1")[:, cols(b)], x1n[:, b, :], ident[:])
                ins.then_inc(*fills("xnT1"))
                pe.wait_ge(*is_taken(i, "xnT1"))
                pe.wait_ge(*is_free(i, "logit1"))
                for b in range(NB):
                    ins = mm(bank("logit1")[:, cols(b, NE)], x1nT[:, b, WIN:KEYS], gateW[:])
                ins.then_inc(*fills("logit1"))
                for g in "qk":
                    pe.wait_ge(*is_free(i, g + "1"))
                    mm(bank(g + "1")[:], attnW[g][:], x1nT[:, :, WIN:KEYS]).then_inc(*fills(g + "1"))
                pe.wait_ge(*is_free(i, "v1"))
                for b in range(NB):
                    ins = mm(bank("v1")[:, cols(b)], x1nT[:, b, WIN:KEYS], attnW["v"][:])
                ins.then_inc(*fills("v1"))
                pe.wait_ge(*is_free(i, "v1p"))
                for b in range(NB):
                    ins = mm(bank("v1p")[0:WIN, cols(b)], x1nT[:, b, 0:WIN], attnW["v"][:])
                ins.then_inc(*fills("v1p"))

                def scores(n):
                    b, p = n // NPAIR, n % NPAIR
                    if n == 0:
                        pe.wait_ge(*is_taken(i, "k1"))
                        pe.wait_ge(*is_taken(i, "q1"))
                    pe.wait_ge(*is_free(i, f"sc{n}"))
                    mm(bank(f"sc{n}")[:, 0:2 * KEYS], ident16[:], key_mask_now[:].rearrange("p j s -> p (j s)"))
                    for j in range(2):
                        h = 2 * p + j
                        r = slice(32 * (h // HPG), 32 * (h // HPG + 1))
                        ins = mm(bank(f"sc{n}")[:, cols(j, KEYS)], q1[r, h % HPG, cols(b)], kT1[r, b, :], start=False, onto=True)
                    ins.then_inc(*fills(f"sc{n}"))

                def turn(n):
                    pe.wait_ge(*is_taken(i, f"sc{n}"))
                    pe.wait_ge(*is_free(i, f"pt{n}"))
                    for j in range(2):
                        pe.transpose(bank(f"pt{n}")[:, cols(j)], prob[:, n % 3, j, WIN:KEYS], ident[:])
                    for j in range(2):
                        ins = pe.transpose(bank(f"pt{n}")[0:WIN, 2 * P + WIN * j:2 * P + WIN * (j + 1)],
                                           prob[0:WIN, n % 3, j, 0:WIN], ident[0:WIN, 0:WIN])
                    ins.then_inc(*fills(f"pt{n}"))

                def weigh(n):
                    b, p = n // NPAIR, n % NPAIR
                    if n == 0:
                        pe.wait_ge(*is_taken(i, "v1p"))
                    if p == 0:
                        pe.wait_ge(*is_free(i, f"av{b}"))
                    pe.wait_ge(*is_taken(i, f"pt{n}"))
                    for j in range(2):
                        h = 2 * p + j
                        mm(bank(f"av{b}")[:, cols(h, D1)], pT[:, n % 2, j, :], v1[:, b, cols(h, D1)])
                        ins = mm(bank(f"av{b}")[0:WIN, cols(h, D1)], pTp[:, n % 2, j, :], v1p[:, b, cols(h, D1)],
                                 start=False, onto=True)
                    ins.then_inc(*makes("av_done"))

                for n in range(NB * NPAIR + 2):
                    if n < NB * NPAIR:
                        scores(n)
                    if 1 <= n <= NB * NPAIR:
                        turn(n - 1)
                    if n >= 2:
                        weigh(n - 2)
                pe.wait_ge(*is_taken(i, f"av{NB - 1}"))
                pe.wait_ge(*is_free(i, "cT"))
                for b in range(NB):
                    ins = pe.transpose(bank("cT")[:, cols(b)], ctx1[:, b, :], ident[:])
                ins.then_inc(*fills("cT"))
                pe.wait_ge(*is_taken(i, "cT"))
                pe.wait_ge(*is_free(i, "o1"))
                for b in range(NB):
                    ins = mm(bank("o1")[:, cols(b)], cT[:, cols(b)], attnW["o"][:])
                ins.then_inc(*fills("o1"))
                for e in range(NF):
                    for k in range(K1 * e, K1 * (e + 1)):
                        pe.wait_ge(*is_free(i, f"h1_{k}"))
                        mm(bank(f"h1_{k}")[:], F1[:, cols(k)], x1nT[:, :, WIN:KEYS]).then_inc(*fills(f"h1_{k}"))
                    pe.wait_ge(*is_taken(i, f"h1_{K1 * e + K1 - 1}"))
                    pe.wait_ge(*is_free(i, f"y1_{e}"))
                    for b in range(NB):
                        for k in range(K1):
                            ins = mm(bank(f"y1_{e}")[:, cols(b)], hid[:, e % 2, k, cols(b)], F2[:, K1 * e + k, :],
                                     start=k == 0, stop=k == K1 - 1)
                    ins.then_inc(*fills(f"y1_{e}"))

        for name, (_, n) in per_tile.items():
            assert counted.get(name) == n, (name, counted.get(name), n)


def kernel(**inputs):
    import concourse.bacc as _bacc
    from concourse.bass_utils import run_bass_kernel_spmd as _run

    a = {n.removeprefix("L0_attn_"): np.asarray(v) for n, v in inputs.items()}
    f1 = np.concatenate([a["L1_ffn_shared_w1"][None], a["L1_ffn_experts_w1"]])
    f2 = np.concatenate([a["L1_ffn_shared_w2"][None], a["L1_ffn_experts_w2"]])
    laid = {
        "x": a["x"], "x_A": a["x_A"], "x_B_lo": a["x_B"][0:4].reshape(P, P), "x_B_hi": a["x_B"][4:6].reshape(2 * MIXK, P),
        "lambdas": a["lambdas"].reshape(NG, P).T, "gn_gamma": a["gn_gamma"], "gn_beta": a["gn_beta"],
        **{n: a[n].reshape(P, 1) for n in VECS},
        **{f"{g}_{s}": a[f"{g}_{s}"] for g in "wkag" for s in "AB"},
        **{f"{g}W_T": a[f"{g}W"].T for g in "rkvo"},
        "Wr": a["L0_ffn_Wr"],
        "W1": a["L0_ffn_W1"].transpose(1, 0, 2).reshape(P, NE * HID0),
        "W3": a["L0_ffn_W3"].transpose(1, 0, 2).reshape(P, NE * HID0),
        "W2": a["L0_ffn_W2"].reshape(K0, P, P).transpose(1, 0, 2),
        **{f"W{g}": a[f"L1_attn_W{g}"] for g in "qkvo"},
        "gateW": a["L1_ffn_gate_w"].T,
        "F1": f1.transpose(2, 0, 1).reshape(P, NF * K1 * P),
        "F2": f2.reshape(NF, P, K1, P).transpose(3, 0, 2, 1).reshape(P, NF * K1, P),
    }
    nc = _bacc.Bacc("TRN2", target_bir_lowering=False, num_devices=1)
    arrays, io = {}, {}
    for name, v in laid.items():
        arrays[f"in_{name}"] = np.ascontiguousarray(v)
        io[name] = nc.dram_tensor(f"in_{name}", v.shape, mybir.dt.from_np(v.dtype), kind="ExternalInput").ap()
    out = nc.dram_tensor("out", a["x"].shape, F32, kind="ExternalOutput").ap()
    build(nc, io, out)
    r = _run(nc, [arrays], core_ids=[0])
    return r.results[0]["out"]
```

```python
from contextlib import ExitStack

import numpy as np

import concourse.bass as bass
from concourse import mybir

ALU = mybir.AluOpType
ACT = mybir.ActivationFunctionType
AX = mybir.AxisListType
F32 = mybir.dt.float32
BF16 = mybir.dt.bfloat16
I32 = mybir.dt.int32
U32 = mybir.dt.uint32

P = 128
NB = 4
TOK = NB * P
LN_EPS = 1e-5

NG = 6
MIXK = 32
LORA = 64
NH = 2
HS = P // NH
NU = NB * NH
GN_EPS = 1e-5 * NH
LEVELS = [1, 2, 4, 8, 16, 32, 64]

NE = 8
HID0 = 192
K0 = NE * HID0 // P
PAIR_TILES = 2 * HID0 // P

H1 = 16
D1 = P // H1
WIN = 64
KEYS = WIN + P
HPG = 32 // D1
NPAIR = H1 // 2
MASKED = -1.0e30

NF = NE + 1
K1 = 4

EXPERT_FIRST = [("hid", k) for k in range(4)]
EXPERT_SLOTS = [[("out", 0)], [("hid", 4)], [("out", 1)], [("hid", 5)], [], [("hid", 6)], [("out", 2)], [("hid", 7)],
                [("out", 3)], [("hid", 8)], [], [("hid", 9)], [("out", 4)], [("hid", 10)], [], [("hid", 11)]]
EXPERT_LAST = [5, 6, 7]
NPAIRS = NB * NPAIR
STEPS1 = NF * K1 + 2

VECS = ["w_miu", "a_time", "x_miu", "x_time"]


def psum_plan():
    plan, turn = [], [0]

    def use(name, bank=None):
        if bank is None:
            bank = turn[0] % 8
            turn[0] += 1
        plan.append((name, bank))

    for n in ["xnT0", "logit0", "mixA", "mixB"] + [f"miu{g}" for g in range(NG)]:
        use(n)
    for n in ["low_w", "low_k", "low_a", "low_g", "r", "w", "k", "a", "v", "g"]:
        use(n)

    def expert_item(kind, n):
        for name in ((f"h0_{n}", f"g0_{n}") if kind == "hid" else (f"y0_{n}",)):
            use(name)

    use("norm")
    expert_item(*EXPERT_FIRST[0])
    use("norm_inv")
    for item in EXPERT_FIRST[1:]:
        expert_item(*item)
    for s, items in enumerate(EXPERT_SLOTS):
        for w in (2 * s % 4, 2 * s % 4 + 1):
            use(f"lev{([0] + LEVELS)[s // 2]}_{w}")
        for item in items:
            expert_item(*item)
    for n in LEVELS[1:]:
        for s in ("T", "Z", "D"):
            for q in range(2):
                use(f"inv{n}{s}{q}")
    for n in ["btok", "ktok", "bonus", "X0", "X1", "U", "Y0", "Y1", "S"] + [f"y0_{e}" for e in EXPERT_LAST] + ["zT", "o0"]:
        use(n)
    for n in ["xnT1", "logit1", "q1", "k1", "v1", "v1p"]:
        use(n)
    for n in range(STEPS1):
        if n < NPAIRS:
            use(f"sc{n}", n % 2)
        if n < NF * K1:
            use(f"h1_{n}", 5 + n % 2)
        if 1 <= n <= NPAIRS:
            use(f"pt{n - 1}", 2 + (n - 1) % 2)
        if n == 2:
            use("av", 4)
        if n >= K1 + 1 and (n - 1) % K1 == 0:
            use(f"y1_{(n - 1) // K1 - 1}", 7)
        if n == NPAIRS + 2:
            use("cT", 0)
        if n == NPAIRS + 3:
            use("o1", 1)
    return plan


def build(nc, io, out):
    x_dram = io["x"]
    T = x_dram.shape[1]
    NT = T // P
    plan = psum_plan()
    bank_of, turn_of, turns = {}, {}, [0] * 8
    fill_of, fills_of = {}, [0] * 8
    for name, b in plan:
        bank_of[name], turn_of[name], fill_of[name] = b, turns[b], fills_of[b]
        turns[b] += 1
        fills_of[b] += name != "av"

    with ExitStack() as ctx:
        def sb(name, shape, dt=F32):
            return ctx.enter_context(nc.sbuf_tensor(name, shape, dt))

        def sem(name):
            return ctx.enter_context(nc.semaphore(name))

        banks = [ctx.enter_context(nc.psum_tensor(f"bank{b}", [P, 512], F32)) for b in range(8)]
        bank_filled = [sem(f"bank_filled{b}") for b in range(8)]
        bank_taken = [sem(f"bank_taken{b}") for b in range(8)]

        def bank(name):
            return banks[bank_of[name]]

        def is_free(i, name):
            return bank_taken[bank_of[name]], i * turns[bank_of[name]] + turn_of[name] + 1

        def is_filled(i, name):
            return bank_filled[bank_of[name]], i * fills_of[bank_of[name]] + fill_of[name] + 1

        def is_taken(i, name):
            return bank_taken[bank_of[name]], i * turns[bank_of[name]] + turn_of[name] + 2

        def fills(name):
            return bank_filled[bank_of[name]], 1

        def takes(name):
            return bank_taken[bank_of[name]], 1

        x_tile = sb("x_tile", [P, NB, P])
        xA = sb("xA", [P, NG * MIXK])
        xB_lo = sb("xB_lo", [P, P])
        xB_hi = sb("xB_hi", [2 * MIXK, P])
        lowA = {g: sb(f"{g}_A", [P, n]) for g, n in (("w", LORA), ("k", LORA), ("a", LORA), ("g", P))}
        lowB = {g: sb(f"{g}_B", [n, P]) for g, n in (("w", LORA), ("k", LORA), ("a", LORA), ("g", P))}
        proj = {g: sb(f"{g}W_T", [P, P]) for g in "rkvo"}
        lam = sb("lam", [P, NG])
        vec = {n: sb(n, [P, 1]) for n in VECS}
        gamma = sb("gamma", [P, P])
        beta = sb("beta", [P, P])
        Wr = sb("Wr", [P, NE])
        W1 = sb("W1", [P, NE * HID0])
        W3 = sb("W3", [P, NE * HID0])
        W2 = sb("W2", [P, K0, P])
        attnW = {g: sb(f"W{g}", [P, P]) for g in "qkvo"}
        gateW = sb("gateW", [P, NE])
        F1 = sb("F1", [P, NF * K1 * P])
        F2 = sb("F2", [P, NF * K1, P])

        ident = sb("ident", [P, P])
        ident16 = sb("ident16", [P, P], BF16)
        ones = sb("ones", [P, P])
        head_ones = sb("head_ones", [P, NH])
        group_head = sb("group_head", [P, HPG])
        level_mask = sb("level_mask", [P, len(LEVELS), P])
        expert_no = sb("expert_no", [P, NE])
        key_mask = sb("key_mask", [P, 2, KEYS], BF16)
        key_mask_now = sb("key_mask_now", [P, 2, KEYS], BF16)

        xnT = sb("xnT", [P, NB, 1 + P])
        state = sb("state", [P, NB, HS])
        x1nT = sb("x1nT", [P, NB, KEYS])
        kT1 = sb("kT1", [P, NB, KEYS])

        stats = sb("stats", [P, NB, 6])
        moments = sb("moments", [P, NB, 2])
        rstd = sb("rstd", [P, NB])
        dx = sb("dx", [P, NB, P])
        mixA = sb("mixA", [P, TOK])
        mixB = sb("mixB", [2 * MIXK, TOK])
        xd = sb("xd", [P, NG, TOK])
        xn = xd[:, 0, :].rearrange("p (b t) -> p b t", b=NB)
        x1n = xd[:, 1, :].rearrange("p (b t) -> p b t", b=NB)
        ctx1 = xn
        q1 = xd[:, 2:2 + HPG, :]
        low = {g: sb(f"low_{g}", [n, TOK]) for g, n in (("w", LORA), ("k", LORA), ("g", P))}
        low["a"] = mixB
        r_raw = sb("r_raw", [P, TOK])
        k_raw = sb("k_raw", [P, TOK])
        xm = k_raw
        k_sq = sb("k_sq", [P, TOK])
        rkx = k_sq
        kn = sb("kn", [P, TOK])
        norm = sb("norm", [P, NB])
        norm_inv = sb("norm_inv", [P, NB])
        decay = sb("decay", [P, TOK])
        v_tok = sb("v_tok", [P, NB, P])
        g_tok = sb("g_tok", [P, NB, P])
        ra = sb("ra", [P, 2, TOK])
        bk = sb("bk", [P, 2, TOK])
        root_decay, gate_a = bk[:, 0, :], bk[:, 1, :]
        block_decay = {2 * n: sb(f"block_decay{2 * n}", [P, TOK // (2 * n)]) for n in LEVELS}
        norm_diag = xd[:, 0, :].rearrange("p (b t) -> p b t", b=NB)
        A = sb("A", [P, NU, 4, P])
        A_level = sb("A_level", [P, NU, P])
        inv = sb("inv", [P, NU, P])
        invT = sb("invT", [P, NU, P])
        AZ = sb("AZ", [P, NU, P])
        b_tok, k_tok = A_level[:, 0:NB, :], A_level[:, NB:2 * NB, :]
        bonus = sb("bonus", [P, NU])
        XU = AZ[:].rearrange("p (s u) (v d) -> p s (u v) d", s=2, d=HS)
        X, U = XU[:, 0], XU[:, 1]
        y = sb("y", [P, NU, HS])
        gn_stats = sb("gn_stats", [P, NU, 6])
        gn_mom = sb("gn_mom", [P, NU, 2])
        gn_rstd = sb("gn_rstd", [P, NU])
        y_mul = y
        bonus_v = dx[:].rearrange("p b (h d) -> p (b h) d", h=NH)
        zT = sb("zT", [P, TOK])
        state_dec = sb("state_dec", [P, NB, HS])

        logits = sb("logits", [P, NB, NE])
        top = sb("top", [P, NB, 8])
        top_at = sb("top_at", [P, NB, 8], U32)
        top_atf = sb("top_atf", [P, NB, 8])
        top_gap = sb("top_gap", [P, NB])
        top_exp = sb("top_exp", [P, NB])
        top_sum = sb("top_sum", [P, NB])
        top_w = sb("top_w", [P, 2, NB])
        hot = sb("hot", [P, 2, NB, NE])
        comb = [sb(f"comb{l}", [P, NB, NE]) for l in range(2)]
        acc0 = sb("acc0", [P, NB, P])
        act0 = sb("act0", [P, 2, TOK])
        hid = sb("hid", [P, 2, K1, TOK])
        v1 = sb("v1", [P, NB, P])
        v1p = low["k"][:].rearrange("p (b d) -> p b d", b=NB)
        neg_max = sb("neg_max", [P, 3, 2])
        prob = sb("prob", [P, 3, 2, KEYS])
        prob_sum = sb("prob_sum", [P, NB, H1])
        prob_inv = sb("prob_inv", [P, NB, H1])
        pT = sb("pT", [P, 2, 2, P])
        pTp = sb("pTp", [WIN, 2, 2, WIN])
        cT = zT
        acc1 = sb("acc1", [P, NB, P])
        out_tile = sb("out_tile", [P, NB, P])

        weights_in = sem("weights_in")
        x_in = sem("x_in")
        out_done = sem("out_done")
        const_step = sem("const_step")
        consts = sem("consts")
        settled = sem("settled")
        per_tile, counted = {}, {}

        def step(name, n=1):
            per_tile[name] = (sem(name), n)

        for name, n in [
            ("norm_stats0", NB), ("norm_moments0", NB), ("norm_var0", 1), ("norm_root0", 1), ("norm_rstd0", 1), ("xn_ready", NB), ("front_kept", 1), ("dx_ready", 1), ("xm_ready", 1),
            ("xd_ready", NG), ("decay_ready", 1), ("root_ready", 1),
            ("wkv_in", 4), ("rkx_ready", 1), ("blocks_grown", 2 * len(LEVELS)), ("block_decay_ready", len(LEVELS)),
            ("inv_base", 1), ("inv_start", 1), ("A_level_ready", len(LEVELS) - 1), ("state_step", 1),
            ("gn_stats_ready", NU), ("gn_mom_ready", NU), ("y_step", 4), ("bonus_v_ready", 1), ("z_step", 2), ("z_ready", 1), ("av_done", NPAIRS),
            ("top_ready0", 3), ("gap_ready0", 1), ("top_exp0", 1), ("top_w_step0", 3), ("hot_step0", 2), ("comb_ready0", 1),
            ("top_ready1", 3), ("gap_ready1", 1), ("top_exp1", 1), ("top_w_step1", 3), ("hot_step1", 2), ("comb_ready1", 1),
            ("norm_stats1", NB), ("norm_moments1", NB), ("norm_var1", 1), ("norm_root1", 1), ("norm_rstd1", 1), ("gn_var", 1), ("gn_root", 1), ("norm_inv_ready", 1), ("norm_diag_ready", 1), ("norm_root", 1),
            ("x1n_ready", NB), ("fronts_kept", 2), ("neg_max_ready", NPAIRS), ("mask_kept", 1),
            ("prob_inv_ready", 1), ("tanh_done", NF * K1),
        ]:
            step(name, n)

        def made(i, name, k=None):
            s, n = per_tile[name]
            return s, i * n + (n if k is None else k)

        def last_tile(i):
            assert turn_of["o1"] == turns[bank_of["o1"]] - 1
            return bank_taken[bank_of["o1"]], i * turns[bank_of["o1"]] + 1

        def makes(name):
            counted[name] = counted.get(name, 0) + 1
            return per_tile[name][0], 1

        def settle(eng):
            eng.sem_inc(settled, 1)

        block = ctx.enter_context(nc.Block())

        loads = [
            (xA, io["x_A"]), (xB_lo, io["x_B_lo"]), (xB_hi, io["x_B_hi"]), (lam, io["lambdas"]),
            *[(vec[n], io[n]) for n in VECS],
            *[(lowA[g], io[f"{g}_A"]) for g in "wkag"], *[(lowB[g], io[f"{g}_B"]) for g in "wkag"],
            *[(proj[g], io[f"{g}W_T"]) for g in "rkvo"],
            (Wr, io["Wr"]), (W1, io["W1"]), (W3, io["W3"]), (W2, io["W2"]),
            *[(attnW[g], io[f"W{g}"]) for g in "qkvo"], (gateW, io["gateW"]), (F1, io["F1"]), (F2, io["F2"]),
        ]

        @block.sync
        def _(sp):
            sp.dma_start(x_tile[:], x_dram[:, 0:P, :].rearrange("b t d -> t b d")).then_inc(x_in, 16)
            for dst, src in loads:
                sp.dma_start(dst[:], src[:]).then_inc(weights_in, 16)
            for dst, src in ((gamma, io["gn_gamma"]), (beta, io["gn_beta"])):
                sp.dma_start(dst[:], src[:].partition_broadcast(P)).then_inc(weights_in, 16)
            with sp.Fori(0, NT) as i:
                sp.wait_ge(*is_taken(i, "y0_0"))
                sp.dma_start(x_tile[:], x_dram[:, bass.ds(sp.snap((i + 1) % NT * P), P), :].rearrange("b t d -> t b d")).then_inc(x_in, 16)
                sp.wait_ge(*is_taken(i, "o1"))
                sp.dma_start(out[:, bass.ts(i, P), :].rearrange("b t d -> t b d"), out_tile[:]).then_inc(out_done, 16)
            sp.wait_ge(out_done, 16 * NT + 16)

        @block.gpsimd
        def _(pool):
            for s in bank_taken:
                pool.sem_inc(s, 1)
            pool.sem_inc(out_done, 16)
            n = 0

            def link(ins):
                nonlocal n
                n += 1
                ins.then_inc(const_step, 1)
                pool.wait_ge(const_step, n)

            link(pool.memset(ident[:], 0.0))
            link(pool.affine_select(out=ident[:], in_=ident[:], compare_op=ALU.not_equal, fill=1.0, base=0,
                                    pattern=[[-1, P]], channel_multiplier=1))
            link(pool.tensor_copy(ident16[:], ident[:]))
            link(pool.memset(ones[:], 1.0))
            link(pool.memset(head_ones[:], 1.0))
            link(pool.affine_select(out=head_ones[:, 0:1], in_=head_ones[:, 0:1], compare_op=ALU.is_ge, fill=0.0,
                                    base=HS - 1, pattern=[[0, 1]], channel_multiplier=-1))
            link(pool.affine_select(out=head_ones[:, 1:2], in_=head_ones[:, 1:2], compare_op=ALU.is_ge, fill=0.0,
                                    base=-HS, pattern=[[0, 1]], channel_multiplier=1))
            link(pool.memset(group_head[:], 0.0))
            for grp in range(P // 32):
                for j in range(HPG):
                    lo = 32 * grp + D1 * j
                    link(pool.affine_select(out=level_mask[:, 0, 0:1], in_=ones[:, 0:1], compare_op=ALU.is_ge, fill=0.0,
                                            base=-lo, pattern=[[0, 1]], channel_multiplier=1))
                    link(pool.affine_select(out=level_mask[:, 0, 0:1], in_=level_mask[:, 0, 0:1], compare_op=ALU.is_ge,
                                            fill=0.0, base=lo + D1 - 1, pattern=[[0, 1]], channel_multiplier=-1))
                    link(pool.tensor_tensor(group_head[:, j:j + 1], group_head[:, j:j + 1], level_mask[:, 0, 0:1], ALU.add))
            link(pool.tensor_scalar(group_head[:], group_head[:], float(D1) ** -0.5, None, ALU.mult))
            link(pool.memset(level_mask[:], 0.0))
            for m, L in enumerate(LEVELS):
                v = level_mask[:, m, :].rearrange("p (g h t) -> p g h t", h=2, t=L)[:, :, 1, :]
                G = P // (2 * L)
                link(pool.memset(v, 1.0))
                link(pool.affine_select(out=v, in_=v, compare_op=ALU.is_ge, fill=0.0, base=0,
                                        pattern=[[-2 * L, G], [0, L]], channel_multiplier=1))
                link(pool.affine_select(out=v, in_=v, compare_op=ALU.is_ge, fill=0.0, base=L - 1,
                                        pattern=[[2 * L, G], [0, L]], channel_multiplier=-1))
            link(pool.iota(expert_no[:], pattern=[[1, NE]], base=0, channel_multiplier=0,
                           allow_small_or_imprecise_dtypes=True))
            link(pool.memset(key_mask[:], 0.0))
            link(pool.affine_select(out=key_mask[:], in_=key_mask[:], compare_op=ALU.is_ge, fill=MASKED, base=WIN,
                                    pattern=[[0, 2], [-1, KEYS]], channel_multiplier=1))
            link(pool.affine_select(out=key_mask[:], in_=key_mask[:], compare_op=ALU.is_ge, fill=MASKED, base=-1,
                                    pattern=[[0, 2], [1, KEYS]], channel_multiplier=-1))
            link(pool.affine_select(out=key_mask_now[:], in_=key_mask[:], compare_op=ALU.is_ge, fill=MASKED, base=-WIN,
                                    pattern=[[0, 2], [1, KEYS]], channel_multiplier=0))
            link(pool.memset(A[:], 0.0))
            link(pool.memset(state[:], 0.0))
            link(pool.memset(xnT[:, :, P:P + 1], 0.0))
            link(pool.memset(x1nT[:, :, P:KEYS], 0.0))
            pool.memset(kT1[:, :, P:KEYS], 0.0).then_inc(consts, 1)

            with pool.Fori(0, NT) as i:
                pool.wait_ge(*last_tile(i))
                settle(pool)
                pool.tensor_copy(xnT[:, :, 0:1], xnT[:, :, P:P + 1]).then_inc(*makes("front_kept"))
                for g in range(NG):
                    pool.wait_ge(*is_taken(i, f"miu{g}"))
                    pool.tensor_tensor(xd[:, g, :].rearrange("p (b t) -> p b t", b=NB), xnT[:, :, 1:1 + P],
                                            xd[:, g, :].rearrange("p (b t) -> p b t", b=NB), ALU.add).then_inc(*makes("xd_ready"))
                for n, L in enumerate(LEVELS[1:]):
                    if n == 0:
                        pool.wait_ge(*made(i, "inv_base"))
                    else:
                        pool.wait_ge(*is_filled(i, f"inv{LEVELS[n]}Z1"))
                    pool.tensor_tensor(A_level[:], A[:, :, 3, :],
                                            level_mask[:, n + 1, :].unsqueeze(1).broadcast_to([P, NU, P]), ALU.mult).then_inc(*makes("A_level_ready"))
                pool.wait_ge(*is_taken(i, "bonus"))
                pool.tensor_tensor(bonus_v, v_tok[:].rearrange("p b (h n) -> p (b h) n", h=NH),
                                        bonus[:].unsqueeze(2).broadcast_to([P, NU, HS]), ALU.mult).then_inc(*makes("bonus_v_ready"))
                pool.tensor_copy(x1nT[:, :, 0:WIN], x1nT[:, :, P:KEYS]).then_inc(*makes("fronts_kept"))
                pool.tensor_copy(kT1[:, :, 0:WIN], kT1[:, :, P:KEYS]).then_inc(*makes("fronts_kept"))
                pool.wait_ge(*is_filled(i, f"sc{NPAIRS - 1}"))
                settle(pool)
                pool.tensor_copy(key_mask_now[:], key_mask[:]).then_inc(*makes("mask_kept"))

        @block.scalar
        def _(act):
            def silu0(i, k):
                act.wait_ge(*is_filled(i, f"h0_{k}"))
                if k >= 2:
                    act.wait_ge(*is_taken(i, f"g0_{k - 2}"))
                act.activation(act0[:, k % 2, :], bank(f"h0_{k}")[:], ACT.Silu).then_inc(*takes(f"h0_{k}"))

            act.wait_ge(consts, 1)
            act.wait_ge(weights_in, 16 * (len(loads) + 2))
            with act.Fori(0, NT) as i:
                act.wait_ge(*made(i, "norm_var0"))
                act.activation(rstd[:], rstd[:], ACT.Sqrt).then_inc(*makes("norm_root0"))
                act.wait_ge(*made(i, "front_kept"))
                act.wait_ge(*is_filled(i, "xnT0"))
                act.activation(xnT[:, :, 1:1 + P], bank("xnT0")[:].rearrange("p (b t) -> p b t", b=NB), ACT.Copy).then_inc(*takes("xnT0"))
                act.wait_ge(*made(i, "gap_ready0"))
                act.activation(top_exp[:], top_gap[:], ACT.Exp).then_inc(*makes("top_exp0"))
                act.wait_ge(*is_filled(i, "mixA"))
                act.activation(mixA[:], bank("mixA")[:], ACT.Tanh).then_inc(*takes("mixA"))
                act.wait_ge(*is_filled(i, "mixB"))
                act.activation(mixB[:], bank("mixB")[0:2 * MIXK, :], ACT.Tanh).then_inc(*takes("mixB"))
                for g, f in (("w", ACT.Tanh), ("k", ACT.Tanh), ("a", ACT.Copy), ("g", ACT.Tanh)):
                    m = low[g].shape[0]
                    act.wait_ge(*is_filled(i, f"low_{g}"))
                    act.activation(low[g][:], bank(f"low_{g}")[0:m, :], f).then_inc(*takes(f"low_{g}"))
                act.wait_ge(*is_filled(i, "r"))
                act.activation(r_raw[:], bank("r")[:], ACT.Copy).then_inc(*takes("r"))
                act.wait_ge(*is_filled(i, "w"))
                act.activation(decay[:], bank("w")[:], ACT.Sigmoid, bias=vec["w_miu"][:]).then_inc(*takes("w"))
                act.wait_ge(*is_filled(i, "k"))
                act.activation(k_raw[:], bank("k")[:], ACT.Copy)
                act.activation(k_sq[:], bank("k")[:], ACT.Square).then_inc(*takes("k"))
                act.wait_ge(*is_filled(i, "a"))
                act.activation(gate_a, bank("a")[:], ACT.Sigmoid, bias=vec["a_time"][:]).then_inc(*takes("a"))
                act.wait_ge(*is_filled(i, "v"))
                act.activation(v_tok[:].rearrange("p b d -> p (b d)"), bank("v")[:], ACT.Copy).then_inc(*takes("v"))
                act.wait_ge(*is_filled(i, "g"))
                act.activation(g_tok[:].rearrange("p b d -> p (b d)"), bank("g")[:], ACT.Copy).then_inc(*takes("g"))
                act.wait_ge(*is_taken(i, "norm"))
                act.activation(norm[:], norm[:], ACT.Sqrt).then_inc(*makes("norm_root"))
                act.wait_ge(*made(i, "decay_ready"))
                act.activation(root_decay, decay[:], ACT.Sqrt).then_inc(*makes("root_ready"))
                for k in range(K0):
                    silu0(i, k)
                for n in LEVELS[1:]:
                    for q in range(2):
                        act.wait_ge(*is_filled(i, f"inv{n}T{q}"))
                        act.activation(inv[:, 4 * q:4 * q + 4, :].rearrange("p u t -> p (u t)"), bank(f"inv{n}T{q}")[:], ACT.Copy).then_inc(*takes(f"inv{n}T{q}"))
                    for q in range(2):
                        act.wait_ge(*is_filled(i, f"inv{n}Z{q}"))
                        act.activation(AZ[:, 4 * q:4 * q + 4, :].rearrange("p u t -> p (u t)"), bank(f"inv{n}Z{q}")[:], ACT.Copy).then_inc(*takes(f"inv{n}Z{q}"))
                act.wait_ge(*is_filled(i, "btok"))
                act.activation(b_tok.rearrange("p b d -> p (b d)"), bank("btok")[:], ACT.Copy).then_inc(*takes("btok"))
                act.wait_ge(*is_filled(i, "ktok"))
                act.activation(k_tok.rearrange("p b d -> p (b d)"), bank("ktok")[:], ACT.Copy).then_inc(*takes("ktok"))
                act.wait_ge(*is_filled(i, "bonus"))
                act.activation(bonus[:], bank("bonus")[:, 0:NU], ACT.Copy).then_inc(*takes("bonus"))
                for h in range(NH):
                    act.wait_ge(*is_filled(i, f"X{h}"))
                    act.activation(X[:, NB * h:NB * (h + 1)], bank(f"X{h}")[:, 0:NB * HS].rearrange("p (b d) -> p b d", b=NB), ACT.Copy).then_inc(*takes(f"X{h}"))
                act.wait_ge(*is_filled(i, "U"))
                act.activation(U.rearrange("p u d -> p (u d)"), bank("U")[:], ACT.Copy).then_inc(*takes("U"))
                for h in range(NH):
                    act.wait_ge(*is_filled(i, f"Y{h}"))
                    act.activation(y[:].rearrange("p (b h) d -> p h b d", h=NH)[:, h], bank(f"Y{h}")[:, 0:NB * HS].rearrange("p (b d) -> p b d", b=NB), ACT.Copy).then_inc(*takes(f"Y{h}"))
                act.wait_ge(*made(i, "gn_var"))
                act.activation(gn_rstd[:], gn_rstd[:], ACT.Sqrt).then_inc(*makes("gn_root"))
                act.wait_ge(*is_filled(i, "zT"))
                act.activation(zT[:], bank("zT")[:], ACT.Copy).then_inc(*takes("zT"))
                act.wait_ge(*made(i, "norm_var1"))
                act.activation(rstd[:], rstd[:], ACT.Sqrt).then_inc(*makes("norm_root1"))
                act.wait_ge(*made(i, "fronts_kept"))
                act.wait_ge(*is_filled(i, "xnT1"))
                act.activation(x1nT[:, :, WIN:KEYS], bank("xnT1")[:].rearrange("p (b t) -> p b t", b=NB), ACT.Copy).then_inc(*takes("xnT1"))
                act.wait_ge(*made(i, "gap_ready1"))
                act.activation(top_exp[:], top_gap[:], ACT.Exp).then_inc(*makes("top_exp1"))
                act.wait_ge(*is_filled(i, "q1"))
                for j in range(HPG):
                    ins = act.activation(q1[:, j, :], bank("q1")[:], ACT.Copy, scale=group_head[:, j:j + 1])
                ins.then_inc(*takes("q1"))
                act.wait_ge(*is_filled(i, "k1"))
                act.activation(kT1[:, :, WIN:KEYS], bank("k1")[:].rearrange("p (b t) -> p b t", b=NB), ACT.Copy).then_inc(*takes("k1"))
                act.wait_ge(*is_filled(i, "v1"))
                act.activation(v1[:].rearrange("p b d -> p (b d)"), bank("v1")[:], ACT.Copy).then_inc(*takes("v1"))
                act.wait_ge(*is_filled(i, "v1p"))
                act.activation(v1p.rearrange("p b d -> p (b d)"), bank("v1p")[0:WIN, :], ACT.Copy).then_inc(*takes("v1p"))
                for n in range(STEPS1):
                    if n < NF * K1:
                        act.wait_ge(*is_filled(i, f"h1_{n}"))
                        if n >= 2:
                            act.wait_ge(*is_taken(i, f"h1_{n - 2}"))
                        act.activation(act0[:, n % 2, :], bank(f"h1_{n}")[:], ACT.Tanh, scale=0.5).then_inc(*makes("tanh_done"))
                    if n < NPAIRS:
                        b, p = n // NPAIR, n % NPAIR
                        act.wait_ge(*made(i, "neg_max_ready", n + 1))
                        if n >= 3:
                            act.wait_ge(*is_filled(i, f"pt{n - 3}"))
                        for j in range(2):
                            ins = act.activation(prob[:, n % 3, j, :], bank(f"sc{n}")[:, KEYS * j:KEYS * (j + 1)], ACT.Exp,
                                                 bias=neg_max[:, n % 3, j:j + 1],
                                                 accum_out=prob_sum[:, b, 2 * p + j:2 * p + j + 1])
                        ins.then_inc(*takes(f"sc{n}"))
                    if n == NPAIRS + 2:
                        act.wait_ge(*is_filled(i, "cT"))
                        act.activation(cT[:], bank("cT")[:], ACT.Copy).then_inc(*takes("cT"))

        @block.vector
        def _(dve):
            def layer_norm(i, layer, src, dst, ready):
                for b in range(NB):
                    dve.bn_stats(stats[:, b, :], src(b)).then_inc(*makes(f"norm_stats{layer}"))
                for b in range(NB):
                    dve.wait_ge(*made(i, f"norm_stats{layer}", b + 1))
                    settle(dve)
                    dve.bn_aggr(moments[:, b, :], stats[:, b, :]).then_inc(*makes(f"norm_moments{layer}"))
                dve.wait_ge(*made(i, f"norm_moments{layer}"))
                dve.tensor_scalar(rstd[:], moments[:, :, 1], LN_EPS, None, ALU.add).then_inc(*makes(f"norm_var{layer}"))
                dve.wait_ge(*made(i, f"norm_root{layer}"))
                dve.reciprocal(rstd[:], rstd[:]).then_inc(*makes(f"norm_rstd{layer}"))
                dve.wait_ge(*made(i, f"norm_rstd{layer}"))
                for b in range(NB):
                    dve.tensor_scalar(dst[:, b, :], src(b), moments[:, b, 0:1], rstd[:, b:b + 1],
                                           ALU.subtract, ALU.mult).then_inc(*makes(ready))

            def route(i, layer):
                L = str(layer)
                dve.wait_ge(*is_filled(i, "logit" + L))
                dve.tensor_copy(logits[:], bank("logit" + L)[:, 0:NB * NE].rearrange("p (b e) -> p b e", b=NB)).then_inc(*takes("logit" + L))
                dve.wait_ge(*is_taken(i, "logit" + L))
                settle(dve)
                for b in range(NB):
                    ins = dve.max(top[:, b, :], logits[:, b, :])
                ins.then_inc(*makes("top_ready" + L))
                dve.wait_ge(*made(i, "top_ready" + L, 1))
                settle(dve)
                for b in range(NB):
                    ins = dve.max_index(top_at[:, b, :], top[:, b, :], logits[:, b, :])
                ins.then_inc(*makes("top_ready" + L))
                dve.tensor_tensor(top_gap[:], top[:, :, 1], top[:, :, 0], ALU.subtract).then_inc(*makes("gap_ready" + L))
                dve.wait_ge(*made(i, "top_ready" + L, 2))
                dve.tensor_copy(top_atf[:], top_at[:]).then_inc(*makes("top_ready" + L))
                dve.wait_ge(*made(i, "top_exp" + L))
                dve.tensor_scalar(top_sum[:], top_exp[:], 1.0, 1.0 + layer, ALU.add, ALU.mult).then_inc(*makes("top_w_step" + L))
                dve.wait_ge(*made(i, "top_w_step" + L, 1))
                dve.reciprocal(top_w[:, 0, :], top_sum[:]).then_inc(*makes("top_w_step" + L))
                dve.wait_ge(*made(i, "top_w_step" + L, 2))
                dve.tensor_tensor(top_w[:, 1, :], top_w[:, 0, :], top_exp[:], ALU.mult).then_inc(*makes("top_w_step" + L))
                dve.wait_ge(*made(i, "top_ready" + L))
                for j in range(2):
                    ins = dve.tensor_tensor(hot[:, j], expert_no[:].unsqueeze(1).broadcast_to([P, NB, NE]),
                                            top_atf[:, :, j:j + 1].broadcast_to([P, NB, NE]), ALU.is_equal)
                ins.then_inc(*makes("hot_step" + L))
                dve.wait_ge(*made(i, "hot_step" + L, 1))
                dve.wait_ge(*made(i, "top_w_step" + L))
                for j in range(2):
                    ins = dve.tensor_tensor(hot[:, j], hot[:, j], top_w[:, j, :].unsqueeze(2).broadcast_to([P, NB, NE]), ALU.mult)
                ins.then_inc(*makes("hot_step" + L))
                dve.wait_ge(*made(i, "hot_step" + L))
                dve.tensor_tensor(comb[layer][:], hot[:, 0], hot[:, 1], ALU.add).then_inc(*makes("comb_ready" + L))

            def probs_out(i, n):
                if n >= 2:
                    dve.wait_ge(*made(i, "av_done", n - 1))
                dve.wait_ge(*is_filled(i, f"pt{n}"))
                dve.tensor_copy(pT[:, n % 2], bank(f"pt{n}")[:, 0:2 * P].rearrange("p (j t) -> p j t", j=2))
                dve.tensor_copy(pTp[:, n % 2], bank(f"pt{n}")[0:WIN, 2 * P:2 * KEYS].rearrange("p (j t) -> p j t", j=2)).then_inc(*takes(f"pt{n}"))

            def context_out(i):
                dve.wait_ge(*made(i, "av_done"))
                dve.reciprocal(prob_inv[:], prob_sum[:]).then_inc(*makes("prob_inv_ready"))
                dve.wait_ge(*made(i, "prob_inv_ready"))
                dve.tensor_tensor(ctx1[:].rearrange("p b (h d) -> p (b h) d", d=D1),
                                  bank("av")[:].rearrange("p (h d) -> p h d", d=D1),
                                  prob_inv[:].rearrange("p b h -> p (b h)").unsqueeze(2).broadcast_to([P, NB * H1, D1]),
                                  ALU.mult).then_inc(*takes("av"))

            def expert_item(i, kind, n):
                if kind == "hid":
                    dve.wait_ge(*is_taken(i, f"h0_{n}"))
                    dve.wait_ge(*is_filled(i, f"g0_{n}"))
                    dve.tensor_tensor(hid[:, n // PAIR_TILES % 2, n % PAIR_TILES, :], act0[:, n % 2, :], bank(f"g0_{n}")[:],
                                      ALU.mult).then_inc(*takes(f"g0_{n}"))
                    return
                dve.wait_ge(*is_filled(i, f"y0_{n}"))
                if n:
                    dve.wait_ge(*is_taken(i, f"y0_{n - 1}"))
                for b in range(NB):
                    ins = dve.scalar_tensor_tensor(out=acc0[:, b, :], in0=bank(f"y0_{n}")[:, b * P:(b + 1) * P],
                                                   scalar=comb[0][:, b, n:n + 1], in1=(acc0 if n else x_tile)[:, b, :],
                                                   op0=ALU.mult, op1=ALU.add)
                ins.then_inc(*takes(f"y0_{n}"))

            def second(t, L):
                return t.rearrange("p s (g h t) -> p s g h t", h=2, t=L)[:, :, :, 1, :]

            def halves(t, L):
                return t[:].rearrange("p s (g h t) -> p s g h t", h=2, t=L)

            dve.wait_ge(consts, 1)
            dve.wait_ge(weights_in, 16 * (len(loads) + 2))
            with dve.Fori(0, NT) as i:
                dve.wait_ge(*last_tile(i))
                dve.wait_ge(x_in, 16 * i + 16)
                layer_norm(i, 0, lambda b: x_tile[:, b, :], xn, "xn_ready")
                dve.wait_ge(*is_taken(i, "xnT0"))
                dve.tensor_tensor(dx[:], xnT[:, :, 0:P], xnT[:, :, 1:1 + P], ALU.subtract).then_inc(*makes("dx_ready"))
                dve.wait_ge(*made(i, "dx_ready"))
                dve.scalar_tensor_tensor(out=xm[:].rearrange("p (b t) -> p b t", b=NB), in0=dx[:], scalar=vec["x_miu"][:],
                                              in1=xnT[:, :, 1:1 + P], op0=ALU.mult, op1=ALU.add).then_inc(*makes("xm_ready"))
                route(i, 0)
                for g in range(NG):
                    dve.wait_ge(*is_filled(i, f"miu{g}"))
                    dve.scalar_tensor_tensor(out=xd[:, g, :], in0=bank(f"miu{g}")[:], scalar=lam[:, g:g + 1],
                                                   in1=dx[:].rearrange("p b t -> p (b t)"), op0=ALU.add, op1=ALU.mult).then_inc(*takes(f"miu{g}"))
                dve.wait_ge(*is_filled(i, "norm"))
                dve.tensor_scalar(norm[:], bank("norm")[:, 0:NB], 1e-24, None, ALU.max).then_inc(*takes("norm"))
                dve.wait_ge(*is_taken(i, "w"))
                dve.tensor_scalar(decay[:], decay[:], 2.0 ** -115, float(np.exp(-0.5)), ALU.max, ALU.mult).then_inc(*makes("decay_ready"))
                dve.wait_ge(*made(i, "norm_root"))
                dve.reciprocal(norm_inv[:], norm[:]).then_inc(*makes("norm_inv_ready"))
                dve.wait_ge(*made(i, "norm_inv_ready"))
                dve.tensor_tensor(norm_diag, ident[:].unsqueeze(1).broadcast_to([P, NB, P]),
                                  norm_inv[:].unsqueeze(2).broadcast_to([P, NB, P]), ALU.mult).then_inc(*makes("norm_diag_ready"))
                dve.wait_ge(*made(i, "decay_ready"))
                dve.tensor_tensor(ra[:, 0, :], r_raw[:], decay[:], ALU.mult).then_inc(*makes("wkv_in"))
                expert_item(i, *EXPERT_FIRST[0])
                dve.wait_ge(*is_filled(i, "norm_inv"))
                dve.wait_ge(*is_taken(i, "k"))
                dve.tensor_tensor(kn[:], k_raw[:], bank("norm_inv")[:], ALU.mult).then_inc(*takes("norm_inv"))
                dve.wait_ge(*is_taken(i, "norm_inv"))
                dve.wait_ge(*made(i, "root_ready"))
                dve.tensor_tensor(bk[:, 0, :], kn[:], root_decay, ALU.mult).then_inc(*makes("wkv_in"))
                dve.scalar_tensor_tensor(out=bk[:, 1, :], in0=gate_a, scalar=2.0, in1=kn[:], op0=ALU.mult, op1=ALU.mult).then_inc(*makes("wkv_in"))
                dve.tensor_scalar(ra[:, 1, :], kn[:], -1.0, None, ALU.mult).then_inc(*makes("wkv_in"))
                dve.scalar_tensor_tensor(out=rkx[:], in0=r_raw[:], scalar=vec["x_time"][:], in1=kn[:],
                                              op0=ALU.mult, op1=ALU.mult).then_inc(*makes("rkx_ready"))

                for item in EXPERT_FIRST[1:]:
                    expert_item(i, *item)

                def keep_level(m, L, w):
                    name = f"lev{L}_{w}"
                    dve.wait_ge(*is_filled(i, name))
                    if L:
                        dve.wait_ge(*is_taken(i, f"lev{L // 2}_{w}"))
                    if L == 0:
                        dst = A[:, 2 * w:2 * w + 2].rearrange("p u (s q) t -> p (u s) q t", s=2)[:, :, 0, :]
                        mask = ident[:].bitcast(I32).unsqueeze(1).broadcast_to([P, 4, P])
                        src = bank(name)[:].rearrange("p (s t) -> p s t", s=4)
                    else:
                        dst = second(A[:, 2 * w:2 * w + 2].rearrange("p u s t -> p (u s) t"), L)
                        mask = level_mask[:, m, :].bitcast(I32).rearrange("p (g h t) -> p g h t", h=2, t=L)[:, :, 1, :]
                        mask = mask.unsqueeze(1).broadcast_to([P, 8, P // (2 * L), L])
                        src = bank(name)[:].rearrange("p (s g t) -> p s g t", s=8, t=L)
                    settle(dve)
                    dve.copy_predicated(dst, mask, src).then_inc(*takes(name))

                def grow(m, L):
                    G = TOK // (2 * L)
                    d = decay[:] if L == 1 else block_decay[L][:]
                    dv = d.rearrange("p (g h) -> p g h", h=2)
                    if L > 1:
                        dve.wait_ge(*made(i, "block_decay_ready", m))
                        dve.wait_ge(*made(i, "blocks_grown", 2 * m))
                    v = halves(ra, L)[:, :, :, 1, :]
                    dve.tensor_tensor(v, v, dv[:, :, 0:1].unsqueeze(1).broadcast_to([P, 2, G, L]), ALU.mult).then_inc(*makes("blocks_grown"))
                    v = halves(bk, L)[:, :, :, 0, :]
                    dve.tensor_tensor(v, v, dv[:, :, 1:2].unsqueeze(1).broadcast_to([P, 2, G, L]), ALU.mult).then_inc(*makes("blocks_grown"))
                    dve.tensor_tensor(block_decay[2 * L][:], dv[:, :, 0], dv[:, :, 1], ALU.mult).then_inc(*makes("block_decay_ready"))

                for s in range(len(EXPERT_SLOTS)):
                    m = s // 2 - 1
                    L = LEVELS[m] if m >= 0 else 0
                    if s % 2 and L:
                        dve.wait_ge(*is_filled(i, f"lev{L}_3"))
                        grow(m, L)
                    for w in (2 * s % 4, 2 * s % 4 + 1):
                        keep_level(m, L, w)
                    for item in EXPERT_SLOTS[s - 1] if s else []:
                        expert_item(i, *item)
                for w in range(4):
                    dve.wait_ge(*is_taken(i, f"lev{LEVELS[-1]}_{w}"))
                dve.tensor_tensor(invT[:], A[:, :, 3, :], level_mask[:, 0, :].unsqueeze(1).broadcast_to([P, NU, P]), ALU.mult).then_inc(*makes("inv_base"))
                dve.wait_ge(*made(i, "inv_base"))
                dve.tensor_tensor(invT[:], invT[:], ident[:].unsqueeze(1).broadcast_to([P, NU, P]), ALU.add).then_inc(*makes("inv_start"))
                for item in EXPERT_SLOTS[-1]:
                    expert_item(i, *item)
                for n in LEVELS[1:]:
                    for q in range(2):
                        dve.wait_ge(*is_filled(i, f"inv{n}D{q}"))
                        v = second(invT[:, 4 * q:4 * q + 4, :], n)
                        d = bank(f"inv{n}D{q}")[:, 0:2 * P].rearrange("p (u g t) -> p u g t", u=4, t=n)
                        dve.tensor_tensor(v, v, d, ALU.add).then_inc(*takes(f"inv{n}D{q}"))
                D = block_decay[2 * LEVELS[-1]]
                dve.wait_ge(*made(i, "block_decay_ready"))
                dve.tensor_tensor(state_dec[:], state[:], D[:].unsqueeze(2).broadcast_to([P, NB, HS]), ALU.mult).then_inc(*makes("state_step"))
                dve.wait_ge(*made(i, "state_step", 1))
                dve.wait_ge(*is_filled(i, "S"))
                dve.tensor_tensor(state[:], state_dec[:], bank("S")[:, 0:NB * HS].rearrange("p (b d) -> p b d", b=NB), ALU.add).then_inc(*takes("S"))
                dve.wait_ge(*is_taken(i, "Y0"))
                dve.wait_ge(*is_taken(i, "Y1"))
                for u in range(NU):
                    dve.bn_stats(gn_stats[:, u, :], y[:, u, :]).then_inc(*makes("gn_stats_ready"))
                for u in range(NU):
                    dve.wait_ge(*made(i, "gn_stats_ready", u + 1))
                    settle(dve)
                    dve.bn_aggr(gn_mom[:, u, :], gn_stats[:, u, :]).then_inc(*makes("gn_mom_ready"))
                dve.wait_ge(*made(i, "gn_mom_ready"))
                dve.tensor_scalar(gn_rstd[:], gn_mom[:, :, 1], GN_EPS, None, ALU.add).then_inc(*makes("gn_var"))
                dve.wait_ge(*made(i, "gn_root"))
                dve.reciprocal(gn_rstd[:], gn_rstd[:]).then_inc(*makes("y_step"))
                dve.tensor_tensor(y_mul[:], y[:], gn_mom[:, :, 0:1].broadcast_to([P, NU, HS]), ALU.subtract).then_inc(*makes("y_step"))
                dve.wait_ge(*made(i, "y_step", 2))
                dve.tensor_tensor(y_mul[:], y_mul[:], gn_rstd[:].unsqueeze(2).broadcast_to([P, NU, HS]), ALU.mult).then_inc(*makes("y_step"))
                dve.wait_ge(*made(i, "y_step", 3))
                ym = y_mul[:].rearrange("p (b h) d -> p b (h d)", h=NH)
                dve.tensor_tensor(ym, ym, gamma[:].unsqueeze(1).broadcast_to([P, NB, P]), ALU.mult).then_inc(*makes("y_step"))
                dve.wait_ge(*made(i, "y_step", 4))
                dve.tensor_tensor(ym, ym, beta[:].unsqueeze(1).broadcast_to([P, NB, P]), ALU.add).then_inc(*makes("z_step"))
                dve.wait_ge(*made(i, "z_step", 1))
                dve.wait_ge(*made(i, "bonus_v_ready"))
                dve.tensor_tensor(y_mul[:], y_mul[:], bonus_v, ALU.add).then_inc(*makes("z_step"))
                dve.wait_ge(*made(i, "z_step", 2))
                dve.wait_ge(*is_taken(i, "g"))
                dve.tensor_tensor(ym, ym, g_tok[:], ALU.mult).then_inc(*makes("z_ready"))
                for e in EXPERT_LAST:
                    expert_item(i, "out", e)
                dve.wait_ge(*is_filled(i, "o0"))
                dve.wait_ge(*is_taken(i, f"y0_{NE - 1}"))
                dve.tensor_tensor(acc0[:], acc0[:],
                                  bank("o0")[:].rearrange("p (b d) -> p b d", b=NB), ALU.add).then_inc(*takes("o0"))
                dve.wait_ge(*is_taken(i, "o0"))
                layer_norm(i, 1, lambda b: acc0[:, b, :], x1n, "x1n_ready")
                route(i, 1)
                for n in range(STEPS1 + 1):
                    if 2 <= n < NPAIRS + 2:
                        probs_out(i, n - 2)
                    if n < NPAIRS:
                        dve.wait_ge(*is_filled(i, f"sc{n}"))
                        if n >= 3:
                            dve.wait_ge(*is_taken(i, f"sc{n - 3}"))
                        dve.tensor_reduce(neg_max[:, n % 3, :], bank(f"sc{n}")[:, 0:2 * KEYS].rearrange("p (j s) -> p j s", j=2),
                                          AX.X, ALU.max, negate=True).then_inc(*makes("neg_max_ready"))
                    if n == NPAIRS + 2:
                        context_out(i)
                    if 1 <= n <= NF * K1:
                        k = n - 1
                        dve.wait_ge(*made(i, "tanh_done", n))
                        dve.scalar_tensor_tensor(out=hid[:, k // K1 % 2, k % K1, :], in0=act0[:, k % 2, :], scalar=1.0,
                                                 in1=bank(f"h1_{k}")[:], op0=ALU.add, op1=ALU.mult).then_inc(*takes(f"h1_{k}"))
                    if n >= K1 + 2 and (n - 2) % K1 == 0:
                        e = (n - 2) // K1 - 1
                        dve.wait_ge(*is_filled(i, f"y1_{e}"))
                        if e == 0:
                            dve.scalar_tensor_tensor(out=acc1[:], in0=bank("y1_0")[:].rearrange("p (b d) -> p b d", b=NB), scalar=0.5,
                                                     in1=acc0[:], op0=ALU.mult, op1=ALU.add).then_inc(*takes("y1_0"))
                            continue
                        dve.wait_ge(*is_taken(i, f"y1_{e - 1}"))
                        for b in range(NB):
                            ins = dve.scalar_tensor_tensor(out=acc1[:, b, :], in0=bank(f"y1_{e}")[:, b * P:(b + 1) * P],
                                                           scalar=comb[1][:, b, e - 1:e], in1=acc1[:, b, :],
                                                           op0=ALU.mult, op1=ALU.add)
                        ins.then_inc(*takes(f"y1_{e}"))
                dve.wait_ge(*is_filled(i, "o1"))
                dve.wait_ge(*is_taken(i, f"y1_{NF - 1}"))
                dve.wait_ge(out_done, 16 * i + 16)
                dve.tensor_tensor(out_tile[:], acc1[:], bank("o1")[:].rearrange("p (b d) -> p b d", b=NB), ALU.add).then_inc(*takes("o1"))

        @block.tensor
        def _(pe):
            def mm(dst, lhsT, rhs, start=True, stop=True, onto=False):
                return pe.matmul(dst, lhsT, rhs, start=start, stop=stop, skip_group_check=onto)

            def cols(b, n=P):
                return slice(b * n, (b + 1) * n)

            def rows(h):
                return slice(h * HS, (h + 1) * HS)

            pe.wait_ge(consts, 1)
            pe.wait_ge(weights_in, 16 * (len(loads) + 2))
            with pe.Fori(0, NT) as i:
                pe.wait_ge(*is_free(i, "xnT0"))
                for b in range(NB):
                    pe.wait_ge(*made(i, "xn_ready", b + 1))
                    ins = pe.transpose(bank("xnT0")[:, cols(b)], xn[:, b, :], ident[:])
                ins.then_inc(*fills("xnT0"))
                pe.wait_ge(*is_taken(i, "xnT0"))
                pe.wait_ge(*is_free(i, "logit0"))
                for b in range(NB):
                    ins = mm(bank("logit0")[:, cols(b, NE)], xnT[:, b, 1:1 + P], Wr[:])
                ins.then_inc(*fills("logit0"))
                pe.wait_ge(*made(i, "xm_ready"))
                pe.wait_ge(*is_free(i, "mixA"))
                mm(bank("mixA")[:], xA[:, 0:P], xm[:]).then_inc(*fills("mixA"))
                pe.wait_ge(*is_free(i, "mixB"))
                mm(bank("mixB")[0:2 * MIXK, :], xA[:, P:NG * MIXK], xm[:]).then_inc(*fills("mixB"))
                for g in range(NG):
                    pe.wait_ge(*is_taken(i, "mixA" if g < 4 else "mixB"))
                    pe.wait_ge(*is_free(i, f"miu{g}"))
                    w, m, at = (xB_lo, mixA, g) if g < 4 else (xB_hi, mixB, g - 4)
                    r = slice(MIXK * at, MIXK * (at + 1))
                    mm(bank(f"miu{g}")[:], w[r, :], m[r, :]).then_inc(*fills(f"miu{g}"))
                at = {g: n for n, g in enumerate("rwkvag")}
                for g in "wkag":
                    pe.wait_ge(*made(i, "xd_ready", at[g] + 1))
                    pe.wait_ge(*is_free(i, f"low_{g}"))
                    mm(bank(f"low_{g}")[0:low[g].shape[0], :], lowA[g][:], xd[:, at[g], :]).then_inc(*fills(f"low_{g}"))
                pe.wait_ge(*is_free(i, "r"))
                mm(bank("r")[:], proj["r"][:], xd[:, at["r"], :]).then_inc(*fills("r"))
                pe.wait_ge(*is_taken(i, "low_w"))
                pe.wait_ge(*is_free(i, "w"))
                mm(bank("w")[:], lowB["w"][:], low["w"][:]).then_inc(*fills("w"))
                pe.wait_ge(*is_free(i, "k"))
                mm(bank("k")[:], proj["k"][:], xd[:, at["k"], :], stop=False)
                pe.wait_ge(*is_taken(i, "low_k"))
                mm(bank("k")[:], lowB["k"][:], low["k"][:], start=False).then_inc(*fills("k"))
                pe.wait_ge(*is_taken(i, "low_a"))
                pe.wait_ge(*is_free(i, "a"))
                mm(bank("a")[:], lowB["a"][:], low["a"][:]).then_inc(*fills("a"))
                pe.wait_ge(*is_free(i, "v"))
                for b in range(NB):
                    ins = mm(bank("v")[:, cols(b)], xd[:, at["v"], cols(b)], proj["v"][:])
                ins.then_inc(*fills("v"))
                pe.wait_ge(*is_taken(i, "low_g"))
                pe.wait_ge(*is_free(i, "g"))
                for b in range(NB):
                    ins = mm(bank("g")[:, cols(b)], low["g"][:, cols(b)], lowB["g"][:])
                ins.then_inc(*fills("g"))
                def expert_item(kind, n):
                    if kind == "hid":
                        for name, w in ((f"h0_{n}", W1), (f"g0_{n}", W3)):
                            pe.wait_ge(*is_free(i, name))
                            mm(bank(name)[:], w[:, cols(n)], xnT[:, :, 1:1 + P]).then_inc(*fills(name))
                        return
                    j, first = n // 2, PAIR_TILES * (n // 2)
                    parts = [(0, 0, P), (1, 0, P // 2)] if n % 2 == 0 else [(1, P // 2, P), (2, 0, P)]
                    last_hid = f"g0_{first + parts[1][0]}"
                    if bank_of[last_hid] != bank_of[f"y0_{n}"]:
                        pe.wait_ge(*is_taken(i, last_hid))
                    pe.wait_ge(*is_free(i, f"y0_{n}"))
                    for b in range(NB):
                        for t, (k, lo, hi) in enumerate(parts):
                            ins = mm(bank(f"y0_{n}")[:, cols(b)], hid[lo:hi, j % 2, k, cols(b)],
                                     W2[lo:hi, first + k, :], start=t == 0, stop=t == 1)
                    ins.then_inc(*fills(f"y0_{n}"))

                pe.wait_ge(*is_taken(i, "k"))
                pe.wait_ge(*is_free(i, "norm"))
                for b in range(NB):
                    ins = mm(bank("norm")[:, b:b + 1], k_sq[:, cols(b)], ones[:, 0:1])
                ins.then_inc(*fills("norm"))
                expert_item(*EXPERT_FIRST[0])
                pe.wait_ge(*is_taken(i, "r"))
                pe.wait_ge(*made(i, "norm_diag_ready"))
                pe.wait_ge(*is_free(i, "norm_inv"))
                mm(bank("norm_inv")[:], ones[:], norm_diag).then_inc(*fills("norm_inv"))
                for item in EXPERT_FIRST[1:]:
                    expert_item(*item)
                pe.wait_ge(*made(i, "wkv_in"))
                for s, items in enumerate(EXPERT_SLOTS):
                    m = s // 2 - 1
                    L = LEVELS[m] if m >= 0 else 0
                    if L > 1 and s % 2 == 0:
                        pe.wait_ge(*made(i, "blocks_grown", 2 * m))
                    for w in (2 * s % 4, 2 * s % 4 + 1):
                        name = f"lev{L}_{w}"
                        pe.wait_ge(*is_free(i, name))
                        for n in range(4):
                            u, q = 2 * w + n // 2, n % 2
                            h, b = u // NB, u % NB
                            target = r_raw[rows(h), cols(b)]
                            if L:
                                target = ra[rows(h), :, cols(b)].rearrange("p s (g h t) -> p s g h t", h=2, t=L)[:, :, :, 1, :]
                            ins = mm(bank(name)[:, cols(n)], bk[rows(h), q, cols(b)], target)
                        ins.then_inc(*fills(name))
                    for item in items:
                        expert_item(*item)
                for n, L in enumerate(LEVELS[1:]):
                    for q in range(2):
                        name = f"inv{L}T{q}"
                        if n == 0:
                            pe.wait_ge(*made(i, "inv_start"))
                        else:
                            pe.wait_ge(*is_taken(i, f"inv{LEVELS[n]}D{q}"))
                        pe.wait_ge(*is_free(i, name))
                        for u in range(4):
                            ins = pe.transpose(bank(name)[:, cols(u)], invT[:, 4 * q + u, :], ident[:])
                        ins.then_inc(*fills(name))
                    pe.wait_ge(*made(i, "A_level_ready", n + 1))
                    for q in range(2):
                        name = f"inv{L}Z{q}"
                        pe.wait_ge(*is_taken(i, f"inv{L}T{q}"))
                        pe.wait_ge(*is_free(i, name))
                        for u in range(4):
                            ins = mm(bank(name)[:, cols(u)], A_level[:, 4 * q + u, :], inv[:, 4 * q + u, :])
                        ins.then_inc(*fills(name))
                    for q in range(2):
                        name = f"inv{L}D{q}"
                        pe.wait_ge(*is_taken(i, f"inv{L}Z{q}"))
                        pe.wait_ge(*is_free(i, name))
                        for u in range(4):
                            ins = mm(bank(name)[:, cols(u, P // 2)], AZ[:, 4 * q + u, :],
                                     invT[:, 4 * q + u, :].rearrange("p (g h t) -> p g h t", h=2, t=L)[:, :, 1, :])
                        ins.then_inc(*fills(name))
                pe.wait_ge(*made(i, "blocks_grown"))
                for name, s in (("btok", 1), ("ktok", 0)):
                    pe.wait_ge(*is_free(i, name))
                    for b in range(NB):
                        ins = pe.transpose(bank(name)[:, cols(b)], bk[:, s, cols(b)], ident[:])
                    ins.then_inc(*fills(name))
                pe.wait_ge(*made(i, "rkx_ready"))
                pe.wait_ge(*is_free(i, "bonus"))
                for b in range(NB):
                    ins = mm(bank("bonus")[:, cols(b, NH)], rkx[:, cols(b)], head_ones[:])
                ins.then_inc(*fills("bonus"))
                pe.wait_ge(*is_taken(i, "v"))
                for h in range(NH):
                    pe.wait_ge(*is_free(i, f"X{h}"))
                    for b in range(NB):
                        mm(bank(f"X{h}")[:, cols(b, HS)], ra[rows(h), 1, cols(b)], state[rows(h), b, :], stop=False)
                        ins = mm(bank(f"X{h}")[:, cols(b, HS)], A[:, NB * h + b, 1, :], v_tok[:, b, rows(h)], start=False)
                    ins.then_inc(*fills(f"X{h}"))
                pe.wait_ge(*is_taken(i, "X0"))
                pe.wait_ge(*is_taken(i, "X1"))
                pe.wait_ge(*is_taken(i, f"inv{LEVELS[-1]}D1"))
                pe.wait_ge(*is_free(i, "U"))
                for u in range(NU):
                    ins = mm(bank("U")[:, cols(u, HS)], invT[:, u, :], X[:, u, :])
                ins.then_inc(*fills("U"))
                pe.wait_ge(*is_taken(i, "U"))
                for h in range(NH):
                    pe.wait_ge(*is_free(i, f"Y{h}"))
                    for b in range(NB):
                        u = NB * h + b
                        mm(bank(f"Y{h}")[:, cols(b, HS)], ra[rows(h), 0, cols(b)], state[rows(h), b, :], stop=False)
                        mm(bank(f"Y{h}")[:, cols(b, HS)], A[:, u, 2, :], U[:, u, :], start=False, stop=False)
                        ins = mm(bank(f"Y{h}")[:, cols(b, HS)], A[:, u, 0, :], v_tok[:, b, rows(h)], start=False)
                    ins.then_inc(*fills(f"Y{h}"))
                pe.wait_ge(*is_taken(i, "btok"))
                pe.wait_ge(*is_taken(i, "ktok"))
                pe.wait_ge(*is_free(i, "S"))
                for u in range(NU):
                    h, b = u // NB, u % NB
                    mm(bank("S")[rows(h), cols(b, HS)], b_tok[:, b, rows(h)], U[:, u, :], stop=False)
                    ins = mm(bank("S")[rows(h), cols(b, HS)], k_tok[:, b, rows(h)], v_tok[:, b, rows(h)], start=False)
                ins.then_inc(*fills("S"))
                for e in EXPERT_LAST:
                    expert_item("out", e)
                pe.wait_ge(*made(i, "z_ready"))
                pe.wait_ge(*is_free(i, "zT"))
                for b in range(NB):
                    ins = pe.transpose(bank("zT")[:, cols(b)], y_mul[:, NH * b:NH * (b + 1), :].rearrange("p h d -> p (h d)"), ident[:])
                ins.then_inc(*fills("zT"))
                pe.wait_ge(*is_taken(i, "zT"))
                pe.wait_ge(*is_free(i, "o0"))
                for b in range(NB):
                    ins = mm(bank("o0")[:, cols(b)], zT[:, cols(b)], proj["o"][:])
                ins.then_inc(*fills("o0"))
                pe.wait_ge(*is_free(i, "xnT1"))
                for b in range(NB):
                    pe.wait_ge(*made(i, "x1n_ready", b + 1))
                    ins = pe.transpose(bank("xnT1")[:, cols(b)], x1n[:, b, :], ident[:])
                ins.then_inc(*fills("xnT1"))
                pe.wait_ge(*is_taken(i, "xnT1"))
                pe.wait_ge(*is_free(i, "logit1"))
                for b in range(NB):
                    ins = mm(bank("logit1")[:, cols(b, NE)], x1nT[:, b, WIN:KEYS], gateW[:])
                ins.then_inc(*fills("logit1"))
                for g in "qk":
                    pe.wait_ge(*is_free(i, g + "1"))
                    mm(bank(g + "1")[:], attnW[g][:], x1nT[:, :, WIN:KEYS]).then_inc(*fills(g + "1"))
                pe.wait_ge(*is_free(i, "v1"))
                for b in range(NB):
                    ins = mm(bank("v1")[:, cols(b)], x1nT[:, b, WIN:KEYS], attnW["v"][:])
                ins.then_inc(*fills("v1"))
                pe.wait_ge(*is_free(i, "v1p"))
                for b in range(NB):
                    ins = mm(bank("v1p")[0:WIN, cols(b)], x1nT[:, b, 0:WIN], attnW["v"][:])
                ins.then_inc(*fills("v1p"))

                def scores(n):
                    b, p = n // NPAIR, n % NPAIR
                    if n == 0:
                        pe.wait_ge(*is_taken(i, "k1"))
                        pe.wait_ge(*is_taken(i, "q1"))
                    pe.wait_ge(*is_free(i, f"sc{n}"))
                    mm(bank(f"sc{n}")[:, 0:2 * KEYS], ident16[:], key_mask_now[:].rearrange("p j s -> p (j s)"))
                    for j in range(2):
                        h = 2 * p + j
                        r = slice(32 * (h // HPG), 32 * (h // HPG + 1))
                        ins = mm(bank(f"sc{n}")[:, cols(j, KEYS)], q1[r, h % HPG, cols(b)], kT1[r, b, :], start=False, onto=True)
                    ins.then_inc(*fills(f"sc{n}"))

                def turn(n):
                    pe.wait_ge(*is_taken(i, f"sc{n}"))
                    pe.wait_ge(*is_free(i, f"pt{n}"))
                    for j in range(2):
                        pe.transpose(bank(f"pt{n}")[:, cols(j)], prob[:, n % 3, j, WIN:KEYS], ident[:])
                    for j in range(2):
                        ins = pe.transpose(bank(f"pt{n}")[0:WIN, 2 * P + WIN * j:2 * P + WIN * (j + 1)],
                                           prob[0:WIN, n % 3, j, 0:WIN], ident[0:WIN, 0:WIN])
                    ins.then_inc(*fills(f"pt{n}"))

                def weigh(n):
                    b, p = n // NPAIR, n % NPAIR
                    if n == 0:
                        pe.wait_ge(*is_taken(i, "v1p"))
                        pe.wait_ge(*is_free(i, "av"))
                    pe.wait_ge(*is_taken(i, f"pt{n}"))
                    for j in range(2):
                        h = 2 * p + j
                        mm(bank("av")[:, cols(H1 * b + h, D1)], pT[:, n % 2, j, :], v1[:, b, cols(h, D1)])
                        ins = mm(bank("av")[0:WIN, cols(H1 * b + h, D1)], pTp[:, n % 2, j, :], v1p[:, b, cols(h, D1)],
                                 start=False, onto=True)
                    ins.then_inc(*makes("av_done"))

                for n in range(STEPS1):
                    if n < NPAIRS:
                        scores(n)
                    if n < NF * K1:
                        pe.wait_ge(*is_free(i, f"h1_{n}"))
                        mm(bank(f"h1_{n}")[:], F1[:, cols(n)], x1nT[:, :, WIN:KEYS]).then_inc(*fills(f"h1_{n}"))
                    if 1 <= n <= NPAIRS:
                        turn(n - 1)
                    if 2 <= n < NPAIRS + 2:
                        weigh(n - 2)
                    if n >= K1 + 1 and (n - 1) % K1 == 0:
                        e = (n - 1) // K1 - 1
                        pe.wait_ge(*is_taken(i, f"h1_{K1 * e + K1 - 1}"))
                        pe.wait_ge(*is_free(i, f"y1_{e}"))
                        for b in range(NB):
                            for k in range(K1):
                                ins = mm(bank(f"y1_{e}")[:, cols(b)], hid[:, e % 2, k, cols(b)], F2[:, K1 * e + k, :],
                                         start=k == 0, stop=k == K1 - 1)
                        ins.then_inc(*fills(f"y1_{e}"))
                    if n == NPAIRS + 2:
                        pe.wait_ge(*is_taken(i, "av"))
                        pe.wait_ge(*is_free(i, "cT"))
                        for b in range(NB):
                            ins = pe.transpose(bank("cT")[:, cols(b)], ctx1[:, b, :], ident[:])
                        ins.then_inc(*fills("cT"))
                    if n == NPAIRS + 3:
                        pe.wait_ge(*is_taken(i, "cT"))
                        pe.wait_ge(*is_free(i, "o1"))
                        for b in range(NB):
                            ins = mm(bank("o1")[:, cols(b)], cT[:, cols(b)], attnW["o"][:])
                        ins.then_inc(*fills("o1"))

        for name, (_, n) in per_tile.items():
            assert counted.get(name) == n, (name, counted.get(name), n)


def kernel(**inputs):
    import concourse.bacc as _bacc
    from concourse.bass_utils import run_bass_kernel_spmd as _run

    a = {n.removeprefix("L0_attn_"): np.asarray(v) for n, v in inputs.items()}
    f1 = np.concatenate([a["L1_ffn_shared_w1"][None], a["L1_ffn_experts_w1"]])
    f2 = np.concatenate([a["L1_ffn_shared_w2"][None], a["L1_ffn_experts_w2"]])
    laid = {
        "x": a["x"], "x_A": a["x_A"], "x_B_lo": a["x_B"][0:4].reshape(P, P), "x_B_hi": a["x_B"][4:6].reshape(2 * MIXK, P),
        "lambdas": a["lambdas"].reshape(NG, P).T, "gn_gamma": a["gn_gamma"], "gn_beta": a["gn_beta"],
        **{n: a[n].reshape(P, 1) for n in VECS},
        **{f"{g}_{s}": a[f"{g}_{s}"] for g in "wkag" for s in "AB"},
        **{f"{g}W_T": a[f"{g}W"].T for g in "rkvo"},
        "Wr": a["L0_ffn_Wr"],
        "W1": a["L0_ffn_W1"].transpose(1, 0, 2).reshape(P, NE * HID0),
        "W3": a["L0_ffn_W3"].transpose(1, 0, 2).reshape(P, NE * HID0),
        "W2": a["L0_ffn_W2"].reshape(K0, P, P).transpose(1, 0, 2),
        **{f"W{g}": a[f"L1_attn_W{g}"] for g in "qkvo"},
        "gateW": a["L1_ffn_gate_w"].T,
        "F1": f1.transpose(2, 0, 1).reshape(P, NF * K1 * P),
        "F2": f2.reshape(NF, P, K1, P).transpose(3, 0, 2, 1).reshape(P, NF * K1, P),
    }
    nc = _bacc.Bacc("TRN2", target_bir_lowering=False, num_devices=1)
    arrays, io = {}, {}
    for name, v in laid.items():
        arrays[f"in_{name}"] = np.ascontiguousarray(v)
        io[name] = nc.dram_tensor(f"in_{name}", v.shape, mybir.dt.from_np(v.dtype), kind="ExternalInput").ap()
    out = nc.dram_tensor("out", a["x"].shape, F32, kind="ExternalOutput").ap()
    build(nc, io, out)
    r = _run(nc, [arrays], core_ids=[0])
    return r.results[0]["out"]
```

```python
from contextlib import ExitStack

import numpy as np

import concourse.bass as bass
from concourse import mybir

ALU = mybir.AluOpType
ACT = mybir.ActivationFunctionType
AX = mybir.AxisListType
F32 = mybir.dt.float32
BF16 = mybir.dt.bfloat16
I32 = mybir.dt.int32
U32 = mybir.dt.uint32

P = 128
NB = 4
TOK = NB * P
LN_EPS = 1e-5

NG = 6
MIXK = 32
LORA = 64
NH = 2
HS = P // NH
NU = NB * NH
GN_EPS = 1e-5 * NH
LEVELS = [1, 2, 4, 8, 16, 32, 64]

NE = 8
HID0 = 192
K0 = NE * HID0 // P
PAIR_TILES = 2 * HID0 // P

H1 = 16
D1 = P // H1
WIN = 64
KEYS = WIN + P
HPG = 32 // D1
NPAIR = H1 // 2
MASKED = -1.0e30

NF = NE + 1
K1 = 4

MIU_HID = {0: 0, 2: 1, 4: 2}
EXPERT_FIRST = [("hid", 3), ("hid", 4), ("hid", 5)]
SLOTS = [[("out", 0)], [("out", 1)], [("out", 2)], [("out", 3)], [("hid", 6)], [("T", 2), ("hid", 7)], [("Z", 2)], [("D", 2)],
         [("T", 4), ("hid", 8)], [("Z", 4)], [("D", 4)], [("T", 8), ("hid", 9)], [("Z", 8)], [("D", 8)],
         [("T", 16), ("hid", 10)], [("Z", 16)]]
SLOTS_LAST = [("D", 16), ("T", 32), ("Z", 32), ("out", 4), ("D", 32), ("T", 64), ("Z", 64), ("D", 64)]
AFTER = {"X0": [("hid", 11)], "U": [("out", 5)], "S": [("out", 6), ("out", 7)]}

NPAIRS = NB * NPAIR
STEPS1 = NF * K1 + 2
FRONT_STEPS = {11: "xnT0", 15: "logit0", 19: "mixA", 23: "mixB"}

VECS = ["w_miu", "a_time", "x_miu", "x_time"]


def psum_plan():
    plan, turn = [], [2]

    def use(name, bank=None):
        if bank is None:
            bank = turn[0] % 8
            turn[0] += 1
        plan.append((name, bank))

    for g in range(NG):
        use(f"h0_{MIU_HID[g]}" if g in MIU_HID else f"g0_{MIU_HID[g - 1]}")
        use(f"miu{g}")
    for n in ["low_w", "low_k", "low_a", "low_g", "r", "w", "k", "a", "v", "g"]:
        use(n)

    def expert_item(kind, n):
        names = {"hid": (f"h0_{n}", f"g0_{n}"), "out": (f"y0_{n}",)}
        for name in names.get(kind, (f"inv{n}{kind}0", f"inv{n}{kind}1")):
            use(name)

    use("norm")
    expert_item(*EXPERT_FIRST[0])
    use("norm_inv")
    for item in EXPERT_FIRST[1:]:
        expert_item(*item)
    for s, items in enumerate(SLOTS):
        for w in (2 * s % 4, 2 * s % 4 + 1):
            use(f"lev{([0] + LEVELS)[s // 2]}_{w}")
        for item in items:
            expert_item(*item)
    for item in SLOTS_LAST:
        expert_item(*item)
    for n in ["btok", "ktok", "bonus", "X0", "h0_11", "g0_11", "X1", "U", "y0_5", "Y0", "Y1", "S", "y0_6", "y0_7", "zT", "o0"]:
        use(n)
    for n in ["xnT1", "logit1", "q1", "k1", "v1", "v1p"]:
        use(n)
    for n in range(STEPS1):
        if n < NPAIRS:
            use(f"sc{n}", n % 2)
        if n < NF * K1:
            use(f"h1_{n}", 5 + n % 2)
        if 1 <= n <= NPAIRS:
            use(f"pt{n - 1}", 2 + (n - 1) % 2)
        if n == 2:
            use("av", 4)
        if n >= K1 + 1 and (n - 1) % K1 == 0:
            use(f"y1_{(n - 1) // K1 - 1}", 7)
        if n in FRONT_STEPS:
            use(FRONT_STEPS[n], 7)
        if n == NPAIRS + 2:
            use("cT", 0)
        if n == NPAIRS + 3:
            use("o1", 1)
    return plan


def build(nc, io, out):
    x_dram = io["x"]
    T = x_dram.shape[1]
    NT = T // P
    plan = psum_plan()
    bank_of, turn_of, turns, turns_before, front_turn = {}, {}, [0] * 8, [0] * 8, {}
    fill_of, fills_of = {}, [0] * 8
    for name, b in plan:
        bank_of[name], turn_of[name], fill_of[name] = b, turns[b], fills_of[b]
        turns[b] += 1
        fills_of[b] += name != "av"
    for name in FRONT_STEPS.values():
        front_turn[name] = turns_before[bank_of[name]]
        turns_before[bank_of[name]] += 1

    with ExitStack() as ctx:
        def sb(name, shape, dt=F32):
            return ctx.enter_context(nc.sbuf_tensor(name, shape, dt))

        def sem(name):
            return ctx.enter_context(nc.semaphore(name))

        banks = [ctx.enter_context(nc.psum_tensor(f"bank{b}", [P, 512], F32)) for b in range(8)]
        bank_filled = [sem(f"bank_filled{b}") for b in range(8)]
        bank_taken = [sem(f"bank_taken{b}") for b in range(8)]

        def bank(name):
            return banks[bank_of[name]]

        def turns_until(i, name):
            b = bank_of[name]
            return front_turn[name] if i is None else i * turns[b] + turn_of[name] + turns_before[b]

        def is_free(i, name):
            return bank_taken[bank_of[name]], turns_until(i, name) + 1

        def is_filled(i, name):
            b = bank_of[name]
            before = front_turn[name] if i is None else i * fills_of[b] + fill_of[name] + turns_before[b]
            return bank_filled[b], before + 1

        def is_taken(i, name):
            return bank_taken[bank_of[name]], turns_until(i, name) + 2

        def fills(name):
            return bank_filled[bank_of[name]], 1

        def takes(name):
            return bank_taken[bank_of[name]], 1

        x_tile = sb("x_tile", [P, NB, P])
        xA = sb("xA", [P, NG * MIXK])
        xB_lo = sb("xB_lo", [P, P])
        xB_hi = sb("xB_hi", [2 * MIXK, P])
        lowA = {g: sb(f"{g}_A", [P, n]) for g, n in (("w", LORA), ("k", LORA), ("a", LORA), ("g", P))}
        lowB = {g: sb(f"{g}_B", [n, P]) for g, n in (("w", LORA), ("k", LORA), ("a", LORA), ("g", P))}
        proj = {g: sb(f"{g}W_T", [P, P]) for g in "rkvo"}
        lam = sb("lam", [P, NG])
        vec = {n: sb(n, [P, 1]) for n in VECS}
        gamma = sb("gamma", [P, P])
        beta = sb("beta", [P, P])
        Wr = sb("Wr", [P, NE])
        W1 = sb("W1", [P, NE * HID0])
        W3 = sb("W3", [P, NE * HID0])
        W2 = sb("W2", [P, K0, P])
        attnW = {g: sb(f"W{g}", [P, P]) for g in "qkvo"}
        gateW = sb("gateW", [P, NE])
        F1 = sb("F1", [P, NF * K1 * P])
        F2 = sb("F2", [P, NF * K1, P])

        ident = sb("ident", [P, P])
        ident16 = sb("ident16", [P, P], BF16)
        ones = sb("ones", [P, P])
        head_ones = sb("head_ones", [P, NH])
        group_head = sb("group_head", [P, HPG])
        level_mask = sb("level_mask", [P, len(LEVELS), P])
        expert_no = sb("expert_no", [P, NE])
        key_mask = sb("key_mask", [P, 2, KEYS], BF16)
        key_mask_now = sb("key_mask_now", [P, 2, KEYS], BF16)

        xnT = sb("xnT", [P, NB, 1 + P])
        state = sb("state", [P, NB, HS])
        x1nT = sb("x1nT", [P, NB, KEYS])
        kT1 = sb("kT1", [P, NB, KEYS])

        stats = sb("stats", [P, NB, 6])
        moments = sb("moments", [P, NB, 2])
        rstd = sb("rstd", [P, NB])
        dx = sb("dx", [P, NB, P])
        mixA = sb("mixA", [P, TOK])
        mixB = sb("mixB", [2 * MIXK, TOK])
        xd = sb("xd", [P, NG, TOK])
        ctx1 = xd[:, 0, :].rearrange("p (b t) -> p b t", b=NB)
        x1n = xd[:, 1, :].rearrange("p (b t) -> p b t", b=NB)
        xn = x1n
        q1 = xd[:, 2:2 + HPG, :]
        low = {g: sb(f"low_{g}", [n, TOK]) for g, n in (("w", LORA), ("k", LORA), ("g", P))}
        low["a"] = mixB
        r_raw = sb("r_raw", [P, TOK])
        k_raw = sb("k_raw", [P, TOK])
        xm = k_raw
        k_sq = sb("k_sq", [P, TOK])
        rkx = k_sq
        kn = sb("kn", [P, TOK])
        norm = sb("norm", [P, NB])
        norm_inv = sb("norm_inv", [P, NB])
        decay = sb("decay", [P, TOK])
        v_tok = sb("v_tok", [P, NB, P])
        g_tok = sb("g_tok", [P, NB, P])
        ra = sb("ra", [P, 2, TOK])
        bk = sb("bk", [P, 2, TOK])
        root_decay, gate_a = bk[:, 0, :], bk[:, 1, :]
        block_decay = {2 * n: sb(f"block_decay{2 * n}", [P, TOK // (2 * n)]) for n in LEVELS}
        norm_diag = xd[:, 0, :].rearrange("p (b t) -> p b t", b=NB)
        A = sb("A", [P, NU, 4, P])
        A_level = sb("A_level", [P, NU, P])
        inv = sb("inv", [P, NU, P])
        invT = sb("invT", [P, NU, P])
        AZ = sb("AZ", [P, NU, P])
        b_tok, k_tok = A_level[:, 0:NB, :], A_level[:, NB:2 * NB, :]
        bonus = sb("bonus", [P, NU])
        XU = AZ[:].rearrange("p (s u) (v d) -> p s (u v) d", s=2, d=HS)
        X, U = XU[:, 0], XU[:, 1]
        y = sb("y", [P, NU, HS])
        gn_stats = sb("gn_stats", [P, NU, 6])
        gn_mom = sb("gn_mom", [P, NU, 2])
        gn_rstd = sb("gn_rstd", [P, NU])
        y_mul = y
        bonus_v = dx[:].rearrange("p b (h d) -> p (b h) d", h=NH)
        zT = sb("zT", [P, TOK])
        state_dec = sb("state_dec", [P, NB, HS])

        logits = sb("logits", [P, NB, NE])
        top = sb("top", [P, NB, 8])
        top_at = sb("top_at", [P, NB, 8], U32)
        top_atf = sb("top_atf", [P, NB, 8])
        top_gap = sb("top_gap", [P, NB])
        top_exp = sb("top_exp", [P, NB])
        top_sum = sb("top_sum", [P, NB])
        top_w = sb("top_w", [P, 2, NB])
        hot = sb("hot", [P, 2, NB, NE])
        comb = [sb(f"comb{l}", [P, NB, NE]) for l in range(2)]
        acc0 = sb("acc0", [P, NB, P])
        act0 = sb("act0", [P, 2, TOK])
        hid = sb("hid", [P, 2, K1, TOK])
        v1 = sb("v1", [P, NB, P])
        v1p = low["g"][:].rearrange("p (b d) -> p b d", b=NB)
        neg_max = sb("neg_max", [P, 3, 2])
        prob = sb("prob", [P, 3, 2, KEYS])
        prob_sum = sb("prob_sum", [P, NB, H1])
        prob_inv = sb("prob_inv", [P, NB, H1])
        pT = sb("pT", [P, 2, 2, P])
        cT = zT
        acc1 = sb("acc1", [P, NB, P])
        out_tile = sb("out_tile", [P, NB, P])

        weights_in = sem("weights_in")
        experts_in = sem("experts_in")
        x_in = sem("x_in")
        out_done = sem("out_done")
        const_step = sem("const_step")
        front_consts = sem("front_consts")
        consts = sem("consts")
        settled = sem("settled")
        per_tile, counted, of_front = {}, {}, set()

        def step(name, n=1):
            per_tile[name] = (sem(name), n)

        for name, n in [
            ("front_ready", 1),
            ("xd_ready", NG), ("decay_ready", 1), ("root_ready", 1),
            ("wkv_in", 4), ("rkx_ready", 1), ("blocks_grown", 2 * len(LEVELS)), ("block_decay_ready", len(LEVELS)),
            ("inv_base", 1), ("inv_start", 1), ("A_level_ready", len(LEVELS) - 1), ("state_step", 1),
            ("gn_stats_ready", NU), ("gn_mom_ready", NU), ("y_step", 4), ("bonus_v_ready", 4), ("z_ready", 1), ("av_done", NPAIRS),
            ("top_ready1", 3), ("gap_ready1", 1), ("top_exp1", 1), ("top_w_step1", 3), ("hot_step1", 2), ("comb_ready1", 1),
            ("norm_stats1", NB), ("norm_moments1", NB), ("norm_var1", 1), ("norm_root1", 1), ("norm_rstd1", 1), ("gn_var", 1), ("gn_root", 1), ("norm_inv_ready", 1), ("norm_diag_ready", 1), ("norm_root", 1),
            ("x1n_ready", NB), ("fronts_kept", 2), ("neg_max_ready", NPAIRS), ("mask_kept", 1),
            ("prob_inv_ready", 1), ("tanh_done", NF * K1),
        ]:
            step(name, n)
        for name, n in [
            ("norm_stats0", NB), ("norm_moments0", NB), ("norm_var0", 1), ("norm_root0", 1), ("norm_rstd0", 1), ("xn_ready", NB),
            ("front_kept", 1), ("dx_ready", 1), ("xm_ready", 1),
            ("top_ready0", 3), ("gap_ready0", 1), ("top_exp0", 1), ("top_w_step0", 3), ("hot_step0", 2), ("comb_ready0", 1),
        ]:
            step(name, n)
            of_front.add(name)

        def made(i, name, k=None):
            s, n = per_tile[name]
            k = n if k is None else k
            if name in of_front:
                return s, k if i is None else i * n + n + k
            return s, i * n + k

        def last_tile(i):
            b = bank_of["o1"]
            assert turn_of["o1"] == turns[b] - 1 and not turns_before[b]
            return bank_taken[b], i * turns[b] + 1

        def makes(name):
            counted[name] = counted.get(name, 0) + 1
            return per_tile[name][0], 1

        def settle(eng):
            eng.sem_inc(settled, 1)

        block = ctx.enter_context(nc.Block())

        loads = [
            (xA, io["x_A"]), (xB_lo, io["x_B_lo"]), (xB_hi, io["x_B_hi"]), (lam, io["lambdas"]),
            *[(vec[n], io[n]) for n in VECS],
            *[(lowA[g], io[f"{g}_A"]) for g in "wkag"], *[(lowB[g], io[f"{g}_B"]) for g in "wkag"],
            *[(proj[g], io[f"{g}W_T"]) for g in "rkvo"],
            (Wr, io["Wr"]), (W1, io["W1"]), (W3, io["W3"]), (W2, io["W2"]),
            *[(attnW[g], io[f"W{g}"]) for g in "qkvo"], (gateW, io["gateW"]),
        ]
        experts = [(F1, io["F1"]), (F2, io["F2"])]

        @block.sync
        def _(sp):
            sp.dma_start(x_tile[:], x_dram[:, 0:P, :].rearrange("b t d -> t b d")).then_inc(x_in, 16)
            for dst, src in loads:
                sp.dma_start(dst[:], src[:]).then_inc(weights_in, 16)
            for dst, src in ((gamma, io["gn_gamma"]), (beta, io["gn_beta"])):
                sp.dma_start(dst[:], src[:].partition_broadcast(P)).then_inc(weights_in, 16)
            for dst, src in experts:
                sp.dma_start(dst[:], src[:]).then_inc(experts_in, 16)
            with sp.Fori(0, NT) as i:
                sp.wait_ge(*is_taken(i, "y0_0"))
                sp.dma_start(x_tile[:], x_dram[:, bass.ds(sp.snap((i + 1) % NT * P), P), :].rearrange("b t d -> t b d")).then_inc(x_in, 16)
                sp.wait_ge(*is_taken(i, "o1"))
                sp.dma_start(out[:, bass.ts(i, P), :].rearrange("b t d -> t b d"), out_tile[:]).then_inc(out_done, 16)
            sp.wait_ge(out_done, 16 * NT + 16)

        @block.gpsimd
        def _(pool):
            for s in bank_taken:
                pool.sem_inc(s, 1)
            pool.sem_inc(out_done, 16)
            pool.sem_inc(per_tile["front_ready"][0], 1)
            n = 0

            def link(ins):
                nonlocal n
                n += 1
                ins.then_inc(const_step, 1)
                pool.wait_ge(const_step, n)

            link(pool.memset(ident[:], 0.0))
            link(pool.affine_select(out=ident[:], in_=ident[:], compare_op=ALU.not_equal, fill=1.0, base=0,
                                    pattern=[[-1, P]], channel_multiplier=1))
            link(pool.memset(xnT[:, :, P:P + 1], 0.0))
            link(pool.tensor_copy(xnT[:, :, 0:1], xnT[:, :, P:P + 1]))
            pool.sem_inc(*makes("front_kept"))
            link(pool.iota(expert_no[:], pattern=[[1, NE]], base=0, channel_multiplier=0,
                           allow_small_or_imprecise_dtypes=True))
            pool.sem_inc(front_consts, 1)
            link(pool.tensor_copy(ident16[:], ident[:]))
            link(pool.memset(ones[:], 1.0))
            link(pool.memset(head_ones[:], 1.0))
            link(pool.affine_select(out=head_ones[:, 0:1], in_=head_ones[:, 0:1], compare_op=ALU.is_ge, fill=0.0,
                                    base=HS - 1, pattern=[[0, 1]], channel_multiplier=-1))
            link(pool.affine_select(out=head_ones[:, 1:2], in_=head_ones[:, 1:2], compare_op=ALU.is_ge, fill=0.0,
                                    base=-HS, pattern=[[0, 1]], channel_multiplier=1))
            every = A[:, 0, 0, 0:P // D1].rearrange("p (g j) -> p g j", j=HPG)
            link(pool.memset(every, 1.0))
            link(pool.affine_select(out=every, in_=every, compare_op=ALU.is_ge, fill=0.0, base=0,
                                    pattern=[[-32, P // 32], [-D1, HPG]], channel_multiplier=1))
            link(pool.affine_select(out=every, in_=every, compare_op=ALU.is_ge, fill=0.0, base=D1 - 1,
                                    pattern=[[32, P // 32], [D1, HPG]], channel_multiplier=-1))
            link(pool.tensor_tensor(group_head[:], every[:, 0, :], every[:, 1, :], ALU.add))
            for grp in range(2, P // 32):
                link(pool.tensor_tensor(group_head[:], group_head[:], every[:, grp, :], ALU.add))
            link(pool.tensor_scalar(group_head[:], group_head[:], float(D1) ** -0.5, None, ALU.mult))
            link(pool.memset(level_mask[:], 0.0))
            for m, L in enumerate(LEVELS):
                v = level_mask[:, m, :].rearrange("p (g h t) -> p g h t", h=2, t=L)[:, :, 1, :]
                G = P // (2 * L)
                link(pool.memset(v, 1.0))
                link(pool.affine_select(out=v, in_=v, compare_op=ALU.is_ge, fill=0.0, base=0,
                                        pattern=[[-2 * L, G], [0, L]], channel_multiplier=1))
                link(pool.affine_select(out=v, in_=v, compare_op=ALU.is_ge, fill=0.0, base=L - 1,
                                        pattern=[[2 * L, G], [0, L]], channel_multiplier=-1))
            link(pool.memset(key_mask[:], 0.0))
            link(pool.affine_select(out=key_mask[:], in_=key_mask[:], compare_op=ALU.is_ge, fill=MASKED, base=WIN,
                                    pattern=[[0, 2], [-1, KEYS]], channel_multiplier=1))
            link(pool.affine_select(out=key_mask[:], in_=key_mask[:], compare_op=ALU.is_ge, fill=MASKED, base=-1,
                                    pattern=[[0, 2], [1, KEYS]], channel_multiplier=-1))
            link(pool.affine_select(out=key_mask_now[:], in_=key_mask[:], compare_op=ALU.is_ge, fill=MASKED, base=-WIN,
                                    pattern=[[0, 2], [1, KEYS]], channel_multiplier=0))
            link(pool.memset(A[:], 0.0))
            link(pool.memset(state[:], 0.0))
            link(pool.memset(x1nT[:, :, P:KEYS], 0.0))
            pool.memset(kT1[:, :, P:KEYS], 0.0).then_inc(consts, 1)

            with pool.Fori(0, NT) as i:
                pool.wait_ge(*last_tile(i))
                for g in range(NG):
                    pool.wait_ge(*is_taken(i, f"miu{g}"))
                    pool.tensor_tensor(xd[:, g, :].rearrange("p (b t) -> p b t", b=NB), xnT[:, :, 1:1 + P],
                                            xd[:, g, :].rearrange("p (b t) -> p b t", b=NB), ALU.add).then_inc(*makes("xd_ready"))
                pool.wait_ge(*is_taken(i, "bonus"))
                pool.tensor_tensor(bonus_v, v_tok[:].rearrange("p b (h n) -> p (b h) n", h=NH),
                                        bonus[:].unsqueeze(2).broadcast_to([P, NU, HS]), ALU.mult).then_inc(*makes("bonus_v_ready"))
                pool.wait_ge(*made(i, "bonus_v_ready", 1))
                pool.tensor_tensor(dx[:], dx[:], beta[:].unsqueeze(1).broadcast_to([P, NB, P]), ALU.add).then_inc(*makes("bonus_v_ready"))
                pool.wait_ge(*is_taken(i, "g"))
                pool.wait_ge(*made(i, "bonus_v_ready", 2))
                pool.tensor_tensor(dx[:], dx[:], g_tok[:], ALU.mult).then_inc(*makes("bonus_v_ready"))
                pool.wait_ge(*made(i, "bonus_v_ready", 3))
                pool.tensor_tensor(g_tok[:], g_tok[:], gamma[:].unsqueeze(1).broadcast_to([P, NB, P]), ALU.mult).then_inc(*makes("bonus_v_ready"))
                pool.tensor_copy(x1nT[:, :, 0:WIN], x1nT[:, :, P:KEYS]).then_inc(*makes("fronts_kept"))
                pool.tensor_copy(kT1[:, :, 0:WIN], kT1[:, :, P:KEYS]).then_inc(*makes("fronts_kept"))
                pool.wait_ge(*is_taken(i, "y0_7"))
                settle(pool)
                pool.tensor_copy(xnT[:, :, 0:1], xnT[:, :, P:P + 1]).then_inc(*makes("front_kept"))
                pool.wait_ge(*is_filled(i, f"sc{NPAIRS - 1}"))
                settle(pool)
                pool.tensor_copy(key_mask_now[:], key_mask[:]).then_inc(*makes("mask_kept"))

        @block.scalar
        def _(act):
            def front(i, part):
                if part == "norm":
                    act.wait_ge(*made(i, "norm_var0"))
                    act.activation(rstd[:], rstd[:], ACT.Sqrt).then_inc(*makes("norm_root0"))
                if part == "xnT0":
                    act.wait_ge(*made(i, "front_kept"))
                    act.wait_ge(*is_filled(i, "xnT0"))
                    act.activation(xnT[:, :, 1:1 + P], bank("xnT0")[:].rearrange("p (b t) -> p b t", b=NB), ACT.Copy).then_inc(*takes("xnT0"))
                if part == "logit0":
                    act.wait_ge(*made(i, "gap_ready0"))
                    act.activation(top_exp[:], top_gap[:], ACT.Exp).then_inc(*makes("top_exp0"))
                if part == "mixA":
                    act.wait_ge(*is_filled(i, "mixA"))
                    act.activation(mixA[:], bank("mixA")[:], ACT.Tanh).then_inc(*takes("mixA"))
                if part == "mixB":
                    act.wait_ge(*is_filled(i, "mixB"))
                    act.activation(mixB[:], bank("mixB")[0:2 * MIXK, :], ACT.Tanh).then_inc(*takes("mixB"))

            def silu0(i, k):
                act.wait_ge(*is_filled(i, f"h0_{k}"))
                if k >= 2:
                    act.wait_ge(*is_taken(i, f"g0_{k - 2}"))
                act.activation(act0[:, k % 2, :], bank(f"h0_{k}")[:], ACT.Silu).then_inc(*takes(f"h0_{k}"))

            act.wait_ge(front_consts, 1)
            for part in ["norm", *FRONT_STEPS.values()]:
                front(None, part)
            act.wait_ge(weights_in, 16 * (len(loads) + 2))
            act.wait_ge(consts, 1)
            with act.Fori(0, NT) as i:
                for k in MIU_HID.values():
                    silu0(i, k)
                for g, f in (("w", ACT.Tanh), ("k", ACT.Tanh), ("a", ACT.Copy), ("g", ACT.Tanh)):
                    m = low[g].shape[0]
                    act.wait_ge(*is_filled(i, f"low_{g}"))
                    act.activation(low[g][:], bank(f"low_{g}")[0:m, :], f).then_inc(*takes(f"low_{g}"))
                act.wait_ge(*is_filled(i, "r"))
                act.activation(r_raw[:], bank("r")[:], ACT.Copy).then_inc(*takes("r"))
                act.wait_ge(*is_filled(i, "w"))
                act.activation(decay[:], bank("w")[:], ACT.Sigmoid, bias=vec["w_miu"][:]).then_inc(*takes("w"))
                act.wait_ge(*is_filled(i, "k"))
                act.activation(k_raw[:], bank("k")[:], ACT.Copy)
                act.activation(k_sq[:], bank("k")[:], ACT.Square).then_inc(*takes("k"))
                act.wait_ge(*is_filled(i, "a"))
                act.activation(gate_a, bank("a")[:], ACT.Sigmoid, bias=vec["a_time"][:]).then_inc(*takes("a"))
                act.wait_ge(*is_filled(i, "v"))
                act.activation(v_tok[:].rearrange("p b d -> p (b d)"), bank("v")[:], ACT.Copy).then_inc(*takes("v"))
                act.wait_ge(*is_filled(i, "g"))
                act.activation(g_tok[:].rearrange("p b d -> p (b d)"), bank("g")[:], ACT.Copy).then_inc(*takes("g"))
                act.wait_ge(*is_taken(i, "norm"))
                act.activation(norm[:], norm[:], ACT.Sqrt).then_inc(*makes("norm_root"))
                act.wait_ge(*made(i, "decay_ready"))
                act.activation(root_decay, decay[:], ACT.Sqrt).then_inc(*makes("root_ready"))
                for kind, n in EXPERT_FIRST + [item for items in SLOTS for item in items] + SLOTS_LAST:
                    if kind == "hid":
                        silu0(i, n)
                    if kind in ("T", "Z"):
                        dst = inv if kind == "T" else AZ
                        for q in range(2):
                            name = f"inv{n}{kind}{q}"
                            act.wait_ge(*is_filled(i, name))
                            act.activation(dst[:, 4 * q:4 * q + 4, :].rearrange("p u t -> p (u t)"), bank(name)[:], ACT.Copy).then_inc(*takes(name))
                act.wait_ge(*is_filled(i, "btok"))
                act.activation(b_tok.rearrange("p b d -> p (b d)"), bank("btok")[:], ACT.Copy).then_inc(*takes("btok"))
                act.wait_ge(*is_filled(i, "ktok"))
                act.activation(k_tok.rearrange("p b d -> p (b d)"), bank("ktok")[:], ACT.Copy).then_inc(*takes("ktok"))
                act.wait_ge(*is_filled(i, "bonus"))
                act.activation(bonus[:], bank("bonus")[:, 0:NU], ACT.Copy).then_inc(*takes("bonus"))
                for h in range(NH):
                    act.wait_ge(*is_filled(i, f"X{h}"))
                    act.activation(X[:, NB * h:NB * (h + 1)], bank(f"X{h}")[:, 0:NB * HS].rearrange("p (b d) -> p b d", b=NB), ACT.Copy).then_inc(*takes(f"X{h}"))
                silu0(i, K0 - 1)
                act.wait_ge(*is_filled(i, "U"))
                act.activation(U.rearrange("p u d -> p (u d)"), bank("U")[:], ACT.Copy).then_inc(*takes("U"))
                for h in range(NH):
                    act.wait_ge(*is_filled(i, f"Y{h}"))
                    act.activation(y[:].rearrange("p (b h) d -> p h b d", h=NH)[:, h], bank(f"Y{h}")[:, 0:NB * HS].rearrange("p (b d) -> p b d", b=NB), ACT.Copy).then_inc(*takes(f"Y{h}"))
                act.wait_ge(*made(i, "gn_var"))
                act.activation(gn_rstd[:], gn_rstd[:], ACT.Sqrt).then_inc(*makes("gn_root"))
                act.wait_ge(*is_filled(i, "zT"))
                act.activation(zT[:], bank("zT")[:], ACT.Copy).then_inc(*takes("zT"))
                act.wait_ge(*made(i, "norm_var1"))
                act.activation(rstd[:], rstd[:], ACT.Sqrt).then_inc(*makes("norm_root1"))
                act.wait_ge(*made(i, "fronts_kept"))
                act.wait_ge(*is_filled(i, "xnT1"))
                act.activation(x1nT[:, :, WIN:KEYS], bank("xnT1")[:].rearrange("p (b t) -> p b t", b=NB), ACT.Copy).then_inc(*takes("xnT1"))
                act.wait_ge(*made(i, "gap_ready1"))
                act.activation(top_exp[:], top_gap[:], ACT.Exp).then_inc(*makes("top_exp1"))
                act.wait_ge(*is_filled(i, "q1"))
                for j in range(HPG):
                    ins = act.activation(q1[:, j, :], bank("q1")[:], ACT.Copy, scale=group_head[:, j:j + 1])
                ins.then_inc(*takes("q1"))
                act.wait_ge(*is_filled(i, "k1"))
                act.activation(kT1[:, :, WIN:KEYS], bank("k1")[:].rearrange("p (b t) -> p b t", b=NB), ACT.Copy).then_inc(*takes("k1"))
                act.wait_ge(*is_filled(i, "v1"))
                act.activation(v1[:].rearrange("p b d -> p (b d)"), bank("v1")[:], ACT.Copy).then_inc(*takes("v1"))
                act.wait_ge(*is_filled(i, "v1p"))
                act.activation(v1p.rearrange("p b d -> p (b d)"), bank("v1p")[:], ACT.Copy).then_inc(*takes("v1p"))
                for n in range(STEPS1):
                    if n < NF * K1:
                        act.wait_ge(*is_filled(i, f"h1_{n}"))
                        if n >= 2:
                            act.wait_ge(*is_taken(i, f"h1_{n - 2}"))
                        act.activation(act0[:, n % 2, :], bank(f"h1_{n}")[:], ACT.Tanh, scale=0.5).then_inc(*makes("tanh_done"))
                    if n < NPAIRS:
                        b, p = n // NPAIR, n % NPAIR
                        act.wait_ge(*made(i, "neg_max_ready", n + 1))
                        if n >= 3:
                            act.wait_ge(*is_filled(i, f"pt{n - 3}"))
                        for j in range(2):
                            ins = act.activation(prob[:, n % 3, j, :], bank(f"sc{n}")[:, KEYS * j:KEYS * (j + 1)], ACT.Exp,
                                                 bias=neg_max[:, n % 3, j:j + 1],
                                                 accum_out=prob_sum[:, b, 2 * p + j:2 * p + j + 1])
                        ins.then_inc(*takes(f"sc{n}"))
                    if n == 8:
                        front(i, "norm")
                    if n - 1 in FRONT_STEPS:
                        front(i, FRONT_STEPS[n - 1])
                    if n == NPAIRS + 2:
                        act.wait_ge(*is_filled(i, "cT"))
                        act.activation(cT[:], bank("cT")[:], ACT.Copy).then_inc(*takes("cT"))
                act.wait_ge(*is_taken(i, "mixB"))
                act.sem_inc(*makes("front_ready"))

        @block.vector
        def _(dve):
            def norm_stats(i, layer, src):
                for b in range(NB):
                    dve.bn_stats(stats[:, b, :], src(b)).then_inc(*makes(f"norm_stats{layer}"))

            def norm_moments(i, layer):
                for b in range(NB):
                    dve.wait_ge(*made(i, f"norm_stats{layer}", b + 1))
                    settle(dve)
                    dve.bn_aggr(moments[:, b, :], stats[:, b, :]).then_inc(*makes(f"norm_moments{layer}"))
                dve.wait_ge(*made(i, f"norm_moments{layer}"))
                dve.tensor_scalar(rstd[:], moments[:, :, 1], LN_EPS, None, ALU.add).then_inc(*makes(f"norm_var{layer}"))

            def norm_apply(i, layer, src, dst, ready):
                dve.wait_ge(*made(i, f"norm_root{layer}"))
                dve.reciprocal(rstd[:], rstd[:]).then_inc(*makes(f"norm_rstd{layer}"))
                dve.wait_ge(*made(i, f"norm_rstd{layer}"))
                for b in range(NB):
                    dve.tensor_scalar(dst[:, b, :], src(b), moments[:, b, 0:1], rstd[:, b:b + 1],
                                           ALU.subtract, ALU.mult).then_inc(*makes(ready))

            def front(i, part):
                if part == "stats":
                    dve.wait_ge(x_in, 16 if i is None else 16 * i + 32)
                    norm_stats(i, 0, lambda b: x_tile[:, b, :])
                if part == "moments":
                    norm_moments(i, 0)
                if part == "norm":
                    norm_apply(i, 0, lambda b: x_tile[:, b, :], xn, "xn_ready")
                if part == "mix":
                    dve.wait_ge(*is_taken(i, "xnT0"))
                    dve.tensor_tensor(dx[:], xnT[:, :, 0:P], xnT[:, :, 1:1 + P], ALU.subtract).then_inc(*makes("dx_ready"))
                    dve.wait_ge(*made(i, "dx_ready"))
                    dve.scalar_tensor_tensor(out=xm[:].rearrange("p (b t) -> p b t", b=NB), in0=dx[:], scalar=vec["x_miu"][:],
                                             in1=xnT[:, :, 1:1 + P], op0=ALU.mult, op1=ALU.add).then_inc(*makes("xm_ready"))
                if part == "top":
                    route_top(i, 0)
                if part == "comb":
                    route_comb(i, 0)

            front_parts = {6: "stats", 7: "moments", 9: "norm", 13: "mix", 16: "top", 18: "comb"}

            def route_top(i, layer):
                L = str(layer)
                dve.wait_ge(*is_filled(i, "logit" + L))
                dve.tensor_copy(logits[:], bank("logit" + L)[:, 0:NB * NE].rearrange("p (b e) -> p b e", b=NB)).then_inc(*takes("logit" + L))
                dve.wait_ge(*is_taken(i, "logit" + L))
                settle(dve)
                for b in range(NB):
                    ins = dve.max(top[:, b, :], logits[:, b, :])
                ins.then_inc(*makes("top_ready" + L))
                dve.wait_ge(*made(i, "top_ready" + L, 1))
                settle(dve)
                for b in range(NB):
                    ins = dve.max_index(top_at[:, b, :], top[:, b, :], logits[:, b, :])
                ins.then_inc(*makes("top_ready" + L))
                dve.tensor_tensor(top_gap[:], top[:, :, 1], top[:, :, 0], ALU.subtract).then_inc(*makes("gap_ready" + L))
                dve.wait_ge(*made(i, "top_ready" + L, 2))
                dve.tensor_copy(top_atf[:], top_at[:]).then_inc(*makes("top_ready" + L))

            def route_comb(i, layer):
                L = str(layer)
                dve.wait_ge(*made(i, "top_exp" + L))
                dve.tensor_scalar(top_sum[:], top_exp[:], 1.0, 1.0 + layer, ALU.add, ALU.mult).then_inc(*makes("top_w_step" + L))
                dve.wait_ge(*made(i, "top_w_step" + L, 1))
                dve.reciprocal(top_w[:, 0, :], top_sum[:]).then_inc(*makes("top_w_step" + L))
                dve.wait_ge(*made(i, "top_w_step" + L, 2))
                dve.tensor_tensor(top_w[:, 1, :], top_w[:, 0, :], top_exp[:], ALU.mult).then_inc(*makes("top_w_step" + L))
                dve.wait_ge(*made(i, "top_ready" + L))
                for j in range(2):
                    ins = dve.tensor_tensor(hot[:, j], expert_no[:].unsqueeze(1).broadcast_to([P, NB, NE]),
                                            top_atf[:, :, j:j + 1].broadcast_to([P, NB, NE]), ALU.is_equal)
                ins.then_inc(*makes("hot_step" + L))
                dve.wait_ge(*made(i, "hot_step" + L, 1))
                dve.wait_ge(*made(i, "top_w_step" + L))
                for j in range(2):
                    ins = dve.tensor_tensor(hot[:, j], hot[:, j], top_w[:, j, :].unsqueeze(2).broadcast_to([P, NB, NE]), ALU.mult)
                ins.then_inc(*makes("hot_step" + L))
                dve.wait_ge(*made(i, "hot_step" + L))
                dve.tensor_tensor(comb[layer][:], hot[:, 0], hot[:, 1], ALU.add).then_inc(*makes("comb_ready" + L))

            def probs_out(i, n):
                if n >= 2:
                    dve.wait_ge(*made(i, "av_done", n - 1))
                dve.wait_ge(*is_filled(i, f"pt{n}"))
                dve.tensor_copy(pT[:, n % 2], bank(f"pt{n}")[:, 0:2 * P].rearrange("p (j t) -> p j t", j=2)).then_inc(*takes(f"pt{n}"))

            def context_out(i):
                dve.wait_ge(*made(i, "av_done"))
                dve.reciprocal(prob_inv[:], prob_sum[:]).then_inc(*makes("prob_inv_ready"))
                dve.wait_ge(*made(i, "prob_inv_ready"))
                dve.tensor_tensor(ctx1[:].rearrange("p b (h d) -> p (b h) d", d=D1),
                                  bank("av")[:].rearrange("p (h d) -> p h d", d=D1),
                                  prob_inv[:].rearrange("p b h -> p (b h)").unsqueeze(2).broadcast_to([P, NB * H1, D1]),
                                  ALU.mult).then_inc(*takes("av"))

            def expert_item(i, kind, n):
                if kind not in ("hid", "out"):
                    return
                if kind == "hid":
                    dve.wait_ge(*is_taken(i, f"h0_{n}"))
                    dve.wait_ge(*is_filled(i, f"g0_{n}"))
                    dve.tensor_tensor(hid[:, n // PAIR_TILES % 2, n % PAIR_TILES, :], act0[:, n % 2, :], bank(f"g0_{n}")[:],
                                      ALU.mult).then_inc(*takes(f"g0_{n}"))
                    return
                dve.wait_ge(*is_filled(i, f"y0_{n}"))
                if n:
                    dve.wait_ge(*is_taken(i, f"y0_{n - 1}"))
                for b in range(NB):
                    ins = dve.scalar_tensor_tensor(out=acc0[:, b, :], in0=bank(f"y0_{n}")[:, b * P:(b + 1) * P],
                                                   scalar=comb[0][:, b, n:n + 1], in1=(acc0 if n else x_tile)[:, b, :],
                                                   op0=ALU.mult, op1=ALU.add)
                ins.then_inc(*takes(f"y0_{n}"))

            def second(t, L):
                return t.rearrange("p s (g h t) -> p s g h t", h=2, t=L)[:, :, :, 1, :]

            def halves(t, L):
                return t[:].rearrange("p s (g h t) -> p s g h t", h=2, t=L)

            dve.wait_ge(front_consts, 1)
            for part in front_parts.values():
                if part == "mix":
                    dve.wait_ge(weights_in, 16 * (len(loads) + 2))
                front(None, part)
            dve.wait_ge(*is_taken(None, "mixB"))
            dve.wait_ge(consts, 1)
            with dve.Fori(0, NT) as i:
                dve.wait_ge(*last_tile(i))
                for g in range(NG):
                    dve.wait_ge(*is_filled(i, f"miu{g}"))
                    dve.scalar_tensor_tensor(out=xd[:, g, :], in0=bank(f"miu{g}")[:], scalar=lam[:, g:g + 1],
                                                   in1=dx[:].rearrange("p b t -> p (b t)"), op0=ALU.add, op1=ALU.mult).then_inc(*takes(f"miu{g}"))
                    if g - 1 in MIU_HID:
                        expert_item(i, "hid", MIU_HID[g - 1])
                dve.wait_ge(*is_filled(i, "norm"))
                dve.tensor_scalar(norm[:], bank("norm")[:, 0:NB], 1e-24, None, ALU.max).then_inc(*takes("norm"))
                dve.wait_ge(*is_taken(i, "w"))
                dve.tensor_scalar(decay[:], decay[:], 2.0 ** -115, float(np.exp(-0.5)), ALU.max, ALU.mult).then_inc(*makes("decay_ready"))
                dve.wait_ge(*made(i, "norm_root"))
                dve.reciprocal(norm_inv[:], norm[:]).then_inc(*makes("norm_inv_ready"))
                dve.wait_ge(*made(i, "norm_inv_ready"))
                dve.tensor_tensor(norm_diag, ident[:].unsqueeze(1).broadcast_to([P, NB, P]),
                                  norm_inv[:].unsqueeze(2).broadcast_to([P, NB, P]), ALU.mult).then_inc(*makes("norm_diag_ready"))
                dve.wait_ge(*made(i, "decay_ready"))
                dve.tensor_tensor(ra[:, 0, :], r_raw[:], decay[:], ALU.mult).then_inc(*makes("wkv_in"))
                expert_item(i, *EXPERT_FIRST[0])
                dve.wait_ge(*is_filled(i, "norm_inv"))
                dve.wait_ge(*is_taken(i, "k"))
                dve.tensor_tensor(kn[:], k_raw[:], bank("norm_inv")[:], ALU.mult).then_inc(*takes("norm_inv"))
                dve.wait_ge(*is_taken(i, "norm_inv"))
                dve.wait_ge(*made(i, "root_ready"))
                dve.tensor_tensor(bk[:, 0, :], kn[:], root_decay, ALU.mult).then_inc(*makes("wkv_in"))
                dve.scalar_tensor_tensor(out=bk[:, 1, :], in0=gate_a, scalar=2.0, in1=kn[:], op0=ALU.mult, op1=ALU.mult).then_inc(*makes("wkv_in"))
                dve.tensor_scalar(ra[:, 1, :], kn[:], -1.0, None, ALU.mult).then_inc(*makes("wkv_in"))
                dve.scalar_tensor_tensor(out=rkx[:], in0=r_raw[:], scalar=vec["x_time"][:], in1=kn[:],
                                              op0=ALU.mult, op1=ALU.mult).then_inc(*makes("rkx_ready"))

                for item in EXPERT_FIRST[1:]:
                    expert_item(i, *item)

                def keep_level(m, L, w):
                    name = f"lev{L}_{w}"
                    dve.wait_ge(*is_filled(i, name))
                    if L:
                        dve.wait_ge(*is_taken(i, f"lev{L // 2}_{w}"))
                    if L == 0:
                        dst = A[:, 2 * w:2 * w + 2].rearrange("p u (s q) t -> p (u s) q t", s=2)[:, :, 0, :]
                        mask = ident[:].bitcast(I32).unsqueeze(1).broadcast_to([P, 4, P])
                        src = bank(name)[:].rearrange("p (s t) -> p s t", s=4)
                    else:
                        dst = second(A[:, 2 * w:2 * w + 2].rearrange("p u s t -> p (u s) t"), L)
                        mask = level_mask[:, m, :].bitcast(I32).rearrange("p (g h t) -> p g h t", h=2, t=L)[:, :, 1, :]
                        mask = mask.unsqueeze(1).broadcast_to([P, 8, P // (2 * L), L])
                        src = bank(name)[:].rearrange("p (s g t) -> p s g t", s=8, t=L)
                    settle(dve)
                    dve.copy_predicated(dst, mask, src).then_inc(*takes(name))

                def grow(m, L):
                    G = TOK // (2 * L)
                    d = decay[:] if L == 1 else block_decay[L][:]
                    dv = d.rearrange("p (g h) -> p g h", h=2)
                    if L > 1:
                        dve.wait_ge(*made(i, "block_decay_ready", m))
                        dve.wait_ge(*made(i, "blocks_grown", 2 * m))
                    v = halves(ra, L)[:, :, :, 1, :]
                    dve.tensor_tensor(v, v, dv[:, :, 0:1].unsqueeze(1).broadcast_to([P, 2, G, L]), ALU.mult).then_inc(*makes("blocks_grown"))
                    v = halves(bk, L)[:, :, :, 0, :]
                    dve.tensor_tensor(v, v, dv[:, :, 1:2].unsqueeze(1).broadcast_to([P, 2, G, L]), ALU.mult).then_inc(*makes("blocks_grown"))
                    dve.tensor_tensor(block_decay[2 * L][:], dv[:, :, 0], dv[:, :, 1], ALU.mult).then_inc(*makes("block_decay_ready"))

                def inverse_item(kind, n, kept):
                    if kind == "T":
                        dve.wait_ge(*is_taken(i, kept))
                        dve.tensor_tensor(A_level[:], A[:, :, 3, :],
                                          level_mask[:, LEVELS.index(n), :].unsqueeze(1).broadcast_to([P, NU, P]),
                                          ALU.mult).then_inc(*makes("A_level_ready"))
                        dve.wait_ge(*made(i, "A_level_ready", LEVELS.index(n)))
                    if kind == "D":
                        for q in range(2):
                            dve.wait_ge(*is_filled(i, f"inv{n}D{q}"))
                            v = second(invT[:, 4 * q:4 * q + 4, :], n)
                            d = bank(f"inv{n}D{q}")[:, 0:2 * P].rearrange("p (u g t) -> p u g t", u=4, t=n)
                            dve.tensor_tensor(v, v, d, ALU.add).then_inc(*takes(f"inv{n}D{q}"))

                for s in range(len(SLOTS)):
                    m = s // 2 - 1
                    L = LEVELS[m] if m >= 0 else 0
                    for item in SLOTS[s - 1] if s else []:
                        inverse_item(*item, kept)
                    if s % 2 and L:
                        dve.wait_ge(*is_filled(i, f"lev{L}_3"))
                        grow(m, L)
                    for w in (2 * s % 4, 2 * s % 4 + 1):
                        keep_level(m, L, w)
                        kept = f"lev{L}_{w}"
                    for item in SLOTS[s - 1] if s else []:
                        expert_item(i, *item)
                    if s == 3:
                        for w in range(4):
                            dve.wait_ge(*is_taken(i, f"lev{LEVELS[0]}_{w}"))
                        dve.tensor_tensor(invT[:], A[:, :, 3, :], level_mask[:, 0, :].unsqueeze(1).broadcast_to([P, NU, P]), ALU.mult).then_inc(*makes("inv_base"))
                        dve.wait_ge(*made(i, "inv_base"))
                        dve.tensor_tensor(invT[:], invT[:], ident[:].unsqueeze(1).broadcast_to([P, NU, P]), ALU.add).then_inc(*makes("inv_start"))
                for item in SLOTS[-1] + SLOTS_LAST:
                    expert_item(i, *item)
                    inverse_item(*item, kept)
                for item in AFTER["X0"] + AFTER["U"]:
                    expert_item(i, *item)
                D = block_decay[2 * LEVELS[-1]]
                dve.wait_ge(*made(i, "block_decay_ready"))
                dve.tensor_tensor(state_dec[:], state[:], D[:].unsqueeze(2).broadcast_to([P, NB, HS]), ALU.mult).then_inc(*makes("state_step"))
                dve.wait_ge(*made(i, "state_step", 1))
                dve.wait_ge(*is_filled(i, "S"))
                dve.tensor_tensor(state[:], state_dec[:], bank("S")[:, 0:NB * HS].rearrange("p (b d) -> p b d", b=NB), ALU.add).then_inc(*takes("S"))
                dve.wait_ge(*is_taken(i, "Y0"))
                dve.wait_ge(*is_taken(i, "Y1"))
                for u in range(NU):
                    dve.bn_stats(gn_stats[:, u, :], y[:, u, :]).then_inc(*makes("gn_stats_ready"))
                for u in range(NU):
                    dve.wait_ge(*made(i, "gn_stats_ready", u + 1))
                    settle(dve)
                    dve.bn_aggr(gn_mom[:, u, :], gn_stats[:, u, :]).then_inc(*makes("gn_mom_ready"))
                dve.wait_ge(*made(i, "gn_mom_ready"))
                dve.tensor_scalar(gn_rstd[:], gn_mom[:, :, 1], GN_EPS, None, ALU.add).then_inc(*makes("gn_var"))
                dve.wait_ge(*made(i, "gn_root"))
                dve.reciprocal(gn_rstd[:], gn_rstd[:]).then_inc(*makes("y_step"))
                dve.tensor_tensor(y_mul[:], y[:], gn_mom[:, :, 0:1].broadcast_to([P, NU, HS]), ALU.subtract).then_inc(*makes("y_step"))
                dve.wait_ge(*made(i, "y_step", 2))
                dve.tensor_tensor(y_mul[:], y_mul[:], gn_rstd[:].unsqueeze(2).broadcast_to([P, NU, HS]), ALU.mult).then_inc(*makes("y_step"))
                dve.wait_ge(*made(i, "y_step", 3))
                ym = y_mul[:].rearrange("p (b h) d -> p b (h d)", h=NH)
                dve.wait_ge(*made(i, "bonus_v_ready"))
                dve.tensor_tensor(ym, ym, g_tok[:], ALU.mult).then_inc(*makes("y_step"))
                dve.wait_ge(*made(i, "y_step", 4))
                dve.tensor_tensor(ym, ym, dx[:], ALU.add).then_inc(*makes("z_ready"))
                for item in AFTER["S"]:
                    expert_item(i, *item)
                dve.wait_ge(*is_filled(i, "o0"))
                dve.wait_ge(*is_taken(i, f"y0_{NE - 1}"))
                dve.tensor_tensor(acc0[:], acc0[:],
                                  bank("o0")[:].rearrange("p (b d) -> p b d", b=NB), ALU.add).then_inc(*takes("o0"))
                dve.wait_ge(*is_taken(i, "o0"))
                norm_stats(i, 1, lambda b: acc0[:, b, :])
                norm_moments(i, 1)
                norm_apply(i, 1, lambda b: acc0[:, b, :], x1n, "x1n_ready")
                route_top(i, 1)
                route_comb(i, 1)
                for n in range(STEPS1 + 1):
                    if 2 <= n < NPAIRS + 2:
                        probs_out(i, n - 2)
                    if n < NPAIRS:
                        dve.wait_ge(*is_filled(i, f"sc{n}"))
                        if n >= 3:
                            dve.wait_ge(*is_taken(i, f"sc{n - 3}"))
                        dve.tensor_reduce(neg_max[:, n % 3, :], bank(f"sc{n}")[:, 0:2 * KEYS].rearrange("p (j s) -> p j s", j=2),
                                          AX.X, ALU.max, negate=True).then_inc(*makes("neg_max_ready"))
                    if n == NPAIRS + 2:
                        context_out(i)
                    if 1 <= n <= NF * K1:
                        k = n - 1
                        dve.wait_ge(*made(i, "tanh_done", n))
                        dve.scalar_tensor_tensor(out=hid[:, k // K1 % 2, k % K1, :], in0=act0[:, k % 2, :], scalar=1.0,
                                                 in1=bank(f"h1_{k}")[:], op0=ALU.add, op1=ALU.mult).then_inc(*takes(f"h1_{k}"))
                    if n in front_parts:
                        front(i, front_parts[n])
                    if n >= K1 + 2 and (n - 2) % K1 == 0:
                        e = (n - 2) // K1 - 1
                        dve.wait_ge(*is_filled(i, f"y1_{e}"))
                        if e == 0:
                            dve.scalar_tensor_tensor(out=acc1[:], in0=bank("y1_0")[:].rearrange("p (b d) -> p b d", b=NB), scalar=0.5,
                                                     in1=acc0[:], op0=ALU.mult, op1=ALU.add).then_inc(*takes("y1_0"))
                            continue
                        dve.wait_ge(*is_taken(i, f"y1_{e - 1}"))
                        for b in range(NB):
                            ins = dve.scalar_tensor_tensor(out=acc1[:, b, :], in0=bank(f"y1_{e}")[:, b * P:(b + 1) * P],
                                                           scalar=comb[1][:, b, e - 1:e], in1=acc1[:, b, :],
                                                           op0=ALU.mult, op1=ALU.add)
                        ins.then_inc(*takes(f"y1_{e}"))
                dve.wait_ge(*is_filled(i, "o1"))
                dve.wait_ge(*is_taken(i, f"y1_{NF - 1}"))
                dve.wait_ge(out_done, 16 * i + 16)
                dve.tensor_tensor(out_tile[:], acc1[:], bank("o1")[:].rearrange("p (b d) -> p b d", b=NB), ALU.add).then_inc(*takes("o1"))

        @block.tensor
        def _(pe):
            def mm(dst, lhsT, rhs, start=True, stop=True, onto=False):
                return pe.matmul(dst, lhsT, rhs, start=start, stop=stop, skip_group_check=onto)

            def cols(b, n=P):
                return slice(b * n, (b + 1) * n)

            def rows(h):
                return slice(h * HS, (h + 1) * HS)

            pe.wait_ge(front_consts, 1)
            def front(i, part):
                if part == "xnT0":
                    pe.wait_ge(*is_free(i, "xnT0"))
                    for b in range(NB):
                        pe.wait_ge(*made(i, "xn_ready", b + 1))
                        ins = pe.transpose(bank("xnT0")[:, cols(b)], xn[:, b, :], ident[:])
                    ins.then_inc(*fills("xnT0"))
                if part == "logit0":
                    pe.wait_ge(*is_free(i, "logit0"))
                    for b in range(NB):
                        ins = mm(bank("logit0")[:, cols(b, NE)], xnT[:, b, 1:1 + P], Wr[:])
                    ins.then_inc(*fills("logit0"))
                if part == "mixA":
                    pe.wait_ge(*made(i, "xm_ready"))
                    pe.wait_ge(*is_free(i, "mixA"))
                    mm(bank("mixA")[:], xA[:, 0:P], xm[:]).then_inc(*fills("mixA"))
                if part == "mixB":
                    pe.wait_ge(*is_free(i, "mixB"))
                    mm(bank("mixB")[0:2 * MIXK, :], xA[:, P:NG * MIXK], xm[:]).then_inc(*fills("mixB"))

            for part in FRONT_STEPS.values():
                if part == "logit0":
                    pe.wait_ge(weights_in, 16 * (len(loads) + 2))
                front(None, part)
            pe.wait_ge(*is_taken(None, "mixB"))
            pe.wait_ge(consts, 1)
            with pe.Fori(0, NT) as i:
                pe.wait_ge(per_tile["front_ready"][0], i + 1)
                for g in range(NG):
                    name, w = (f"h0_{MIU_HID[g]}", W1) if g in MIU_HID else (f"g0_{MIU_HID[g - 1]}", W3)
                    pe.wait_ge(*is_free(i, name))
                    mm(bank(name)[:], w[:, cols(int(name[3:]))], xnT[:, :, 1:1 + P]).then_inc(*fills(name))
                    w, m, at = (xB_lo, mixA, g) if g < 4 else (xB_hi, mixB, g - 4)
                    r = slice(MIXK * at, MIXK * (at + 1))
                    pe.wait_ge(*is_free(i, f"miu{g}"))
                    mm(bank(f"miu{g}")[:], w[r, :], m[r, :]).then_inc(*fills(f"miu{g}"))
                at = {g: n for n, g in enumerate("rwkvag")}
                for g in "wkag":
                    pe.wait_ge(*made(i, "xd_ready", at[g] + 1))
                    pe.wait_ge(*is_free(i, f"low_{g}"))
                    mm(bank(f"low_{g}")[0:low[g].shape[0], :], lowA[g][:], xd[:, at[g], :]).then_inc(*fills(f"low_{g}"))
                pe.wait_ge(*is_free(i, "r"))
                mm(bank("r")[:], proj["r"][:], xd[:, at["r"], :]).then_inc(*fills("r"))
                pe.wait_ge(*is_taken(i, "low_w"))
                pe.wait_ge(*is_free(i, "w"))
                mm(bank("w")[:], lowB["w"][:], low["w"][:]).then_inc(*fills("w"))
                pe.wait_ge(*is_free(i, "k"))
                mm(bank("k")[:], proj["k"][:], xd[:, at["k"], :], stop=False)
                pe.wait_ge(*is_taken(i, "low_k"))
                mm(bank("k")[:], lowB["k"][:], low["k"][:], start=False).then_inc(*fills("k"))
                pe.wait_ge(*is_taken(i, "low_a"))
                pe.wait_ge(*is_free(i, "a"))
                mm(bank("a")[:], lowB["a"][:], low["a"][:]).then_inc(*fills("a"))
                pe.wait_ge(*is_free(i, "v"))
                for b in range(NB):
                    ins = mm(bank("v")[:, cols(b)], xd[:, at["v"], cols(b)], proj["v"][:])
                ins.then_inc(*fills("v"))
                pe.wait_ge(*is_taken(i, "low_g"))
                pe.wait_ge(*is_free(i, "g"))
                for b in range(NB):
                    ins = mm(bank("g")[:, cols(b)], low["g"][:, cols(b)], lowB["g"][:])
                ins.then_inc(*fills("g"))
                def expert_item(kind, n):
                    if kind in ("T", "Z", "D"):
                        for q in range(2):
                            name = f"inv{n}{kind}{q}"
                            before = {"T": f"inv{n // 2}D{q}", "Z": f"inv{n}T{q}", "D": f"inv{n}Z{q}"}[kind]
                            if kind == "T" and n == LEVELS[1]:
                                pe.wait_ge(*made(i, "inv_start"))
                            elif bank_of[before] != bank_of[name]:
                                pe.wait_ge(*is_taken(i, before))
                            if kind == "Z" and q == 0:
                                pe.wait_ge(*made(i, "A_level_ready", LEVELS.index(n)))
                            pe.wait_ge(*is_free(i, name))
                            for u in range(4 * q, 4 * q + 4):
                                if kind == "T":
                                    ins = pe.transpose(bank(name)[:, cols(u % 4)], invT[:, u, :], ident[:])
                                if kind == "Z":
                                    ins = mm(bank(name)[:, cols(u % 4)], A_level[:, u, :], inv[:, u, :])
                                if kind == "D":
                                    ins = mm(bank(name)[:, cols(u % 4, P // 2)], AZ[:, u, :],
                                             invT[:, u, :].rearrange("p (g h t) -> p g h t", h=2, t=n)[:, :, 1, :])
                            ins.then_inc(*fills(name))
                        return
                    if kind == "hid":
                        for name, w in ((f"h0_{n}", W1), (f"g0_{n}", W3)):
                            pe.wait_ge(*is_free(i, name))
                            mm(bank(name)[:], w[:, cols(n)], xnT[:, :, 1:1 + P]).then_inc(*fills(name))
                        return
                    j, first = n // 2, PAIR_TILES * (n // 2)
                    parts = [(0, 0, P), (1, 0, P // 2)] if n % 2 == 0 else [(1, P // 2, P), (2, 0, P)]
                    last_hid = f"g0_{first + parts[1][0]}"
                    if bank_of[last_hid] != bank_of[f"y0_{n}"]:
                        pe.wait_ge(*is_taken(i, last_hid))
                    pe.wait_ge(*is_free(i, f"y0_{n}"))
                    for b in range(NB):
                        for t, (k, lo, hi) in enumerate(parts):
                            ins = mm(bank(f"y0_{n}")[:, cols(b)], hid[lo:hi, j % 2, k, cols(b)],
                                     W2[lo:hi, first + k, :], start=t == 0, stop=t == 1)
                    ins.then_inc(*fills(f"y0_{n}"))

                pe.wait_ge(*is_taken(i, "k"))
                pe.wait_ge(*is_free(i, "norm"))
                for b in range(NB):
                    ins = mm(bank("norm")[:, b:b + 1], k_sq[:, cols(b)], ones[:, 0:1])
                ins.then_inc(*fills("norm"))
                expert_item(*EXPERT_FIRST[0])
                pe.wait_ge(*is_taken(i, "r"))
                pe.wait_ge(*made(i, "norm_diag_ready"))
                pe.wait_ge(*is_free(i, "norm_inv"))
                mm(bank("norm_inv")[:], ones[:], norm_diag).then_inc(*fills("norm_inv"))
                for item in EXPERT_FIRST[1:]:
                    expert_item(*item)
                pe.wait_ge(*made(i, "wkv_in"))
                for s, items in enumerate(SLOTS):
                    m = s // 2 - 1
                    L = LEVELS[m] if m >= 0 else 0
                    if L > 1 and s % 2 == 0:
                        pe.wait_ge(*made(i, "blocks_grown", 2 * m))
                    for w in (2 * s % 4, 2 * s % 4 + 1):
                        name = f"lev{L}_{w}"
                        pe.wait_ge(*is_free(i, name))
                        for n in range(4):
                            u, q = 2 * w + n // 2, n % 2
                            h, b = u // NB, u % NB
                            target = r_raw[rows(h), cols(b)]
                            if L:
                                target = ra[rows(h), :, cols(b)].rearrange("p s (g h t) -> p s g h t", h=2, t=L)[:, :, :, 1, :]
                            ins = mm(bank(name)[:, cols(n)], bk[rows(h), q, cols(b)], target)
                        ins.then_inc(*fills(name))
                    for item in items:
                        expert_item(*item)
                for item in SLOTS_LAST:
                    expert_item(*item)
                pe.wait_ge(*made(i, "blocks_grown"))
                for name, s in (("btok", 1), ("ktok", 0)):
                    pe.wait_ge(*is_free(i, name))
                    for b in range(NB):
                        ins = pe.transpose(bank(name)[:, cols(b)], bk[:, s, cols(b)], ident[:])
                    ins.then_inc(*fills(name))
                pe.wait_ge(*made(i, "rkx_ready"))
                pe.wait_ge(*is_free(i, "bonus"))
                for b in range(NB):
                    ins = mm(bank("bonus")[:, cols(b, NH)], rkx[:, cols(b)], head_ones[:])
                ins.then_inc(*fills("bonus"))
                pe.wait_ge(*is_taken(i, "v"))
                for h in range(NH):
                    pe.wait_ge(*is_free(i, f"X{h}"))
                    for b in range(NB):
                        mm(bank(f"X{h}")[:, cols(b, HS)], ra[rows(h), 1, cols(b)], state[rows(h), b, :], stop=False)
                        ins = mm(bank(f"X{h}")[:, cols(b, HS)], A[:, NB * h + b, 1, :], v_tok[:, b, rows(h)], start=False)
                    ins.then_inc(*fills(f"X{h}"))
                    for item in AFTER.get(f"X{h}", []):
                        expert_item(*item)
                pe.wait_ge(*is_taken(i, "X0"))
                pe.wait_ge(*is_taken(i, "X1"))
                pe.wait_ge(*is_taken(i, f"inv{LEVELS[-1]}D1"))
                pe.wait_ge(*is_free(i, "U"))
                for u in range(NU):
                    ins = mm(bank("U")[:, cols(u, HS)], invT[:, u, :], X[:, u, :])
                ins.then_inc(*fills("U"))
                for item in AFTER["U"]:
                    expert_item(*item)
                pe.wait_ge(*is_taken(i, "U"))
                for h in range(NH):
                    pe.wait_ge(*is_free(i, f"Y{h}"))
                    for b in range(NB):
                        u = NB * h + b
                        mm(bank(f"Y{h}")[:, cols(b, HS)], ra[rows(h), 0, cols(b)], state[rows(h), b, :], stop=False)
                        mm(bank(f"Y{h}")[:, cols(b, HS)], A[:, u, 2, :], U[:, u, :], start=False, stop=False)
                        ins = mm(bank(f"Y{h}")[:, cols(b, HS)], A[:, u, 0, :], v_tok[:, b, rows(h)], start=False)
                    ins.then_inc(*fills(f"Y{h}"))
                pe.wait_ge(*is_taken(i, "btok"))
                pe.wait_ge(*is_taken(i, "ktok"))
                pe.wait_ge(*is_free(i, "S"))
                for u in range(NU):
                    h, b = u // NB, u % NB
                    mm(bank("S")[rows(h), cols(b, HS)], b_tok[:, b, rows(h)], U[:, u, :], stop=False)
                    ins = mm(bank("S")[rows(h), cols(b, HS)], k_tok[:, b, rows(h)], v_tok[:, b, rows(h)], start=False)
                ins.then_inc(*fills("S"))
                for item in AFTER["S"]:
                    expert_item(*item)
                pe.wait_ge(*made(i, "z_ready"))
                pe.wait_ge(*is_free(i, "zT"))
                for b in range(NB):
                    ins = pe.transpose(bank("zT")[:, cols(b)], y_mul[:, NH * b:NH * (b + 1), :].rearrange("p h d -> p (h d)"), ident[:])
                ins.then_inc(*fills("zT"))
                pe.wait_ge(*is_taken(i, "zT"))
                pe.wait_ge(*is_free(i, "o0"))
                for b in range(NB):
                    ins = mm(bank("o0")[:, cols(b)], zT[:, cols(b)], proj["o"][:])
                ins.then_inc(*fills("o0"))
                pe.wait_ge(*is_free(i, "xnT1"))
                for b in range(NB):
                    pe.wait_ge(*made(i, "x1n_ready", b + 1))
                    ins = pe.transpose(bank("xnT1")[:, cols(b)], x1n[:, b, :], ident[:])
                ins.then_inc(*fills("xnT1"))
                pe.wait_ge(*is_taken(i, "xnT1"))
                pe.wait_ge(*is_free(i, "logit1"))
                for b in range(NB):
                    ins = mm(bank("logit1")[:, cols(b, NE)], x1nT[:, b, WIN:KEYS], gateW[:])
                ins.then_inc(*fills("logit1"))
                for g in "qk":
                    pe.wait_ge(*is_free(i, g + "1"))
                    mm(bank(g + "1")[:], attnW[g][:], x1nT[:, :, WIN:KEYS]).then_inc(*fills(g + "1"))
                pe.wait_ge(*is_free(i, "v1"))
                for b in range(NB):
                    ins = mm(bank("v1")[:, cols(b)], x1nT[:, b, WIN:KEYS], attnW["v"][:])
                ins.then_inc(*fills("v1"))
                pe.wait_ge(*is_free(i, "v1p"))
                for b in range(NB):
                    ins = mm(bank("v1p")[:, cols(b)], x1nT[:, b, 0:P], attnW["v"][:])
                ins.then_inc(*fills("v1p"))

                def scores(n):
                    b, p = n // NPAIR, n % NPAIR
                    if n == 0:
                        pe.wait_ge(*is_taken(i, "k1"))
                        pe.wait_ge(*is_taken(i, "q1"))
                    pe.wait_ge(*is_free(i, f"sc{n}"))
                    mm(bank(f"sc{n}")[:, 0:2 * KEYS], ident16[:], key_mask_now[:].rearrange("p j s -> p (j s)"))
                    for j in range(2):
                        h = 2 * p + j
                        r = slice(32 * (h // HPG), 32 * (h // HPG + 1))
                        ins = mm(bank(f"sc{n}")[:, cols(j, KEYS)], q1[r, h % HPG, cols(b)], kT1[r, b, :], start=False, onto=True)
                    ins.then_inc(*fills(f"sc{n}"))

                def turn(n):
                    pe.wait_ge(*is_taken(i, f"sc{n}"))
                    pe.wait_ge(*is_free(i, f"pt{n}"))
                    for j in range(2):
                        pe.transpose(bank(f"pt{n}")[:, cols(j)], prob[:, n % 3, j, WIN:KEYS], ident[:])
                        ins = pe.transpose(bank(f"pt{n}")[:, P * j:P * j + WIN], prob[0:WIN, n % 3, j, 0:P], ident[0:WIN, 0:WIN])
                    ins.then_inc(*fills(f"pt{n}"))

                def weigh(n):
                    b, p = n // NPAIR, n % NPAIR
                    if n == 0:
                        pe.wait_ge(*is_taken(i, "v1p"))
                        pe.wait_ge(*is_free(i, "av"))
                    pe.wait_ge(*is_taken(i, f"pt{n}"))
                    for j in range(2):
                        h = 2 * p + j
                        mm(bank("av")[WIN:P, cols(H1 * b + h, D1)], pT[:, n % 2, j, WIN:P], v1[:, b, cols(h, D1)])
                        ins = mm(bank("av")[0:WIN, cols(H1 * b + h, D1)], pT[:, n % 2, j, 0:WIN], v1p[:, b, cols(h, D1)])
                    ins.then_inc(*makes("av_done"))

                pe.wait_ge(experts_in, 16 * len(experts))
                for n in range(STEPS1):
                    if n < NPAIRS:
                        scores(n)
                    if n < NF * K1:
                        pe.wait_ge(*is_free(i, f"h1_{n}"))
                        mm(bank(f"h1_{n}")[:], F1[:, cols(n)], x1nT[:, :, WIN:KEYS]).then_inc(*fills(f"h1_{n}"))
                    if 1 <= n <= NPAIRS:
                        turn(n - 1)
                    if 2 <= n < NPAIRS + 2:
                        weigh(n - 2)
                    if n >= K1 + 1 and (n - 1) % K1 == 0:
                        e = (n - 1) // K1 - 1
                        pe.wait_ge(*is_taken(i, f"h1_{K1 * e + K1 - 1}"))
                        pe.wait_ge(*is_free(i, f"y1_{e}"))
                        for b in range(NB):
                            for k in range(K1):
                                ins = mm(bank(f"y1_{e}")[:, cols(b)], hid[:, e % 2, k, cols(b)], F2[:, K1 * e + k, :],
                                         start=k == 0, stop=k == K1 - 1)
                        ins.then_inc(*fills(f"y1_{e}"))
                    if n in FRONT_STEPS:
                        front(i, FRONT_STEPS[n])
                    if n == NPAIRS + 2:
                        pe.wait_ge(*is_taken(i, "av"))
                        pe.wait_ge(*is_free(i, "cT"))
                        for b in range(NB):
                            ins = pe.transpose(bank("cT")[:, cols(b)], ctx1[:, b, :], ident[:])
                        ins.then_inc(*fills("cT"))
                    if n == NPAIRS + 3:
                        pe.wait_ge(*is_taken(i, "cT"))
                        pe.wait_ge(*is_free(i, "o1"))
                        for b in range(NB):
                            ins = mm(bank("o1")[:, cols(b)], cT[:, cols(b)], attnW["o"][:])
                        ins.then_inc(*fills("o1"))

        for name, (_, n) in per_tile.items():
            assert counted.get(name) == n * (1 + (name in of_front)), (name, counted.get(name), n)


def kernel(**inputs):
    import concourse.bacc as _bacc
    from concourse.bass_utils import run_bass_kernel_spmd as _run

    a = {n.removeprefix("L0_attn_"): np.asarray(v) for n, v in inputs.items()}
    f1 = np.concatenate([a["L1_ffn_shared_w1"][None], a["L1_ffn_experts_w1"]])
    f2 = np.concatenate([a["L1_ffn_shared_w2"][None], a["L1_ffn_experts_w2"]])
    laid = {
        "x": a["x"], "x_A": a["x_A"], "x_B_lo": a["x_B"][0:4].reshape(P, P), "x_B_hi": a["x_B"][4:6].reshape(2 * MIXK, P),
        "lambdas": a["lambdas"].reshape(NG, P).T, "gn_gamma": a["gn_gamma"], "gn_beta": a["gn_beta"],
        **{n: a[n].reshape(P, 1) for n in VECS},
        **{f"{g}_{s}": a[f"{g}_{s}"] for g in "wkag" for s in "AB"},
        **{f"{g}W_T": a[f"{g}W"].T for g in "rkvo"},
        "Wr": a["L0_ffn_Wr"],
        "W1": a["L0_ffn_W1"].transpose(1, 0, 2).reshape(P, NE * HID0),
        "W3": a["L0_ffn_W3"].transpose(1, 0, 2).reshape(P, NE * HID0),
        "W2": a["L0_ffn_W2"].reshape(K0, P, P).transpose(1, 0, 2),
        **{f"W{g}": a[f"L1_attn_W{g}"] for g in "qkvo"},
        "gateW": a["L1_ffn_gate_w"].T,
        "F1": f1.transpose(2, 0, 1).reshape(P, NF * K1 * P),
        "F2": f2.reshape(NF, P, K1, P).transpose(3, 0, 2, 1).reshape(P, NF * K1, P),
    }
    nc = _bacc.Bacc("TRN2", target_bir_lowering=False, num_devices=1)
    arrays, io = {}, {}
    for name, v in laid.items():
        arrays[f"in_{name}"] = np.ascontiguousarray(v)
        io[name] = nc.dram_tensor(f"in_{name}", v.shape, mybir.dt.from_np(v.dtype), kind="ExternalInput").ap()
    out = nc.dram_tensor("out", a["x"].shape, F32, kind="ExternalOutput").ap()
    build(nc, io, out)
    r = _run(nc, [arrays], core_ids=[0])
    return r.results[0]["out"]
```
